# Optimizing a Trainium2 kernel written in Bass

```python
import numpy as np
import jax
import jax.numpy as jnp

def _softmax(x, axis=-1):
    return jax.nn.softmax(x, axis=axis)

def _gelu(x):
    return jax.nn.gelu(x, approximate=True)

def _silu(x):
    return jax.nn.silu(x)

def _sigmoid(x):
    return jax.nn.sigmoid(x)

def _layernorm(x, axis=-1, eps=1e-05):
    m = jnp.mean(x, axis=axis, keepdims=True)
    v = jnp.var(x, axis=axis, keepdims=True)
    return (x - m) / jnp.sqrt(v + eps)

def _scatter_add(tgt, idx, src, axis=0):
    return tgt.at[idx].add(src)

def _segment_sum(src, seg, n):
    return jax.ops.segment_sum(src, seg, n)
kernel_name = 'mk_hybrid_d1_jaxref_r8_0e676f'

def setup_inputs(seed: int=0):
    np.random.seed(seed)
    _w = jnp.asarray

    def _L0_attn_a_setup():
        import jax, jax.numpy as jnp
        import numpy as np
        H, HEADDIM, HIDDEN, DSTATE, G, K, NL = (32, 64, 128, 128, 1, 4, 15)
        DIM = H * HEADDIM
        CONV_DIM = DIM + 2 * G * DSTATE
        PROJ = DIM + CONV_DIM + H * (NL + 1)
        EPS = 1e-05

        def fenwick_level_map(T, num_levels):
            t = np.arange(T)[:, None]
            s = np.arange(T)[None, :]
            lvl = np.zeros((T, T), np.int32)
            for k in range(num_levels - 1):
                lo = t >> k + 1 << k + 1
                hi = t >> k << k
                m = (t >> k & 1 == 1) & (s >= lo) & (s < hi)
                lvl = np.where(m, k + 1, lvl)
            return jnp.asarray(lvl)
        key = jax.random.key(seed)
        ks = jax.random.split(key, 6)
        B, T = (1, 128)
        return {'hidden_states': jax.random.normal(ks[0], (B, T, HIDDEN), jnp.float32), 'in_proj_w': jax.random.normal(ks[1], (PROJ, HIDDEN), jnp.float32) / np.sqrt(HIDDEN).astype(np.float32), 'in_proj_b': jax.random.normal(ks[2], (PROJ,), jnp.float32) * 0.02, 'conv_w': jax.random.normal(ks[3], (CONV_DIM, K), jnp.float32) / np.sqrt(K).astype(np.float32), 'dt_bias': jnp.ones((H,), jnp.float32), 'A_log': jnp.log(jnp.arange(1, H + 1, dtype=jnp.float32)), 'L': jnp.ones((H, NL), jnp.float32), 'D': jnp.ones((H,), jnp.float32), 'norm_w': jnp.ones((DIM,), jnp.float32), 'out_proj_w': jax.random.normal(ks[4], (HIDDEN, DIM), jnp.float32) / np.sqrt(DIM).astype(np.float32), 'out_proj_b': jnp.zeros((HIDDEN,), jnp.float32)}
    _L0_attn_a_in = _L0_attn_a_setup()

    def _L0_attn_b_setup():
        import jax, jax.numpy as jnp
        import numpy as np
        SHIFTS = (-32, -16, -4, -1, 1, 4, 16, 32)
        LN_EPS = 1e-05
        key = jax.random.key(seed)
        k_x, k_g, k_v, k_gm, k_bt = jax.random.split(key, 5)
        B, L, D = (4, 512, 128)
        n = len(SHIFTS) + 1
        scale = 1.0 / np.sqrt(D)
        x = jax.random.normal(k_x, (B, L, D), dtype=jnp.float32)
        gate_W = jax.random.normal(k_g, (n * D, D), dtype=jnp.float32) * scale
        value_W = jax.random.normal(k_v, (D, D), dtype=jnp.float32) * scale
        gamma = jnp.ones((D,), dtype=jnp.float32)
        beta = jnp.zeros((D,), dtype=jnp.float32)
        return {'x': x, 'gate_W': gate_W, 'value_W': value_W, 'gamma': gamma, 'beta': beta}
    _L0_attn_b_in = _L0_attn_b_setup()

    def _L0_ffn_setup():
        import jax, jax.numpy as jnp
        import numpy as np
        D_MODEL = 128
        NHEAD = 16
        HEAD_DIM = D_MODEL // NHEAD
        FF = 256
        NUM_EXPERTS = 8
        EPS = 1e-05

        def _ln(x, g, b):
            m = x.mean(-1, keepdims=True)
            v = ((x - m) ** 2).mean(-1, keepdims=True)
            return (x - m) / jnp.sqrt(v + EPS) * g + b

        def _attention(src, Wq, bq, Wk, bk, Wv, bv, Wo, bo):
            B, T, d = src.shape
            scale = HEAD_DIM ** (-0.5)
            q = (src @ Wq + bq).reshape(B, T, NHEAD, HEAD_DIM)
            k = (src @ Wk + bk).reshape(B, T, NHEAD, HEAD_DIM)
            v = (src @ Wv + bv).reshape(B, T, NHEAD, HEAD_DIM)
            scores = jnp.einsum('bqhd,bkhd->bhqk', q, k) * scale
            probs = jax.nn.softmax(scores, axis=-1)
            out = jnp.einsum('bhqk,bkhd->bqhd', probs, v).reshape(B, T, d)
            return out @ Wo + bo

        def _moe(x, gW, gb, W1, b1, W2, b2):
            B, T, d = x.shape
            xf = x.reshape(-1, d)
            gates = jax.nn.softmax(xf @ gW + gb, axis=-1)
            top2_scores, top2_idx = jax.lax.top_k(gates, 2)
            w = (jax.nn.one_hot(top2_idx, NUM_EXPERTS, dtype=xf.dtype) * top2_scores[..., None]).sum(1)
            h = jax.nn.relu(jnp.einsum('nd,edf->enf', xf, W1) + b1[:, None, :])
            y = jnp.einsum('enf,efd->end', h, W2) + b2[:, None, :]
            out = jnp.einsum('ne,end->nd', w, y)
            return out.reshape(B, T, d)
        key = jax.random.key(seed)
        ks = jax.random.split(key, 12)
        s = 0.02
        d, f, E = (D_MODEL, FF, NUM_EXPERTS)
        return {'src': jax.random.normal(ks[0], (8, 64, d), dtype=jnp.float32), 'Wq': jax.random.normal(ks[1], (d, d), dtype=jnp.float32) * s, 'bq': jnp.zeros((d,), jnp.float32), 'Wk': jax.random.normal(ks[2], (d, d), dtype=jnp.float32) * s, 'bk': jnp.zeros((d,), jnp.float32), 'Wv': jax.random.normal(ks[3], (d, d), dtype=jnp.float32) * s, 'bv': jnp.zeros((d,), jnp.float32), 'Wo': jax.random.normal(ks[4], (d, d), dtype=jnp.float32) * s, 'bo': jnp.zeros((d,), jnp.float32), 'gW': jax.random.normal(ks[5], (d, E), dtype=jnp.float32) * s, 'gb': jnp.zeros((E,), jnp.float32), 'W1': jax.random.normal(ks[6], (E, d, f), dtype=jnp.float32) * s, 'b1': jnp.zeros((E, f), jnp.float32), 'W2': jax.random.normal(ks[7], (E, f, d), dtype=jnp.float32) * s, 'b2': jnp.zeros((E, d), jnp.float32), 'ln1_g': jnp.ones((d,), jnp.float32), 'ln1_b': jnp.zeros((d,), jnp.float32), 'ln2_g': jnp.ones((d,), jnp.float32), 'ln2_b': jnp.zeros((d,), jnp.float32)}
    _L0_ffn_in = _L0_ffn_setup()
    _d = {'L0_attn_a_hidden_states': _L0_attn_a_in['hidden_states'], 'L0_attn_a_in_proj_w': _L0_attn_a_in['in_proj_w'], 'L0_attn_a_in_proj_b': _L0_attn_a_in['in_proj_b'], 'L0_attn_a_conv_w': _L0_attn_a_in['conv_w'], 'L0_attn_a_dt_bias': _L0_attn_a_in['dt_bias'], 'L0_attn_a_A_log': _L0_attn_a_in['A_log'], 'L0_attn_a_L': _L0_attn_a_in['L'], 'L0_attn_a_D': _L0_attn_a_in['D'], 'L0_attn_a_norm_w': _L0_attn_a_in['norm_w'], 'L0_attn_a_out_proj_w': _L0_attn_a_in['out_proj_w'], 'L0_attn_a_out_proj_b': _L0_attn_a_in['out_proj_b'], 'L0_attn_b_gate_W': _L0_attn_b_in['gate_W'], 'L0_attn_b_value_W': _L0_attn_b_in['value_W'], 'L0_attn_b_gamma': _L0_attn_b_in['gamma'], 'L0_attn_b_beta': _L0_attn_b_in['beta'], 'L0_ffn_Wq': _L0_ffn_in['Wq'], 'L0_ffn_bq': _L0_ffn_in['bq'], 'L0_ffn_Wk': _L0_ffn_in['Wk'], 'L0_ffn_bk': _L0_ffn_in['bk'], 'L0_ffn_Wv': _L0_ffn_in['Wv'], 'L0_ffn_bv': _L0_ffn_in['bv'], 'L0_ffn_Wo': _L0_ffn_in['Wo'], 'L0_ffn_bo': _L0_ffn_in['bo'], 'L0_ffn_gW': _L0_ffn_in['gW'], 'L0_ffn_gb': _L0_ffn_in['gb'], 'L0_ffn_W1': _L0_ffn_in['W1'], 'L0_ffn_b1': _L0_ffn_in['b1'], 'L0_ffn_W2': _L0_ffn_in['W2'], 'L0_ffn_b2': _L0_ffn_in['b2'], 'L0_ffn_ln1_g': _L0_ffn_in['ln1_g'], 'L0_ffn_ln1_b': _L0_ffn_in['ln1_b'], 'L0_ffn_ln2_g': _L0_ffn_in['ln2_g'], 'L0_ffn_ln2_b': _L0_ffn_in['ln2_b']}
    _x0 = _d['L0_attn_a_hidden_states']
    _d['L0_attn_a_hidden_states'] = jax.random.normal(jax.random.fold_in(jax.random.key(seed), 1), (16, 256, 128), dtype=_x0.dtype)
    del _x0
    return _d

def reference(L0_attn_a_hidden_states, L0_attn_a_in_proj_w, L0_attn_a_in_proj_b, L0_attn_a_conv_w, L0_attn_a_dt_bias, L0_attn_a_A_log, L0_attn_a_L, L0_attn_a_D, L0_attn_a_norm_w, L0_attn_a_out_proj_w, L0_attn_a_out_proj_b, L0_attn_b_gate_W, L0_attn_b_value_W, L0_attn_b_gamma, L0_attn_b_beta, L0_ffn_Wq, L0_ffn_bq, L0_ffn_Wk, L0_ffn_bk, L0_ffn_Wv, L0_ffn_bv, L0_ffn_Wo, L0_ffn_bo, L0_ffn_gW, L0_ffn_gb, L0_ffn_W1, L0_ffn_b1, L0_ffn_W2, L0_ffn_b2, L0_ffn_ln1_g, L0_ffn_ln1_b, L0_ffn_ln2_g, L0_ffn_ln2_b):

    def _L0_attn_a_ref(hidden_states, in_proj_w, in_proj_b, conv_w, dt_bias, A_log, L, D, norm_w, out_proj_w, out_proj_b):
        import jax, jax.numpy as jnp
        import numpy as np
        H, HEADDIM, HIDDEN, DSTATE, G, K, NL = (32, 64, 128, 128, 1, 4, 15)
        DIM = H * HEADDIM
        CONV_DIM = DIM + 2 * G * DSTATE
        PROJ = DIM + CONV_DIM + H * (NL + 1)
        EPS = 1e-05

        def fenwick_level_map(T, num_levels):
            t = np.arange(T)[:, None]
            s = np.arange(T)[None, :]
            lvl = np.zeros((T, T), np.int32)
            for k in range(num_levels - 1):
                lo = t >> k + 1 << k + 1
                hi = t >> k << k
                m = (t >> k & 1 == 1) & (s >= lo) & (s < hi)
                lvl = np.where(m, k + 1, lvl)
            return jnp.asarray(lvl)
        B, T, _ = hidden_states.shape
        zxbcdtdl = hidden_states @ in_proj_w.T + in_proj_b
        z = zxbcdtdl[..., :DIM]
        xBC = zxbcdtdl[..., DIM:DIM + CONV_DIM]
        dt = zxbcdtdl[..., DIM + CONV_DIM:DIM + CONV_DIM + H]
        dl = zxbcdtdl[..., DIM + CONV_DIM + H:].reshape(B, T, H, NL)
        xp = jnp.pad(xBC, ((0, 0), (K - 1, 0), (0, 0)))
        xBC = sum((xp[:, i:i + T, :] * conv_w[:, i] for i in range(K)))
        xBC = jax.nn.silu(xBC)
        x = xBC[..., :DIM].reshape(B, T, H, HEADDIM)
        Bm = xBC[..., DIM:DIM + G * DSTATE].reshape(B, T, G, DSTATE)
        Cm = xBC[..., DIM + G * DSTATE:].reshape(B, T, G, DSTATE)
        dt = jax.nn.softplus(dt + dt_bias)
        D_res = x * D[None, None, :, None]
        v = x * dt[..., None]
        g = -jnp.exp(A_log)[None, None, :] * dt
        lam = jax.nn.softplus(L[None, None] * dl)
        gc = jnp.cumsum(g, axis=1).transpose(0, 2, 1)
        causal = jnp.tril(jnp.ones((T, T), bool))
        diff = jnp.where(causal, gc[:, :, :, None] - gc[:, :, None, :], -jnp.inf)
        decay = jnp.exp(diff)
        lvl = fenwick_level_map(T, NL)
        lam_ts = jnp.take_along_axis(lam.transpose(0, 2, 1, 3), lvl[None, None], axis=3)
        qk = jnp.einsum('btgn,bsgn->bgts', Cm, Bm)
        qk = jnp.repeat(qk, H // G, axis=1)
        att = qk * decay * lam_ts
        y = jnp.einsum('bhts,bshp->bthp', att, v) + D_res
        y = y.reshape(B, T, DIM)
        yz = y * jax.nn.silu(z)
        y = yz * jax.lax.rsqrt(jnp.mean(yz * yz, axis=-1, keepdims=True) + EPS) * norm_w
        return y @ out_proj_w.T + out_proj_b

    def _L0_attn_b_ref(x, gate_W, value_W, gamma, beta):
        import jax, jax.numpy as jnp
        import numpy as np
        SHIFTS = (-32, -16, -4, -1, 1, 4, 16, 32)
        LN_EPS = 1e-05
        B, L, D = x.shape
        n = len(SHIFTS) + 1
        v = jnp.einsum('bld,ed->ble', x, value_W)
        stacked = jnp.stack([v] + [jnp.roll(v, -s, axis=1) for s in SHIFTS], axis=2)
        gates = jax.nn.sigmoid(jnp.einsum('bld,ed->ble', x, gate_W))
        gates = gates.reshape(B, L, n, D)
        out = jnp.sum(stacked * gates, axis=2)
        mu = jnp.mean(out, axis=-1, keepdims=True)
        var = jnp.mean(jnp.square(out - mu), axis=-1, keepdims=True)
        return (out - mu) * jax.lax.rsqrt(var + LN_EPS) * gamma + beta

    def _L0_ffn_ref(src, Wq, bq, Wk, bk, Wv, bv, Wo, bo, gW, gb, W1, b1, W2, b2, ln1_g, ln1_b, ln2_g, ln2_b):
        import jax, jax.numpy as jnp
        import numpy as np
        D_MODEL = 128
        NHEAD = 16
        HEAD_DIM = D_MODEL // NHEAD
        FF = 256
        NUM_EXPERTS = 8
        EPS = 1e-05

        def _ln(x, g, b):
            m = x.mean(-1, keepdims=True)
            v = ((x - m) ** 2).mean(-1, keepdims=True)
            return (x - m) / jnp.sqrt(v + EPS) * g + b

        def _attention(src, Wq, bq, Wk, bk, Wv, bv, Wo, bo):
            B, T, d = src.shape
            scale = HEAD_DIM ** (-0.5)
            q = (src @ Wq + bq).reshape(B, T, NHEAD, HEAD_DIM)
            k = (src @ Wk + bk).reshape(B, T, NHEAD, HEAD_DIM)
            v = (src @ Wv + bv).reshape(B, T, NHEAD, HEAD_DIM)
            scores = jnp.einsum('bqhd,bkhd->bhqk', q, k) * scale
            probs = jax.nn.softmax(scores, axis=-1)
            out = jnp.einsum('bhqk,bkhd->bqhd', probs, v).reshape(B, T, d)
            return out @ Wo + bo

        def _moe(x, gW, gb, W1, b1, W2, b2):
            B, T, d = x.shape
            xf = x.reshape(-1, d)
            gates = jax.nn.softmax(xf @ gW + gb, axis=-1)
            top2_scores, top2_idx = jax.lax.top_k(gates, 2)
            w = (jax.nn.one_hot(top2_idx, NUM_EXPERTS, dtype=xf.dtype) * top2_scores[..., None]).sum(1)
            h = jax.nn.relu(jnp.einsum('nd,edf->enf', xf, W1) + b1[:, None, :])
            y = jnp.einsum('enf,efd->end', h, W2) + b2[:, None, :]
            out = jnp.einsum('ne,end->nd', w, y)
            return out.reshape(B, T, d)
        attn_out = _attention(src, Wq, bq, Wk, bk, Wv, bv, Wo, bo)
        x = _ln(src + attn_out, ln1_g, ln1_b)
        ff = _moe(x, gW, gb, W1, b1, W2, b2)
        return _ln(x + ff, ln2_g, ln2_b)
    x = L0_attn_a_hidden_states
    x = x + _L0_attn_a_ref(_layernorm(x, axis=-1), L0_attn_a_in_proj_w, L0_attn_a_in_proj_b, L0_attn_a_conv_w, L0_attn_a_dt_bias, L0_attn_a_A_log, L0_attn_a_L, L0_attn_a_D, L0_attn_a_norm_w, L0_attn_a_out_proj_w, L0_attn_a_out_proj_b)
    x = x + _L0_ffn_ref(_layernorm(x, axis=-1), L0_ffn_Wq, L0_ffn_bq, L0_ffn_Wk, L0_ffn_bk, L0_ffn_Wv, L0_ffn_bv, L0_ffn_Wo, L0_ffn_bo, L0_ffn_gW, L0_ffn_gb, L0_ffn_W1, L0_ffn_b1, L0_ffn_W2, L0_ffn_b2, L0_ffn_ln1_g, L0_ffn_ln1_b, L0_ffn_ln2_g, L0_ffn_ln2_b)
    x = x + _L0_attn_b_ref(_layernorm(x, axis=-1), L0_attn_b_gate_W, L0_attn_b_value_W, L0_attn_b_gamma, L0_attn_b_beta)
    x = x + _L0_ffn_ref(_layernorm(x, axis=-1), L0_ffn_Wq, L0_ffn_bq, L0_ffn_Wk, L0_ffn_bk, L0_ffn_Wv, L0_ffn_bv, L0_ffn_Wo, L0_ffn_bo, L0_ffn_gW, L0_ffn_gb, L0_ffn_W1, L0_ffn_b1, L0_ffn_W2, L0_ffn_b2, L0_ffn_ln1_g, L0_ffn_ln1_b, L0_ffn_ln2_g, L0_ffn_ln2_b)
    return x

_drawn_inputs = setup_inputs


def setup_inputs(seed=0):
    import zlib

    import numpy as np

    out = dict(_drawn_inputs(seed))
    spreads = {'L0_attn_a_dt_bias': (1.0, 0.2),
     'L0_attn_a_L': (1.0, 0.2),
     'L0_attn_a_D': (1.0, 0.2),
     'L0_attn_a_norm_w': (1.0, 0.2),
     'L0_attn_a_out_proj_b': (0.0, 0.1),
     'L0_attn_b_gamma': (1.0, 0.2),
     'L0_attn_b_beta': (0.0, 0.1),
     'L0_ffn_bq': (0.0, 0.8),
     'L0_ffn_bk': (0.0, 0.8),
     'L0_ffn_bv': (0.0, 0.477),
     'L0_ffn_bo': (0.0, 0.1),
     'L0_ffn_gb': (0.0, 0.8),
     'L0_ffn_b1': (0.0, 0.8),
     'L0_ffn_b2': (0.0, 0.572),
     'L0_ffn_ln1_g': (1.0, 0.2),
     'L0_ffn_ln1_b': (0.0, 0.1),
     'L0_ffn_ln2_g': (1.0, 0.2),
     'L0_ffn_ln2_b': (0.0, 0.1)}
    factors = {'L0_ffn_Wq': 8.0,
     'L0_ffn_Wk': 8.0,
     'L0_ffn_Wv': 8.0,
     'L0_ffn_Wo': 3.224,
     'L0_ffn_gW': 4.244,
     'L0_ffn_W1': 8.0,
     'L0_ffn_W2': 6.759}
    for name, (base, spread) in spreads.items():
        noise = np.random.default_rng([zlib.crc32(name.encode()), seed]).standard_normal(out[name].shape)
        drawn = base * np.exp(spread * noise) if base else spread * noise
        out[name] = jnp.asarray(drawn.astype(out[name].dtype))
    for name, factor in factors.items():
        out[name] = (out[name] * factor).astype(out[name].dtype)
    return out
```

```python
import numpy as np
import concourse.bass as bass
from concourse import mybir
from concourse.alu_op_type import AluOpType as ALU
from contextlib import ExitStack

F32 = mybir.dt.float32
BF16 = mybir.dt.bfloat16
ACT = mybir.ActivationFunctionType
AX = mybir.AxisListType

P = 128
BATCH, T, HID = 16, 256, 128
NT = T // P
H, HD, NS, NLV_W, KCONV = 32, 64, 128, 15, 4
DIM = H * HD
NF = DIM // P
CONV = DIM + 2 * NS
NLV = T.bit_length() - 1
QT = 32
NQ = P // QT
NODES = QT - 1
LOW = QT.bit_length() - 1
HG = 8
NSML = H * (1 + NLV + 1)
OFF_MASK, OFF_NODE = 0, QT
OFF_HIGH, OFF_TOP = 3 * H, 3 * H + 9
R_LOW, R_HIGH = QT + 3 * NODES, 3 * H + 12
NH, AD, FF, NE = 16, 8, 256, 8
SLOTROWS = 96
ROW_MAX = 9 * AD
GS = 1
GT = GS * NT
GW = GS * T
SHIFTS = (-32, -16, -4, -1, 1, 4, 16, 32)
NG = len(SHIFTS) + 1
MAXSH = max(SHIFTS)
EPS = 1e-5
NEG = -1e30
TINY = 1e-30


class Queue:

    def __init__(self, sem):
        self.sem, self.count, self.ops, self.seen = sem, 0, [], {}

    def wait(self, marks):
        for m in marks:
            if m is None:
                continue
            sem, value = m
            if self.seen.get(id(sem), 0) < value:
                self.seen[id(sem)] = value
                self.ops.append(lambda e, s=sem, v=value: e.wait_ge(s, v))

    def run(self, make, *marks):
        self.wait(marks)
        self.ops.append(make)

    def do(self, make, *marks):
        self.wait(marks)
        self.count += 1
        self.ops.append(lambda e: make(e).then_inc(self.sem, 1))
        return (self.sem, self.count)

    def dma(self, line, out, in_, *marks):
        self.wait(marks)
        line[1] += 16
        self.ops.append(lambda e, s=line[0]: e.dma_start(out, in_).then_inc(s, 16))
        return (line[0], line[1])


class Slots:

    def __init__(self, bufs):
        self.free = [(b, ()) for b in bufs]

    def take(self):
        return self.free.pop(0)

    def give(self, buf, *marks):
        self.free.append((buf, marks))


def bc(ap, axis, n):
    dims = [list(d) for d in ap.ap]
    dims.insert(axis, [0, n])
    return bass.AP(tensor=ap.tensor, offset=ap.offset, ap=dims)


def dram(ap, offset, dims):
    return bass.AP(tensor=ap.tensor, offset=ap.offset + offset, ap=dims)


def shape_constants():
    c = {}
    c["ident"] = np.eye(P, dtype=np.float32)
    c["tri"] = np.triu(np.ones((P, P), np.float32))
    low = np.zeros((P, NQ, P), np.float32)
    for q in range(NQ):
        for r in range(QT):
            low[OFF_MASK + r, q, q * QT + r:] = NEG
        for k in range(LOW):
            for j in range(QT >> (k + 1)):
                s0 = q * QT + (j << (k + 1))
                for part in range(3):
                    low[OFF_NODE + part * NODES + node_row(k, j), q, s0:s0 + (1 << k)] = 1.0
    c["low_sel"] = low.reshape(P, NQ * P)
    hi = np.zeros((P, 2, P), np.float32)
    for part in range(3):
        hi[OFF_HIGH + 3 * part + 0, 0, 0:QT] = 1.0
        hi[OFF_HIGH + 3 * part + 1, 0, 2 * QT:3 * QT] = 1.0
        hi[OFF_HIGH + 3 * part + 2, 0, 0:2 * QT] = 1.0
        hi[OFF_TOP + part, 1, :] = 1.0
    c["high_sel"] = hi.reshape(P, 2 * P)
    ind = np.zeros((P, H), np.float32)
    for r in range(3 * H):
        ind[r, r % H] = 1.0
    c["head_ind"] = ind
    before = np.zeros((P, NE, NE), np.float32)
    for e in range(NE):
        before[:, e, :e] = 1.0
    c["before"] = before.reshape(P, NE * NE)
    return c


def node_row(k, j):
    return sum(QT >> (i + 1) for i in range(k)) + j


def build(nc, d, out, n_batch=BATCH, layers="afbf"):
    ctx = ExitStack()
    with ctx:
        def sb(name, shape, dt=F32):
            return ctx.enter_context(nc.sbuf_tensor(name, shape, dt))

        def ring(name, n, shape, dt=F32):
            return Slots([sb(f"{name}{i}", shape, dt) for i in range(n)])

        def line(name):
            return [ctx.enter_context(nc.semaphore(name)), 0]

        pe, act, dve, pool, sp = (Queue(ctx.enter_context(nc.semaphore(n)))
                                  for n in ("pe_done", "act_done", "dve_done", "pool_done", "sp_done"))

        const_line = line("const_loaded")
        loaded = {}

        def load(name, shape, src, dt=F32):
            t = sb("c_" + name, shape, dt)
            sp.dma(const_line, t[tuple(slice(None) for _ in shape)], src)
            loaded[name] = t
            return t

        def row_bc(ap, n):
            return dram(ap, 0, [[0, P], [1, n]])

        w_in = load("w_in", [P, DIM + CONV], d["in_wT"])
        w_small = load("w_small", [P, NSML], d["small_wT"])
        b_small = load("b_small", [P, NSML], row_bc(d["small_b"], NSML))
        dt_bias = load("dt_bias", [P, H], row_bc(d["dt_bias"], H))
        lvl_scale = load("lvl_scale", [P, (NLV + 1) * H], row_bc(d["L_lvl"], (NLV + 1) * H))
        neg_a = load("neg_a", [P, H], row_bc(d["A_log"], H))
        d_skip = load("d_skip", [P, H], row_bc(d["D"], H))
        b_in = load("b_in", [P, 2 * NF + 2], d["in_b_cols"])
        conv_w = load("conv_w", [P, NF + 2, KCONV], d["conv_cols"])
        w_out = load("w_out", [P, NF, HID], d["out_wT"])
        norm_w = load("norm_w", [P, NF], d["norm_cols"])
        b_out = load("b_out", [P, HID], row_bc(d["out_b"], HID))
        ident = load("ident", [P, P], d["ident"])
        tri = load("tri", [P, P], d["tri"])
        before = load("before", [P, NE * NE], d["before"])
        head_ind = load("head_ind", [P, H], d["head_ind"])
        w_q, w_k, w_v, w_o = (load(n, [P, P], d[n]) for n in ("Wq", "Wk", "Wv", "Wo"))
        b_q, b_k = (load(n, [P, 1], d[n]) for n in ("bq", "bk"))
        b_v, b_o, ln1_g, ln1_b, ln2_g, ln2_b, mix_g, mix_b = (
            load(n, [P, HID], row_bc(d[n], HID))
            for n in ("bv", "bo", "ln1_g", "ln1_b", "ln2_g", "ln2_b", "gamma", "beta"))
        w_gate = load("w_gate", [P, NE], d["gW"])
        b_gate = load("b_gate", [P, NE], row_bc(d["gb"], NE))
        w_1 = load("w_1", [P, NE, FF], d["W1"])
        b_1 = load("b_1", [P, NE * FF // P], d["b1_cols"])
        w_2 = load("w_2", [P, NE * FF // P, HID], d["W2"])
        b_2 = load("b_2", [NE, HID], d["b2"])
        w_mix = load("w_mix", [P, NG * HID], d["gate_WT"])
        w_val = load("w_val", [P, HID], d["value_WT"])
        consts = (const_line[0], const_line[1])

        x_ring = ring("x_", 3, [P, GT, HID])
        xn_a = sb("xn_a", [P, NT, HID])
        xnT_a = sb("xnT_a", [P, T])
        U = sb("U", [P, NT, NSML])
        W1t = sb("W1t", [P, NT, NSML])
        W2t = sb("W2t", [P, NT, NSML])
        SPL = sb("SPL", [P, NT, NSML])
        g_t = sb("g_t", [P, NT, H])
        gc = sb("gc", [P, NT, H])
        CL = W1t[:, :, 0:NLV * H].rearrange("p i (l h) -> p i l h", h=H)
        c_parts = sb("c_parts", [P, NT, 3, NLV * H], BF16)
        s_parts = sb("s_parts", [P, NT, 3, H], BF16)
        gr = sb("gr", [P, NT, H])
        ln_dt = sb("ln_dt", [P, NT, H])
        ccoef = sb("ccoef", [P, NT, H])
        qk_diag = sb("qk_diag", [P, NT])
        pad_ring = ring("pad", 2, [P, KCONV - 1 + T])
        conv_ring = ring("conv", 2, [P, T])
        xs_ring = ring("xs", 2, [P, 2, T])
        bmT, cmT = sb("bmT", [P, T]), sb("cmT", [P, T])
        QK = sb("QK", [P, 3, P])
        X = sb("X", [P, NT, DIM])
        own_ring = ring("own", 2, [P, HG * HD])
        Z = sb("Z", [P, NF, T])
        low_bufs = [sb(f"low{i}", [P, P, H], BF16) for i in range(1)]
        high_buf = sb("high", [P, P, H], BF16)
        low_sel = sb("low_sel", [P, NQ, P], BF16)
        high_sel = [sb(f"high_sel{i}", [P, P], BF16) for i in range(3)]
        att_ring = ring("att", 4, [P, HG, P])
        ssq = sb("ssq", [P, T])
        rms = sb("rms", [P, NT])
        ident_bf = sb("ident_bf", [P, P], BF16)
        ones_f = sb("ones_f", [P, P])
        share = sb("share", [P, 1])
        eps_c = sb("eps_c", [P, 1])
        lnst_a = sb("lnst_a", [P, GT, 6])
        lnmv_a = sb("lnmv_a", [P, GT, 2])
        lnrs_a = sb("lnrs_a", [P, GT])
        osb, qk_scr = xn_a, xn_a[:, 0, :]

        src_t = sb("src_t", [P, GT, HID])
        srcT = sb("srcT", [P, GW])
        qf = sb("qf", [P, GW])
        qr = sb("qr", [P, GW])
        qparts = sb("qparts", [P, 3, GW], BF16)
        q_stack = sb("q_stack", [SLOTROWS, NH, GW], BF16)
        k_stack = sb("k_stack", [SLOTROWS, NH, GW], BF16)
        V9 = sb("V9", [P, GT, NH, 32])
        nmax = sb("nmax", [P, GT, NH])
        nmax_bf = sb("nmax_bf", [P, GT, NH], BF16)
        maxT = sb("maxT", [NH, GW], BF16)
        pt_ring = ring("pt", 5, [P, 2, T])
        O_sb = sb("O_sb", [P, 4, T])
        rden = sb("rden", [P, NH])
        x1 = sb("x1", [P, GT, HID])
        x1T = sb("x1T", [P, GW])
        gate_l = sb("gate_l", [P, GT, NE])
        gate_s = sb("gate_s", [P, GT])
        gate_g = sb("gate_g", [P, GT, NE, NE])
        gate_q = sb("gate_q", [P, GT, NE, NE])
        w_e = sb("w_e", [P, GT, NE])
        w_eT = sb("w_eT", [NE, GW])
        h_ring = pt_ring
        ff = sb("ff", [P, GT, HID])
        o_tok = ff
        v_ext = O_sb[:, :, :].rearrange("p g t -> p (g t)")[:, 0:GS * (T + 2 * MAXSH)].rearrange("p (s t) -> p s t", s=GS)
        mix_acc = x1T
        lnst = sb("lnst", [P, GT, 6])
        lnmv = sb("lnmv", [P, GT, 2])
        lnrs = sb("lnrs", [P, GT])

        psA = Slots([ctx.enter_context(nc.psum_tensor(f"psA{i}", [P, 512], F32)) for i in range(4)])
        psB = Slots([ctx.enter_context(nc.psum_tensor(f"psB{i}", [P, 512], F32)) for i in range(4)])

        lvl_scr = [nc.dram_tensor(f"lvl_scr{i}", [3, NLV, P, H], BF16)[:, :, :, :] for i in range(NT)]
        qk_scrd = [nc.dram_tensor(f"qk_scr{i}", [3, P, GW], BF16)[:, :, :] for i in range(2)]
        lvl_out = [line(f"lvl_stored{i}") for i in range(NT)]
        lvl_in = [line(f"lvl_loaded{i}") for i in range(NT)]
        qk_out = [line("q_stored"), line("k_stored")]
        qk_in = [line("q_stacked"), line("k_stacked")]
        max_in = line("max_stacked")
        x_in = [line(f"x_loaded{i}") for i in range(3)]
        x_out = line("x_stored")

        done = {}
        done["eps"] = dve.do(lambda e: e.memset(eps_c[:, :], EPS))
        done["ones"] = dve.do(lambda e: e.memset(ones_f[:, :], 1.0))
        done["share"] = dve.do(lambda e: e.memset(share[:, :], 1.0 / 32))
        done["identb"] = dve.do(lambda e: e.tensor_copy(ident_bf[:, :], ident[:, :]), consts)
        fold = [dve.do(lambda e: e.tensor_tensor(b_small[:, 0:H], b_small[:, 0:H], dt_bias[:, :], ALU.add), consts),
                act.do(lambda e: e.activation(neg_a[:, :], neg_a[:, :], ACT.Exp), consts)]
        fold.append(dve.do(lambda e: e.tensor_scalar(neg_a[:, :], neg_a[:, :], -1.0, None, ALU.mult), fold[1]))
        for f in range(NF):
            m = dve.do(lambda e, f=f: e.tensor_scalar(w_out[:, f, :], w_out[:, f, :], norm_w[:, f:f + 1], None, ALU.mult))
            fold.append(m)
        done["fold"] = fold[-1]
        setup_line = line("setup_loaded")
        zf = Z[:, :, :].rearrange("p f t -> p (f t)")
        l = sp.dma(setup_line, zf[:, 0:NQ * P], d["low_sel"])
        l = sp.dma(setup_line, zf[:, NQ * P:NQ * P + 2 * P], d["high_sel"])
        dve.do(lambda e: e.tensor_copy(low_sel[:, :, :].rearrange("p q s -> p (q s)"), zf[:, 0:NQ * P]), l)
        for i in range(3):
            o = NQ * P + (P if i == 2 else 0)
            done["z_free"] = dve.do(lambda e, i=i, o=o: e.tensor_copy(high_sel[i][:, :], zf[:, o:o + P]))
        done["sel"] = done["z_free"]
        z0 = pool.do(lambda e: e.memset(high_buf[:, :, :], 0.0))
        done["high0"] = pool.do(lambda e: e.tensor_copy(high_buf[0:3 * H, :, :], bc(head_ind[0:3 * H, :], 1, P)), z0, consts)
        for lb in low_bufs:
            z0 = pool.do(lambda e, lb=lb: e.memset(lb[:, :, :], 0.0), done["high0"])
            for q in range(NQ):
                done["low0"] = pool.do(lambda e, lb=lb, q=q: e.tensor_copy(
                    lb[0:QT, q * QT:(q + 1) * QT, :], bc(ident[0:QT, 0:QT], 2, H)), z0)
        for pad, _ in pad_ring.free:
            done["pad0"] = dve.do(lambda e, pad=pad: e.memset(pad[:, 0:KCONV - 1], 0.0))
        for st in (q_stack, k_stack):
            z0 = pool.do(lambda e, st=st: e.memset(st[:, :, :], 0.0), done["low0"])
        done["stack0"] = pool.do(lambda e: e.memset(k_stack[64:SLOTROWS, :, :], 1.0), z0)
        z0 = pool.do(lambda e: e.memset(V9[:, :, :, :], 0.0), done["stack0"])
        done["v9"] = pool.do(lambda e: e.memset(V9[:, :, :, AD:AD + 1], 1.0), z0)

        def layer_norm_stats(x, n, st, mv, rs, *marks):
            for i in range(n):
                m = dve.do(lambda e, i=i: e.bn_stats(st[:, i, :], x[:, i, :]), *marks)
            for i in range(n):
                m2 = dve.do(lambda e, i=i: e.bn_aggr(mv[:, i, :], st[:, i, :]), m)
            m3 = act.do(lambda e: e.activation(rs[:, 0:n], mv[:, 0:n, 1], ACT.Ln, bias=eps_c[:, 0:1]), m2, done["eps"])
            return act.do(lambda e: e.activation(rs[:, 0:n], rs[:, 0:n], ACT.Exp, scale=-0.5), m3), m2

        def normalise(out_, x, n, mv, rs, m_rs, *marks):
            for i in range(n):
                m = dve.do(lambda e, i=i: e.tensor_scalar(out_[:, i, :], x[:, i, :], mv[:, i, 0:1], rs[:, i:i + 1],
                                                          ALU.subtract, ALU.mult), m_rs, *marks)
            return m

        def transpose_tiles(out_, x, n, ps, m_x, *marks):
            bank, free = ps.take()
            for i in range(n):
                m = pe.do(lambda e, i=i: e.transpose(bank[:, i * P:(i + 1) * P], x[:, i, :], ident[:, :]),
                          m_x, consts, *free)
            m = act.do(lambda e: e.activation(out_[:, 0:n * P], bank[:, 0:n * P], ACT.Copy), m, *marks)
            ps.give(bank, m)
            return m

        last = {}

        def ssm_layer(x, s, m_x, n):
            par = 0
            xs = x[:, s * NT:(s + 1) * NT, :]
            L = last.get
            m_rs, _ = layer_norm_stats(xs, NT, lnst_a, lnmv_a, lnrs_a, *m_x)
            m = normalise(xn_a, xs, NT, lnmv_a, lnrs_a, m_rs, L("xn_a"))
            m_xnT = transpose_tiles(xnT_a, xn_a, NT, psA, m, L("xnT_a"))
            last["xn_a"] = m_xnT

            for i in range(NT):
                bank, free = psA.take()
                m = pe.do(lambda e, i=i, bank=bank: e.matmul(bank[:, 0:NSML], xnT_a[:, i * P:(i + 1) * P], w_small[:, :],
                                                             start=True, stop=True), m_xnT, *free)
                m = dve.do(lambda e, i=i, bank=bank: e.tensor_tensor(U[:, i, :], bank[:, 0:NSML], b_small[:, :], ALU.add),
                           m, L("U"), fold[0])
                psA.give(bank, m)
            m = dve.do(lambda e: e.tensor_tensor(U[:, :, H:], U[:, :, H:], bc(lvl_scale[:, :], 1, NT), ALU.mult), m, consts)
            m_u = m
            yield
            m = act.do(lambda e: e.activation(W1t[:, :, :], U[:, :, :], ACT.Abs), m, L("W1t"))
            m_e = act.do(lambda e: e.activation(W1t[:, :, :], W1t[:, :, :], ACT.Exp, scale=-1.0), m)
            m_w = dve.do(lambda e: e.tensor_scalar(W2t[:, :, :], W1t[:, :, :], 1.0, None, ALU.add), m_e, L("W2t"))
            m_ln = act.do(lambda e: e.activation(SPL[:, :, :], W2t[:, :, :], ACT.Ln), m_w, L("SPL"))
            m_d = dve.do(lambda e: e.tensor_scalar(W2t[:, :, :], W2t[:, :, :], -1.0, TINY, ALU.add, ALU.max), m_ln)
            m_d = dve.do(lambda e: e.reciprocal(W2t[:, :, :], W2t[:, :, :]), m_d)
            m = dve.do(lambda e: e.scalar_tensor_tensor(out=W1t[:, :, :], in0=SPL[:, :, :], scalar=TINY, in1=W1t[:, :, :],
                                                        op0=ALU.max, op1=ALU.mult), m_ln)
            m = dve.do(lambda e: e.tensor_tensor(W1t[:, :, :], W1t[:, :, :], W2t[:, :, :], ALU.mult), m, m_d)
            m_sp = dve.do(lambda e: e.scalar_tensor_tensor(out=SPL[:, :, :], in0=U[:, :, :], scalar=0.0, in1=W1t[:, :, :],
                                                           op0=ALU.max, op1=ALU.add), m)
            last["U"] = last["W1t"] = last["W2t"] = m_sp
            dt = SPL[:, :, 0:H]
            m_g = dve.do(lambda e: e.tensor_tensor(g_t[:, :, :], dt, bc(neg_a[:, :], 1, NT), ALU.mult), m_sp, fold[2], L("g_t"))
            bank, free = psA.take()
            for i in range(NT):
                for j in range(i + 1):
                    m = pe.do(lambda e, i=i, j=j, bank=bank: e.matmul(
                        bank[:, i * H:(i + 1) * H], (tri if i == j else ones_f)[:, :], g_t[:, j, :],
                        start=(j == 0), stop=(j == i)), m_g, done["ones"], *free)
            last["g_t"] = m
            m_gc = dve.do(lambda e, bank=bank: e.tensor_copy(gc[:, :, :].rearrange("p i h -> p (i h)"), bank[:, 0:NT * H]),
                          m, L("gc"))
            psA.give(bank, m_gc)
            m = dve.do(lambda e: e.tensor_scalar(CL[:, :, :, :].rearrange("p i l h -> p i (l h)"), SPL[:, :, 2 * H:],
                                                 1e-37, None, ALU.max), m_sp)
            m = act.do(lambda e: e.activation(CL[:, :, :, :], CL[:, :, :, :], ACT.Ln), m)
            for i in range(NT):
                m_c = dve.do(lambda e, i=i: e.tensor_tensor(CL[:, i, :, :], CL[:, i, :, :], bc(gc[:, i, :], 1, NLV), ALU.add),
                             m, m_gc)
            cl = CL[:, :, :, :].rearrange("p i l h -> p i (l h)")
            cr = W2t[:, :, 0:NLV * H]
            m = dve.do(lambda e: e.tensor_copy(c_parts[:, :, 0, :], cl), m_c, *last.get("c_parts", ()))
            m = dve.do(lambda e: e.tensor_tensor(cr, cl, c_parts[:, :, 0, :], ALU.subtract), m)
            m = dve.do(lambda e: e.tensor_copy(c_parts[:, :, 1, :], cr), m)
            m_cp = dve.do(lambda e: e.tensor_tensor(c_parts[:, :, 2, :], cr, c_parts[:, :, 1, :], ALU.subtract), m)
            last["W1t"] = last["W2t"] = m_cp
            m = dve.do(lambda e: e.tensor_scalar(ln_dt[:, :, :], dt, 1e-37, None, ALU.max), m_sp, L("s_parts"))
            m = act.do(lambda e: e.activation(ln_dt[:, :, :], ln_dt[:, :, :], ACT.Ln), m)
            m = dve.do(lambda e: e.tensor_tensor(gc[:, :, :], ln_dt[:, :, :], gc[:, :, :], ALU.subtract), m_c, m)
            m = dve.do(lambda e: e.tensor_copy(s_parts[:, :, 0, :], gc[:, :, :]), m, L("s_parts"))
            m = dve.do(lambda e: e.tensor_tensor(gr[:, :, :], gc[:, :, :], s_parts[:, :, 0, :], ALU.subtract), m)
            m = dve.do(lambda e: e.tensor_copy(s_parts[:, :, 1, :], gr[:, :, :]), m)
            m_s = dve.do(lambda e: e.tensor_tensor(s_parts[:, :, 2, :], gr[:, :, :], s_parts[:, :, 1, :], ALU.subtract), m)
            last["gc"] = m_s
            bank, free = psA.take()
            bview = bank[:, :].bitcast(BF16)
            for i in range(NT):
                m = pe.do(lambda e, i=i, bview=bview: e.transpose(
                    bview[0:3 * H, i * P:(i + 1) * P], s_parts[:, i, :, :].rearrange("p a h -> p (a h)"), ident_bf[:, :]),
                    m_s, done["identb"], *free)
            last["s_parts"] = m
            for i, src in enumerate((0, 1, 0)):
                m_hs = dve.do(lambda e, i=i, src=src, bview=bview: e.tensor_copy(
                    high_sel[i][0:3 * H, :], bview[0:3 * H, src * P:(src + 1) * P]), m, L("high_sel"), done["sel"])
            psA.give(bank, m_hs)
            stored = []
            for i in range(NT):
                stored.append(sp.dma(lvl_out[i], dram(lvl_scr[i], 0, [[H, P], [P * H, 3 * NLV], [1, H]]),
                                     c_parts[:, i, :, :].rearrange("p a (l h) -> p (a l) h", h=H), m_cp, L(f"scr{i}")))
            last["c_parts"] = tuple(stored)
            yield

            def conv_tile(c, out_, *marks):
                bank, free = psA.take()
                m = pe.do(lambda e: e.matmul(bank[:, 0:T], w_in[:, DIM + c * P:DIM + (c + 1) * P], xnT_a[:, :],
                                             start=True, stop=True), m_xnT, consts, *free)
                pad, pfree = pad_ring.take()
                m = act.do(lambda e: e.activation(pad[:, KCONV - 1:], bank[:, 0:T], ACT.Identity,
                                                  bias=b_in[:, NF + c:NF + c + 1]), m, done["pad0"], *pfree)
                psA.give(bank, m)
                cv, cfree = conv_ring.take()
                m = dve.do(lambda e: e.tensor_scalar(cv[:, :], pad[:, 0:T], conv_w[:, c, 0:1], None, ALU.mult), m, *cfree)
                for k in range(1, KCONV):
                    m = dve.do(lambda e, k=k: e.scalar_tensor_tensor(out=cv[:, :], in0=pad[:, k:k + T],
                                                                     scalar=conv_w[:, c, k:k + 1], in1=cv[:, :],
                                                                     op0=ALU.mult, op1=ALU.add), m)
                pad_ring.give(pad, m)
                m = act.do(lambda e: e.activation(out_, cv[:, :], ACT.Silu), m, *marks)
                conv_ring.give(cv, m)
                return m

            m_b = conv_tile(NF, bmT[:, :], L("bmT"))
            m_cc = conv_tile(NF + 1, cmT[:, :], L("bmT"))
            bank, free = psA.take()
            for k, (s_, t_) in enumerate(((0, 0), (1, 1), (0, 1))):
                m = pe.do(lambda e, k=k, s_=s_, t_=t_, bank=bank: e.matmul(
                    bank[:, k * P:(k + 1) * P], bmT[:, s_ * P:(s_ + 1) * P], cmT[:, t_ * P:(t_ + 1) * P],
                    start=True, stop=True), m_b, m_cc, *free)
            last["bmT"] = m
            m_qk = dve.do(lambda e, bank=bank: e.tensor_copy(QK[:, :, :].rearrange("p k t -> p (k t)"), bank[:, 0:3 * P]),
                          m, L("QK"))
            psA.give(bank, m_qk)
            m = m_qk
            for i in range(NT):
                m = dve.do(lambda e, i=i: e.tensor_tensor(qk_scr, QK[:, i, :], ident[:, :], ALU.mult), m, last["xn_a"])
                m = dve.do(lambda e, i=i: e.tensor_reduce(qk_diag[:, i:i + 1], qk_scr, AX.X, ALU.add), m)
            for i in range(NT):
                m1 = dve.do(lambda e, i=i: e.scalar_tensor_tensor(
                    out=ccoef[:, i, :], in0=SPL[:, i, H:2 * H], scalar=qk_diag[:, i:i + 1], in1=SPL[:, i, 0:H],
                    op0=ALU.mult, op1=ALU.mult), m, L("ccoef"))
            m_cf = dve.do(lambda e: e.tensor_tensor(ccoef[:, :, :], ccoef[:, :, :], bc(d_skip[:, :], 1, NT), ALU.add), m1)
            yield

            for f2 in range(NF // 2):
                xb, xfree = xs_ring.take()
                for k in range(2):
                    m_s2 = conv_tile(2 * f2 + k, xb[:, k, :], *xfree)
                bank, free = psA.take()
                for i in range(NT):
                    for k in range(2):
                        m = pe.do(lambda e, i=i, k=k, bank=bank, xb=xb: e.transpose(
                            bank[:, i * 2 * P + k * P:i * 2 * P + (k + 1) * P], xb[:, k, i * P:(i + 1) * P], ident[:, :]),
                            m_s2, *free)
                xs_ring.give(xb, m)
                m_x = act.do(lambda e, bank=bank, f2=f2: e.activation(
                    X[:, :, f2 * 2 * P:(f2 + 1) * 2 * P], bank[:, :].rearrange("p (i c) -> p i c", i=NT), ACT.Copy),
                    m, L("X"))
                psA.give(bank, m_x)
                for k in range(2):
                    f = 2 * f2 + k
                    bank, free = psA.take()
                    m = pe.do(lambda e, f=f, bank=bank: e.matmul(bank[:, 0:T], w_in[:, f * P:(f + 1) * P], xnT_a[:, :],
                                                                 start=True, stop=True), *free)
                    last["xnT_a"] = m
                    m_z = act.do(lambda e, f=f, bank=bank: e.activation(Z[:, f, :], bank[:, 0:T], ACT.Silu,
                                                                        bias=b_in[:, f:f + 1]), m, L("Z"), done["z_free"])
                    psA.give(bank, m_z)
                yield
            last["SPL"] = m_cf

            m_x_all = m_x
            for t in range(NT):
                low = low_bufs[par]
                w = (stored[t], L("low"), L("high"), done["low0"], done["high0"])
                row = NLV * P * H
                for k in range(LOW):
                    for j in range(QT >> (k + 1)):
                        r, t0, n_t = OFF_NODE + node_row(k, j), (j << (k + 1)) + (1 << k), 1 << k
                        for part in range(3):
                            m_ld = sp.dma(lvl_in[t], low[r + part * NODES:r + part * NODES + 1, :, :].rearrange(
                                "o (q i) h -> o q (i h)", q=NQ)[:, :, t0 * H:(t0 + n_t) * H],
                                dram(lvl_scr[t], part * row + (k * P + t0) * H, [[0, 1], [QT * H, NQ], [1, n_t * H]]), *w)
                for part in range(3):
                    for node, (k, t0, n_t) in enumerate(((LOW, QT, QT), (LOW, 3 * QT, QT), (LOW + 1, 2 * QT, 2 * QT))):
                        r = OFF_HIGH + 3 * part + node
                        m_ld = sp.dma(lvl_in[t], high_buf[r:r + 1, t0:t0 + n_t, :],
                                      dram(lvl_scr[t], part * row + (k * P + t0) * H, [[0, 1], [H, n_t], [1, H]]), *w)
                if t:
                    for part in range(3):
                        r = OFF_TOP + part
                        m_ld = sp.dma(lvl_in[t], high_buf[r:r + 1, :, :],
                                      dram(lvl_scr[t], part * row + (NLV - 1) * P * H, [[0, 1], [H, P], [1, H]]), *w)
                last[f"scr{t}"] = m_ld
                for hg in range(H // HG):
                    tiles = []
                    h0 = hg * HG
                    for s_ in ([t] if t == 0 else [0, t]):
                        diag = s_ == t
                        att, afree = att_ring.take()
                        sel = high_sel[t if diag else 2]
                        for half in range(2):
                            bank, free = psA.take()
                            bv = bank[:, :].rearrange("p (t h) -> p t h", h=HG)
                            c = half * 64
                            m = pe.do(lambda e, bv=bv, c=c, sel=sel, diag=diag, h0=h0: e.matmul(
                                bv, sel[0:R_HIGH, :], high_buf[0:R_HIGH, c:c + 64, h0:h0 + HG],
                                start=True, stop=not diag, skip_group_check=True), m_ld, m_hs, *free)
                            if diag:
                                for q in (2 * half, 2 * half + 1):
                                    m = pe.do(lambda e, bv=bv, c=c, q=q, low=low, h0=h0: e.matmul(
                                        bv[:, q * QT - c:(q + 1) * QT - c, :], low_sel[0:R_LOW, q, :],
                                        low[0:R_LOW, q * QT:(q + 1) * QT, h0:h0 + HG],
                                        start=False, stop=(q % 2 == 1), skip_group_check=True), m_ld)
                            m_x = act.do(lambda e, bv=bv, c=c, att=att: e.activation(
                                att[:, :, c:c + 64].rearrange("p h t -> p t h"), bv, ACT.Exp), m, *afree)
                            psA.give(bank, m_x)
                        last["low"] = last["high"] = last["high_sel"] = m
                        kq = t if diag else 2
                        m_a = dve.do(lambda e, att=att, kq=kq: e.tensor_tensor(
                            att[:, :, :], att[:, :, :], bc(QK[:, kq, :], 1, HG), ALU.mult), m_x, m_qk)
                        tiles.append((att, s_))
                    own, ofree = own_ring.take()
                    m_own = pool.do(lambda e, own=own, t=t, h0=h0: e.tensor_tensor(
                        own[:, :].rearrange("p (h c) -> p h c", c=HD),
                        X[:, t, h0 * HD:(h0 + HG) * HD].rearrange("p (h c) -> p h c", c=HD),
                        bc(ccoef[:, t, h0:h0 + HG], 2, HD), ALU.mult), m_x_all, m_cf, *ofree)
                    last["ccoef"] = m_own
                    bank, free = psA.take()
                    for f in range(HG // 2):
                        yv = bank[:, f * P:(f + 1) * P]
                        fc = (hg * HG // 2 + f) * P
                        pe.run(lambda e, yv=yv, f=f, own=own: e.matmul(yv, own[:, f * P:(f + 1) * P], ident[:, :], start=True, stop=False,
                                                                skip_group_check=True), m_own, *free)
                        for att, s_ in tiles:
                            for k in range(2):
                                m = pe.do(lambda e, f=f, k=k, att=att, s_=s_, bank=bank, fc=fc, t=t: e.matmul(
                                    bank[k * HD:(k + 1) * HD, f * P:(f + 1) * P], X[:, s_, fc + k * HD:fc + (k + 1) * HD],
                                    att[:, 2 * f + k, :], start=False, stop=(s_ == t), skip_group_check=True), m_a, m_x_all)
                    for att, _ in tiles:
                        att_ring.give(att, m)
                    own_ring.give(own, m)
                    last["X"] = m
                    f0 = hg * HG // 2
                    m_yz = dve.do(lambda e, bank=bank, f0=f0, t=t: e.tensor_tensor(
                        Z[:, f0:f0 + HG // 2, t * P:(t + 1) * P], bank[:, :].rearrange("p (f t) -> p f t", t=P),
                        Z[:, f0:f0 + HG // 2, t * P:(t + 1) * P], ALU.mult), m, m_z)
                    psA.give(bank, m_yz)
                    yield
            last["QK"] = m_a

            bank, free = psA.take()
            for g4 in range(NF // 4):
                sqa, sfree = att_ring.take()
                sq = sqa[:, :, :].rearrange("p (a b) t -> p a (b t)", b=NT)
                m = act.do(lambda e, g4=g4, sq=sq: e.activation(sq, Z[:, 4 * g4:4 * g4 + 4, :], ACT.Square),
                           m_yz, *sfree)
                for j in range(4):
                    m = pe.do(lambda e, j=j, sq=sq, g4=g4, bank=bank: e.matmul(
                        bank[32 * j:32 * j + 32, 0:T], ones_f[:, 0:32], sq[:, j, :], start=(g4 == 0),
                        stop=(g4 == NF // 4 - 1), skip_group_check=True), m, *free)
                att_ring.give(sqa, m)
            m = act.do(lambda e, bank=bank: e.activation(ssq[:, :], bank[:, 0:T], ACT.Copy), m, L("ssq"))
            for i in range(NT):
                m_ss = pe.do(lambda e, i=i, bank=bank: e.matmul(bank[:, T + i:T + i + 1], ssq[:, i * P:(i + 1) * P],
                                                                share[:, :], start=True, stop=True, skip_group_check=True),
                             m, done["share"])
            last["ssq"] = m_ss
            m = act.do(lambda e, bank=bank: e.activation(rms[:, :], bank[:, T:T + NT], ACT.Ln, scale=1.0 / DIM,
                                                         bias=eps_c[:, 0:1]), m_ss, L("rms"))
            psA.give(bank, m)
            m_rms = act.do(lambda e: e.activation(rms[:, :], rms[:, :], ACT.Exp, scale=-0.5), m)
            yield
            bank, free = psA.take()
            for i in range(NT):
                for f in range(NF):
                    m = pe.do(lambda e, i=i, f=f, bank=bank: e.matmul(
                        bank[:, i * P:(i + 1) * P], Z[:, f, i * P:(i + 1) * P], w_out[:, f, :],
                        start=(f == 0), stop=(f == NF - 1)), m_yz, done["fold"], *free)
            last["Z"] = m
            for i in range(NT):
                m2 = dve.do(lambda e, i=i, bank=bank: e.scalar_tensor_tensor(
                    out=osb[:, i, :], in0=bank[:, i * P:(i + 1) * P], scalar=rms[:, i:i + 1], in1=b_out[:, :],
                    op0=ALU.mult, op1=ALU.add), m, m_rms)
            psA.give(bank, m2)
            last["rms"] = m2
            m2 = dve.do(lambda e: e.tensor_tensor(xs, xs, osb[:, :, :], ALU.add), m2)
            last["xn_a"] = m2
            yield
            return m2

        late = {}

        def affine(y, g, b, m):
            m = dve.do(lambda e: e.tensor_tensor(y[:, :, :], y[:, :, :], bc(g[:, :], 1, GT), ALU.mult), m)
            return dve.do(lambda e: e.tensor_tensor(y[:, :, :], y[:, :, :], bc(b[:, :], 1, GT), ALU.add), m)

        def ffn_layer(x, m_x):
            L = late.get
            m_rs, _ = layer_norm_stats(x, GT, lnst, lnmv, lnrs, *m_x)
            m_src = normalise(src_t, x, GT, lnmv, lnrs, m_rs, L("src_t"))
            m_sT = transpose_tiles(srcT, src_t, GT, psB, m_src, L("srcT"))
            yield
            m_max_ready = None
            for side, (w, b, st) in enumerate(((w_q, b_q, q_stack), (w_k, b_k, k_stack))):
                bank, free = psB.take()
                m = pe.do(lambda e, w=w, bank=bank: e.matmul(bank[:, 0:GW], w[:, :], srcT[:, :], start=True, stop=True),
                          m_sT, *free)
                m = act.do(lambda e, b=b, bank=bank: e.activation(qf[:, :], bank[:, 0:GW], ACT.Identity, bias=b[:, 0:1]),
                           m, L("qf"))
                psB.give(bank, m)
                m = dve.do(lambda e: e.tensor_copy(qparts[:, 0, :], qf[:, :]), m, L("qparts"))
                m = dve.do(lambda e: e.tensor_tensor(qr[:, :], qf[:, :], qparts[:, 0, :], ALU.subtract), m)
                m = dve.do(lambda e: e.tensor_copy(qparts[:, 1, :], qr[:, :]), m)
                m = dve.do(lambda e: e.tensor_tensor(qparts[:, 2, :], qr[:, :], qparts[:, 1, :], ALU.subtract), m)
                late["qf"] = m
                scr = qk_scrd[side]
                m = sp.dma(qk_out[side], scr.rearrange("a p t -> p a t"), qparts[:, :, :], m, L("stacked"))
                late["qparts"] = m
                for i in range(3):
                    for j in range(3):
                        r = (3 * i + j) * AD
                        part = i if side == 0 else j
                        m_st = sp.dma(qk_in[side], st[r:r + AD, :, :],
                                      dram(scr, part * P * GW, [[GW, AD], [AD * GW, NH], [1, GW]]),
                                      m, L("stack_free"), done["stack0"])
                if side == 0:
                    m_qst = m_st
                yield
            late["stacked"] = m_st
            bank, free = psB.take()
            for i in range(GT):
                m = pe.do(lambda e, i=i, bank=bank: e.matmul(bank[:, i * P:(i + 1) * P], srcT[:, i * P:(i + 1) * P], w_v[:, :],
                                                             start=True, stop=True), *free)
            late["srcT"] = m
            for i in range(GT):
                m_v = dve.do(lambda e, i=i, bank=bank: e.tensor_tensor(
                    V9[:, i, :, 0:AD], bank[:, i * P:(i + 1) * P].rearrange("p (h c) -> p h c", c=AD),
                    b_v[:, :].rearrange("p (h c) -> p h c", c=AD), ALU.add), m, L("V9"), done["v9"])
            psB.give(bank, m_v)
            yield
            for i in range(GT):
                s0 = (i // NT) * T
                for h2 in range(NH // 2):
                    bank, free = psB.take()
                    for k in range(2):
                        h = 2 * h2 + k
                        m = pe.do(lambda e, h=h, k=k, i=i, s0=s0, bank=bank: e.matmul(
                            bank[:, k * T:(k + 1) * T], q_stack[0:ROW_MAX, h, i * P:(i + 1) * P],
                            k_stack[0:ROW_MAX, h, s0:s0 + T], start=True, stop=True), m_qst, m_st, *free)
                    m = dve.do(lambda e, i=i, h2=h2, bank=bank: e.tensor_reduce(
                        nmax[:, i, 2 * h2:2 * h2 + 2], bank[:, :].rearrange("p (h k) -> p h k", k=T), AX.X, ALU.max),
                        m, L("nmax"))
                    psB.give(bank, m)
                    if h2 % 4 == 3:
                        yield
            m = dve.do(lambda e: e.tensor_scalar(nmax_bf[:, :, :], nmax[:, :, :], -1.0, None, ALU.mult), m, L("nmax"))
            bank, free = psB.take()
            bview = bank[:, :].bitcast(BF16)
            for i in range(GT):
                m2 = pe.do(lambda e, i=i, bview=bview: e.transpose(bview[0:NH, i * P:(i + 1) * P], nmax_bf[:, i, :],
                                                                   ident_bf[:, :]), m, *free)
            late["nmax"] = m2
            m = act.do(lambda e, bview=bview: e.activation(maxT[:, :], bview[0:NH, 0:GW], ACT.Copy), m2, L("maxT"))
            psB.give(bank, m)
            for h in range(NH):
                m_mx = sp.dma(max_in, q_stack[ROW_MAX:ROW_MAX + 1, h, :], maxT[h:h + 1, :], m)
            late["maxT"] = m_mx
            yield
            for s in range(GS):
                for g in range(NH // 4):
                    pts = []
                    for kt in range(NT):
                        for h2 in range(2):
                            bank, free = psB.take()
                            for k in range(2):
                                h = 4 * g + 2 * h2 + k
                                m = pe.do(lambda e, h=h, k=k, kt=kt, s=s, bank=bank: e.matmul(
                                    bank[:, k * T:(k + 1) * T], k_stack[:, h, s * T + kt * P:s * T + (kt + 1) * P],
                                    q_stack[:, h, s * T:(s + 1) * T], start=True, stop=True), m_mx, *free)
                            late["stack_free"] = m
                            pt, pfree = pt_ring.take()
                            m_p = act.do(lambda e, pt=pt, bank=bank: e.activation(
                                pt[:, :, :].rearrange("p h q -> p (h q)"), bank[:, :], ACT.Exp, scale=float(AD) ** -0.5),
                                m, *pfree)
                            psB.give(bank, m_p)
                            pts.append((pt, kt, h2))
                    if g % 2 == 0:
                        obank, ofree = psB.take()
                    c0 = (g % 2) * T
                    for kt in range(NT):
                        for j in range(4):
                            pt = [p_ for p_, kt_, h2_ in pts if kt_ == kt and h2_ == j // 2][0]
                            m = pe.do(lambda e, j=j, kt=kt, pt=pt, s=s, g=g, obank=obank, c0=c0: e.matmul(
                                obank[32 * j:32 * j + 32, c0:c0 + T], V9[:, s * NT + kt, 4 * g + j, :], pt[:, j % 2, :],
                                start=(kt == 0), stop=(kt == NT - 1), skip_group_check=True), m_p, m_v, *ofree)
                    for pt, _, _ in pts:
                        pt_ring.give(pt, m)
                    if g % 2:
                        m_o = dve.do(lambda e, g=g, obank=obank: e.tensor_copy(
                            O_sb[:, g - 1:g + 1, :].rearrange("p g t -> p (g t)"), obank[:, :]), m, L("O_sb"))
                        psB.give(obank, m_o)
                    yield
                late["V9"] = m
                for qt in range(NT):
                    bank, free = psB.take()
                    for g in range(4):
                        m = pe.do(lambda e, g=g, qt=qt, bank=bank: e.transpose(
                            bank[:, g * P:(g + 1) * P], O_sb[:, g, qt * P:(qt + 1) * P], ident[:, :]), m_o, *free)
                    bh = bank[:, :].rearrange("p (h c) -> p h c", c=32)
                    m = dve.do(lambda e, bh=bh: e.reciprocal(rden[:, :], bh[:, :, AD]), m, L("rden"))
                    m = dve.do(lambda e, bh=bh, i=s * NT + qt: e.tensor_tensor(
                        o_tok[:, i, :].rearrange("p (h c) -> p h c", c=AD), bh[:, :, 0:AD], bc(rden[:, :], 2, AD), ALU.mult),
                        m, L("ff"))
                    psB.give(bank, m)
                    late["rden"] = m
                late["O_sb"] = m
            m_oT = transpose_tiles(qf, o_tok, GT, psB, m, late["qf"])
            late["ff"] = m_oT
            bank, free = psB.take()
            for i in range(GT):
                m = pe.do(lambda e, i=i, bank=bank: e.matmul(bank[:, i * P:(i + 1) * P], qf[:, i * P:(i + 1) * P], w_o[:, :],
                                                             start=True, stop=True), m_oT, *free)
            late["qf"] = m
            m = dve.do(lambda e, bank=bank: e.tensor_tensor(x1[:, :, :], bank[:, 0:GW].rearrange("p (i c) -> p i c", c=HID),
                                                            src_t[:, :, :], ALU.add), m, L("x1"))
            late["src_t"] = m
            psB.give(bank, m)
            m = dve.do(lambda e: e.tensor_tensor(x1[:, :, :], x1[:, :, :], bc(b_o[:, :], 1, GT), ALU.add), m)
            m_rs, _ = layer_norm_stats(x1, GT, lnst, lnmv, lnrs, m)
            m = normalise(x1, x1, GT, lnmv, lnrs, m_rs)
            m_x1 = affine(x1, ln1_g, ln1_b, m)
            m_x1T = transpose_tiles(x1T, x1, GT, psB, m_x1, L("x1T"))
            yield
            bank, free = psB.take()
            for i in range(GT):
                m = pe.do(lambda e, i=i, bank=bank: e.matmul(bank[:, i * NE:(i + 1) * NE], x1T[:, i * P:(i + 1) * P],
                                                             w_gate[:, :], start=True, stop=True), m_x1T, *free)
            m = dve.do(lambda e, bank=bank: e.tensor_tensor(gate_l[:, :, :], bank[:, 0:GT * NE].rearrange("p (i n) -> p i n", n=NE),
                                                            bc(b_gate[:, :], 1, GT), ALU.add), m)
            psB.give(bank, m)
            m = dve.do(lambda e: e.tensor_reduce(gate_s[:, :], gate_l[:, :, :], AX.X, ALU.max), m)
            m = dve.do(lambda e: e.tensor_tensor(gate_l[:, :, :], gate_l[:, :, :], bc(gate_s[:, :], 2, NE), ALU.subtract), m)
            m = act.do(lambda e: e.activation(gate_l[:, :, :], gate_l[:, :, :], ACT.Exp), m)
            m = dve.do(lambda e: e.tensor_reduce(gate_s[:, :], gate_l[:, :, :], AX.X, ALU.add), m)
            m = dve.do(lambda e: e.reciprocal(gate_s[:, :], gate_s[:, :]), m)
            m = dve.do(lambda e: e.tensor_tensor(gate_l[:, :, :], gate_l[:, :, :], bc(gate_s[:, :], 2, NE), ALU.mult), m)
            mine, other = bc(gate_l[:, :, :], 3, NE), bc(gate_l[:, :, :], 2, NE)
            m1 = dve.do(lambda e: e.tensor_tensor(gate_g[:, :, :, :], other, mine, ALU.is_gt), m)
            m = dve.do(lambda e: e.tensor_tensor(gate_q[:, :, :, :], other, mine, ALU.is_equal), m)
            bf = bc(before[:, :].rearrange("p (a b) -> p a b", b=NE), 1, GT)
            m = dve.do(lambda e: e.tensor_tensor(gate_q[:, :, :, :], gate_q[:, :, :, :], bf, ALU.mult), m)
            m = dve.do(lambda e: e.tensor_tensor(gate_g[:, :, :, :], gate_g[:, :, :, :], gate_q[:, :, :, :], ALU.add), m, m1)
            m = dve.do(lambda e: e.tensor_reduce(w_e[:, :, :], gate_g[:, :, :, :], AX.X, ALU.add), m, L("w_e"))
            m_w = dve.do(lambda e: e.scalar_tensor_tensor(out=w_e[:, :, :], in0=w_e[:, :, :], scalar=1.5, in1=gate_l[:, :, :],
                                                          op0=ALU.is_lt, op1=ALU.mult), m)
            bank, free = psB.take()
            for i in range(GT):
                m = pe.do(lambda e, i=i, bank=bank: e.transpose(bank[0:NE, i * P:(i + 1) * P], w_e[:, i, :], ident[:, :]),
                          m_w, *free)
            m = act.do(lambda e, bank=bank: e.activation(w_eT[:, :], bank[0:NE, 0:GW], ACT.Copy), m, L("w_eT"))
            psB.give(bank, m)
            bank, free = psB.take()
            for i in range(GT):
                m2 = pe.do(lambda e, i=i, bank=bank: e.matmul(bank[:, i * P:(i + 1) * P], w_eT[:, i * P:(i + 1) * P], b_2[:, :],
                                                              start=True, stop=True), m, *free)
            late["w_eT"] = m2
            m_ff = dve.do(lambda e, bank=bank: e.tensor_tensor(ff[:, :, :], bank[:, 0:GW].rearrange("p (i c) -> p i c", c=HID),
                                                               x1[:, :, :], ALU.add), m2, L("ff"))
            late["x1"] = m_ff
            psB.give(bank, m_ff)
            yield
            for ex in range(NE):
                hb, hfree = h_ring.take()
                for k in range(2):
                    bank, free = psB.take()
                    m = pe.do(lambda e, ex=ex, k=k, bank=bank: e.matmul(bank[:, 0:GW], w_1[:, ex, k * P:(k + 1) * P], x1T[:, :],
                                                                        start=True, stop=True), *free)
                    late["x1T"] = m
                    m_h = act.do(lambda e, ex=ex, k=k, bank=bank, hb=hb: e.activation(
                        hb[:, k, :], bank[:, 0:GW], ACT.Relu, bias=b_1[:, 2 * ex + k:2 * ex + k + 1]), m, *hfree)
                    psB.give(bank, m_h)
                bank, free = psB.take()
                for i in range(GT):
                    for k in range(2):
                        m = pe.do(lambda e, ex=ex, i=i, k=k, bank=bank, hb=hb: e.matmul(
                            bank[:, i * P:(i + 1) * P], hb[:, k, i * P:(i + 1) * P], w_2[:, 2 * ex + k, :],
                            start=(k == 0), stop=(k == 1)), m_h, *free)
                h_ring.give(hb, m)
                for i in range(GT):
                    m_ff2 = dve.do(lambda e, ex=ex, i=i, bank=bank: e.scalar_tensor_tensor(
                        out=ff[:, i, :], in0=bank[:, i * P:(i + 1) * P], scalar=w_e[:, i, ex:ex + 1], in1=ff[:, i, :],
                        op0=ALU.mult, op1=ALU.add), m, m_ff)
                psB.give(bank, m_ff2)
                m_ff = m_ff2
                yield
            late["w_e"] = m_ff
            m_rs, _ = layer_norm_stats(ff, GT, lnst, lnmv, lnrs, m_ff)
            m = normalise(ff, ff, GT, lnmv, lnrs, m_rs)
            m = affine(ff, ln2_g, ln2_b, m)
            m = dve.do(lambda e: e.tensor_tensor(x[:, :, :], x[:, :, :], ff[:, :, :], ALU.add), m)
            late["ff"] = m
            yield
            return m

        def mix_layer(x, m_x):
            L = late.get
            m_rs, _ = layer_norm_stats(x, GT, lnst, lnmv, lnrs, *m_x)
            m = normalise(src_t, x, GT, lnmv, lnrs, m_rs, L("src_t"))
            m_sT = transpose_tiles(srcT, src_t, GT, psB, m, L("srcT"))
            late["src_t"] = m_sT
            bank, free = psB.take()
            m = pe.do(lambda e, bank=bank: e.matmul(bank[:, 0:GW], w_val[:, :], srcT[:, :], start=True, stop=True), m_sT, *free)
            bv = bank[:, 0:GW].rearrange("p (s t) -> p s t", t=T)
            act.do(lambda e, bv=bv: e.activation(v_ext[:, :, MAXSH:MAXSH + T], bv, ACT.Copy), m, L("O_sb"))
            act.do(lambda e, bv=bv: e.activation(v_ext[:, :, 0:MAXSH], bv[:, :, T - MAXSH:], ACT.Copy))
            m_v = act.do(lambda e, bv=bv: e.activation(v_ext[:, :, MAXSH + T:], bv[:, :, 0:MAXSH], ACT.Copy))
            psB.give(bank, m_v)
            m_acc = None
            for k, shift in enumerate((0,) + SHIFTS):
                bank, free = psB.take()
                m = pe.do(lambda e, k=k, bank=bank: e.matmul(bank[:, 0:GW], w_mix[:, k * P:(k + 1) * P], srcT[:, :],
                                                             start=True, stop=True), *free)
                buf, bfree = pt_ring.take()
                sg = buf[:, 0, :] if GS == 1 else None
                m_s = act.do(lambda e, sg=sg, bank=bank: e.activation(sg, bank[:, 0:GW], ACT.Sigmoid), m, *bfree)
                psB.give(bank, m_s)
                vv = v_ext[:, :, MAXSH + shift:MAXSH + shift + T]
                sv = sg.rearrange("p (s t) -> p s t", t=T)
                prod = mix_acc[:, :] if k == 0 else buf[:, 1, :]
                m_acc = dve.do(lambda e, vv=vv, sv=sv, prod=prod: e.tensor_tensor(
                    prod.rearrange("p (s t) -> p s t", t=T), sv, vv, ALU.mult), m_s, m_v, m_acc, L("x1T"))
                if k:
                    m_acc = dve.do(lambda e, prod=prod: e.tensor_tensor(mix_acc[:, :], mix_acc[:, :], prod, ALU.add), m_acc)
                pt_ring.give(buf, m_acc)
                yield
            late["srcT"], late["O_sb"] = m_s, m_acc
            bank, free = psB.take()
            for i in range(GT):
                m = pe.do(lambda e, i=i, bank=bank: e.transpose(bank[:, i * P:(i + 1) * P], mix_acc[:, i * P:(i + 1) * P],
                                                                ident[:, :]), m_acc, *free)
            late["x1T"] = m
            m = act.do(lambda e, bank=bank: e.activation(ff[:, :, :].rearrange("p i c -> p (i c)"), bank[:, 0:GW], ACT.Copy),
                       m, L("ff"))
            psB.give(bank, m)
            m_rs, _ = layer_norm_stats(ff, GT, lnst, lnmv, lnrs, m)
            m = normalise(ff, ff, GT, lnmv, lnrs, m_rs)
            m = affine(ff, mix_g, mix_b, m)
            m = dve.do(lambda e: e.tensor_tensor(x[:, :, :], x[:, :, :], ff[:, :, :], ALU.add), m)
            late["ff"] = m
            yield
            return m

        xin = d["x"].rearrange("b (i p) c -> p (b i) c", p=P)
        xout = out.rearrange("b (i p) c -> p (b i) c", p=P)
        n_groups = n_batch // GS
        group_x = {}

        def front(g):
            x, free = x_ring.take()
            m = sp.dma(x_in[g % 3], x[:, :, :], xin[:, g * GT:(g + 1) * GT, :], *free)
            m = (m,)
            for s in range(GS):
                if "a" in layers:
                    m2 = yield from ssm_layer(x, s, m, g * GS + s)
                    m = m + (m2,)
            group_x[g] = (x, m)

        def back(g):
            x, m = group_x.pop(g)
            for kind in layers:
                if kind == "f":
                    m = ((yield from ffn_layer(x, m)),)
                elif kind == "b":
                    m = ((yield from mix_layer(x, m)),)
            m = sp.dma(x_out, xout[:, g * GT:(g + 1) * GT, :], x[:, :, :], *m)
            x_ring.give(x, m)
            yield

        def drain(gen):
            steps = 0
            for _ in gen:
                steps += 1
            return steps

        def weave(a, b, na, nb):
            ia = ib = 0
            while a is not None or b is not None:
                if b is None or (a is not None and ia * nb <= ib * na):
                    try:
                        next(a)
                        ia += 1
                    except StopIteration:
                        a = None
                else:
                    try:
                        next(b)
                        ib += 1
                    except StopIteration:
                        b = None

        n_front = drain(front(0))
        for g in range(1, n_groups):
            weave(front(g), back(g - 1), n_front, N_BACK)
        drain(back(n_groups - 1))
        sp.wait([(x_out[0], x_out[1])])

        block = ctx.enter_context(nc.Block())

        @block.sync
        def _(e):
            for op in sp.ops:
                op(e)

        @block.tensor
        def _(e):
            for op in pe.ops:
                op(e)

        @block.scalar
        def _(e):
            for op in act.ops:
                op(e)

        @block.vector
        def _(e):
            for op in dve.ops:
                op(e)

        @block.gpsimd
        def _(e):
            for op in pool.ops:
                op(e)


N_BACK = 95


def lay_out(i):
    def f(a):
        return np.ascontiguousarray(a)

    a = {k: np.asarray(v) for k, v in i.items()}
    pa, pb, pf = "L0_attn_a_", "L0_attn_b_", "L0_ffn_"
    w, b = a[pa + "in_proj_w"], a[pa + "in_proj_b"]
    n_big = DIM + CONV
    lvl_w = w[n_big + H:].reshape(H, NLV_W, HID).transpose(1, 0, 2)[:NLV + 1].reshape(-1, HID)
    lvl_b = b[n_big + H:].reshape(H, NLV_W).T[:NLV + 1].reshape(-1)
    o = {
        "x": a[pa + "hidden_states"],
        "in_wT": f(w[:n_big].T), "in_b_cols": f(b[:n_big].reshape(-1, P).T),
        "small_wT": f(np.concatenate([w[n_big:n_big + H], lvl_w]).T),
        "small_b": np.concatenate([b[n_big:n_big + H], lvl_b]),
        "dt_bias": a[pa + "dt_bias"], "A_log": a[pa + "A_log"], "D": a[pa + "D"],
        "L_lvl": f(a[pa + "L"].T[:NLV + 1]).reshape(-1),
        "conv_cols": f(a[pa + "conv_w"].reshape(-1, P, KCONV).transpose(1, 0, 2)),
        "norm_cols": f(a[pa + "norm_w"].reshape(-1, P).T),
        "out_wT": f(a[pa + "out_proj_w"].T.reshape(NF, P, HID).transpose(1, 0, 2)), "out_b": a[pa + "out_proj_b"],
        "gate_WT": f(a[pb + "gate_W"].T), "value_WT": f(a[pb + "value_W"].T),
        "gamma": a[pb + "gamma"], "beta": a[pb + "beta"],
        "bq": a[pf + "bq"].reshape(P, 1), "bk": a[pf + "bk"].reshape(P, 1),
        "W1": f(a[pf + "W1"].transpose(1, 0, 2)),
        "b1_cols": f(a[pf + "b1"].reshape(-1, P).T),
        "W2": f(a[pf + "W2"].reshape(-1, P, HID).transpose(1, 0, 2)), "b2": a[pf + "b2"],
    }
    for n in ("Wq", "Wk", "Wv", "Wo", "bv", "bo", "gW", "gb", "ln1_g", "ln1_b", "ln2_g", "ln2_b"):
        o[n] = a[pf + n]
    o.update(shape_constants())
    return o


def kernel(**inputs):
    import concourse.bacc as _bacc
    from concourse.bass_utils import run_bass_kernel_spmd as _run

    nc = _bacc.Bacc("TRN2", target_bir_lowering=False, num_devices=1)
    arrays = lay_out(inputs)
    d = {n: nc.dram_tensor("in_" + n, v.shape, mybir.dt.from_np(v.dtype), kind="ExternalInput").ap()
         for n, v in arrays.items()}
    out = nc.dram_tensor("out_0", (BATCH, T, HID), F32, kind="ExternalOutput").ap()
    build(nc, d, out)
    r = _run(nc, [{"in_" + n: v for n, v in arrays.items()}], core_ids=[0])
    return r.results[0]["out_0"]
```

```python
import numpy as np
import concourse.bass as bass
from concourse import mybir
from concourse.alu_op_type import AluOpType as ALU
from contextlib import ExitStack

F32 = mybir.dt.float32
BF16 = mybir.dt.bfloat16
I32 = mybir.dt.int32
ACT = mybir.ActivationFunctionType
AX = mybir.AxisListType

P = 128
BATCH, T, HID = 16, 256, 128
NT = T // P
H, HD, NS, NLV_W, KCONV = 32, 64, 128, 15, 4
DIM = H * HD
NF = DIM // P
CONV = DIM + 2 * NS
NLV = T.bit_length() - 1
QT = 32
NQ = P // QT
NODES = QT - 1
LOW = QT.bit_length() - 1
HG = 8
NSML = H * (1 + NLV + 1)
OFF_MASK, OFF_NODE = 0, QT
NHI = 3
OFF_HIGH, OFF_TOP = 3 * H, 3 * H + 3 * NHI * NT
R_LOW, R_HIGH = QT + 3 * NODES, OFF_TOP + 3
NH, AD, FF, NE = 16, 8, 256, 8
SLOTROWS = 96
ROW_MAX = 9 * AD
GS = 1
GT = GS * NT
GW = GS * T
SHIFTS = (-32, -16, -4, -1, 1, 4, 16, 32)
NG = len(SHIFTS) + 1
MAXSH = max(SHIFTS)
EPS = 1e-5
ROOT_GUESS = 0x5F3759DF
NEG = -1e30
TINY = 1e-30


class Queue:

    def __init__(self, sem):
        self.sem, self.count, self.ops, self.seen = sem, 0, [], {}

    def wait(self, marks):
        for m in marks:
            if m is None:
                continue
            sem, value = m
            if self.seen.get(id(sem), 0) < value:
                self.seen[id(sem)] = value
                self.ops.append(lambda e, s=sem, v=value: e.wait_ge(s, v))

    def run(self, make, *marks):
        self.wait(marks)
        self.ops.append(make)

    def do(self, make, *marks):
        self.wait(marks)
        self.count += 1
        self.ops.append(lambda e: make(e).then_inc(self.sem, 1))
        return (self.sem, self.count)

    def dma(self, line, out, in_, *marks):
        self.wait(marks)
        line[1] += 16
        self.ops.append(lambda e, s=line[0]: e.dma_start(out, in_).then_inc(s, 16))
        return (line[0], line[1])


class Slots:

    def __init__(self, bufs):
        self.free = [(b, ()) for b in bufs]

    def take(self):
        return self.free.pop(0)

    def give(self, buf, *marks):
        self.free.append((buf, marks))


def bc(ap, axis, n):
    dims = [list(d) for d in ap.ap]
    dims.insert(axis, [0, n])
    return bass.AP(tensor=ap.tensor, offset=ap.offset, ap=dims)


def dram(ap, offset, dims):
    return bass.AP(tensor=ap.tensor, offset=ap.offset + offset, ap=dims)


def shape_constants():
    c = {}
    c["ident"] = np.eye(P, dtype=np.float32)
    c["tri"] = np.triu(np.ones((P, P), np.float32))
    low = np.zeros((P, NQ, P), np.float32)
    for q in range(NQ):
        for r in range(QT):
            low[OFF_MASK + r, q, q * QT + r:] = NEG
        for k in range(LOW):
            for j in range(QT >> (k + 1)):
                s0 = q * QT + (j << (k + 1))
                for part in range(3):
                    low[OFF_NODE + part * NODES + node_row(k, j), q, s0:s0 + (1 << k)] = 1.0
    c["low_sel"] = low.reshape(P, NQ * P)
    hi = np.zeros((P, NT + 1, P), np.float32)
    for t in range(NT):
        for part in range(3):
            for node, (s0, s1) in enumerate(((0, QT), (2 * QT, 3 * QT), (0, 2 * QT))):
                hi[high_row(t, node) + part, t, s0:s1] = 1.0
            hi[OFF_TOP + part, NT, :] = 1.0
    c["high_sel"] = hi.reshape(P, (NT + 1) * P)
    ind = np.zeros((P, H), np.float32)
    for r in range(3 * H):
        ind[r, r % H] = 1.0
    c["head_ind"] = ind
    before = np.zeros((P, NE, NE), np.float32)
    for e in range(NE):
        before[:, e, :e] = 1.0
    c["before"] = before.reshape(P, NE * NE)
    return c


def node_row(k, j):
    return sum(QT >> (i + 1) for i in range(k)) + j


def high_row(t, node):
    return OFF_HIGH + 3 * (NHI * t + node)


def build(nc, d, out, n_batch=BATCH, layers="afbf"):
    ctx = ExitStack()
    with ctx:
        def sb(name, shape, dt=F32):
            return ctx.enter_context(nc.sbuf_tensor(name, shape, dt))

        def ring(name, n, shape, dt=F32):
            return Slots([sb(f"{name}{i}", shape, dt) for i in range(n)])

        def line(name):
            return [ctx.enter_context(nc.semaphore(name)), 0]

        pe, act, dve, pool, sp = (Queue(ctx.enter_context(nc.semaphore(n)))
                                  for n in ("pe_done", "act_done", "dve_done", "pool_done", "sp_done"))

        const_line = line("const_loaded")
        loaded = {}

        def load(name, shape, src, dt=F32):
            t = sb("c_" + name, shape, dt)
            sp.dma(const_line, t[tuple(slice(None) for _ in shape)], src)
            loaded[name] = t
            return t

        def row_bc(ap, n):
            return dram(ap, 0, [[0, P], [1, n]])

        w_in = load("w_in", [P, DIM + CONV], d["in_wT"])
        w_small = load("w_small", [P, NSML], d["small_wT"])
        b_small = load("b_small", [P, NSML], row_bc(d["small_b"], NSML))
        dt_bias = load("dt_bias", [P, H], row_bc(d["dt_bias"], H))
        lvl_scale = load("lvl_scale", [P, (NLV + 1) * H], row_bc(d["L_lvl"], (NLV + 1) * H))
        neg_a = load("neg_a", [P, H], row_bc(d["A_log"], H))
        d_skip = load("d_skip", [P, H], row_bc(d["D"], H))
        b_in = load("b_in", [P, 2 * NF + 2], d["in_b_cols"])
        conv_w = load("conv_w", [P, NF + 2, KCONV], d["conv_cols"])
        w_out = load("w_out", [P, NF, HID], d["out_wT"])
        norm_w = load("norm_w", [P, NF], d["norm_cols"])
        b_out = load("b_out", [P, HID], row_bc(d["out_b"], HID))
        ident = load("ident", [P, P], d["ident"])
        tri = load("tri", [P, P], d["tri"])
        before = load("before", [P, NE * NE], d["before"])
        head_ind = load("head_ind", [P, H], d["head_ind"])
        w_q, w_k, w_v, w_o = (load(n, [P, P], d[n]) for n in ("Wq", "Wk", "Wv", "Wo"))
        b_q, b_k = (load(n, [P, 1], d[n]) for n in ("bq", "bk"))
        b_v, b_o, ln1_g, ln1_b, ln2_g, ln2_b, mix_g, mix_b = (
            load(n, [P, HID], row_bc(d[n], HID))
            for n in ("bv", "bo", "ln1_g", "ln1_b", "ln2_g", "ln2_b", "gamma", "beta"))
        w_gate = load("w_gate", [P, NE], d["gW"])
        b_gate = load("b_gate", [P, NE], row_bc(d["gb"], NE))
        w_1 = load("w_1", [P, NE, FF], d["W1"])
        b_1 = load("b_1", [P, NE * FF // P], d["b1_cols"])
        w_2 = load("w_2", [P, NE * FF // P, HID], d["W2"])
        b_2 = load("b_2", [NE, HID], d["b2"])
        w_mix = load("w_mix", [P, NG * HID], d["gate_WT"])
        w_val = load("w_val", [P, HID], d["value_WT"])
        consts = (const_line[0], const_line[1])

        x_ring = ring("x_", 5, [P, GT, HID])
        xn_a = sb("xn_a", [P, NT, HID])
        xnT_a = sb("xnT_a", [P, T])
        SPL = sb("SPL", [P, NT, NSML])
        Z = sb("Z", [P, NF, T])
        z_flat = Z[:, :, :].rearrange("p f t -> p (f t)")
        U, W1t, W2t = (z_flat[:, k * NT * NSML:(k + 1) * NT * NSML].rearrange("p (i c) -> p i c", i=NT) for k in range(3))
        CL = W1t[:, :, 0:NLV * H].rearrange("p i (l h) -> p i l h", h=H)
        z_at = 3 * NT * NSML
        g_t, gr, ln_dt = (z_flat[:, z_at + k * NT * H:z_at + (k + 1) * NT * H].rearrange("p (i h) -> p i h", i=NT)
                          for k in range(3))
        z_at += 3 * NT * H
        c_parts = z_flat[:, z_at:z_at + NT * 3 * NLV * H // 2].bitcast(BF16).rearrange("p (i a c) -> p i a c", i=NT, a=3)
        gc = sb("gc", [P, NT, H])
        s_parts = sb("s_parts", [P, NT, 3, H], BF16)
        ccoef = sb("ccoef", [P, NT, H])
        qk_diag = sb("qk_diag", [P, NT])
        pad_ring = ring("pad", 2, [P, KCONV - 1 + T])
        conv_ring = ring("conv", 4, [P, T])
        xs_ring = ring("xs", 2, [P, 2, T])
        bmT, cmT = sb("bmT", [P, T]), sb("cmT", [P, T])
        QK = sb("QK", [P, 3, P])
        X = sb("X", [P, NT, DIM])
        own_ring = ring("own", 2, [P, HG * HD])
        low_bufs = [sb(f"low{i}", [P, P, H], BF16) for i in range(NT)]
        high_buf = sb("high", [P, P, H], BF16)
        low_sel = sb("low_sel", [P, NQ, P], BF16)
        high_sel = [sb(f"high_sel{i}", [P, P], BF16) for i in range(3)]
        att_ring = ring("att", 4, [P, HG, P])
        rms = sb("rms", [P, NT])
        ident_bf = sb("ident_bf", [P, P], BF16)
        ones_f = sb("ones_f", [P, P])
        share = sb("share", [P, 1])
        eps_col = sb("eps_col", [P, 1])
        root_v, root_t = sb("root_v", [P, GT]), sb("root_t", [P, GT])
        lnst_a = sb("lnst_a", [P, GT, 6])
        lnmv_a = sb("lnmv_a", [P, GT, 2])
        lnrs_a = sb("lnrs_a", [P, GT])
        osb, qk_scr = xn_a, xn_a[:, 0, :]

        src_t = sb("src_t", [P, GT, HID])
        srcT = sb("srcT", [P, GW])
        qf = sb("qf", [P, GW])
        qr = sb("qr", [P, GW])
        qparts = sb("qparts", [P, 3, GW], BF16)
        q_stack = sb("q_stack", [SLOTROWS, NH, GW], BF16)
        k_stack = sb("k_stack", [SLOTROWS, NH, GW], BF16)
        V9 = sb("V9", [P, GT, NH, 32])
        nmax = sb("nmax", [P, GT, NH])
        nmax_bf = sb("nmax_bf", [P, GT, NH], BF16)
        maxT = sb("maxT", [NH, GW], BF16)
        pt_ring = ring("pt", 5, [P, 2, T])
        O_sb = sb("O_sb", [P, 4, T])
        rden = sb("rden", [P, NH])
        x1_b = [sb(f"x1_{i}", [P, GT, HID]) for i in range(2)]
        x1T_b = [sb(f"x1T_{i}", [P, GW]) for i in range(2)]
        gate_l = sb("gate_l", [P, GT, NE])
        gate_s = sb("gate_s", [P, GT])
        w_e_b = [sb(f"w_e{i}", [P, GT, NE]) for i in range(2)]
        w_eT = qr[0:NE, :]
        h_ring = pt_ring
        ff = sb("ff", [P, GT, HID])
        o_tok = ff
        gate_g, gate_q = (ff[:, :, :].rearrange("p i c -> p (i c)")[:, k * GT * NE * NE:(k + 1) * GT * NE * NE].rearrange(
            "p (i a b) -> p i a b", i=GT, a=NE) for k in range(2))
        v_ext = O_sb[:, :, :].rearrange("p g t -> p (g t)")[:, 0:GS * (T + 2 * MAXSH)].rearrange("p (s t) -> p s t", s=GS)
        mix_acc = x1T_b[0]
        lnst = sb("lnst", [P, GT, 6])
        lnmv = sb("lnmv", [P, GT, 2])
        lnrs = sb("lnrs", [P, GT])

        psA = Slots([ctx.enter_context(nc.psum_tensor(f"psA{i}", [P, 512], F32)) for i in range(4)])
        psB = Slots([ctx.enter_context(nc.psum_tensor(f"psB{i}", [P, 512], F32)) for i in range(4)])

        lvl_scr = [nc.dram_tensor(f"lvl_scr{i}", [3, NLV, P, H], BF16)[:, :, :, :] for i in range(NT)]
        qk_scrd = [nc.dram_tensor(f"qk_scr{i}", [3, P, GW], BF16)[:, :, :] for i in range(2)]
        lvl_out = [line(f"lvl_stored{i}") for i in range(NT)]
        lvl_in = [line(f"lvl_loaded{i}") for i in range(NT)]
        qk_out = [line("q_stored"), line("k_stored")]
        qk_in = [line("q_stacked"), line("k_stacked")]
        max_in = line("max_stacked")
        x_in = [line(f"x_loaded{i}") for i in range(5)]
        x_out = line("x_stored")

        done = {}
        done["ones"] = dve.do(lambda e: e.memset(ones_f[:, :], 1.0))
        done["eps"] = dve.do(lambda e: e.memset(eps_col[:, :], EPS))
        done["share"] = dve.do(lambda e: e.memset(share[:, :], 1.0 / 32))
        done["identb"] = dve.do(lambda e: e.tensor_copy(ident_bf[:, :], ident[:, :]), consts)
        fold = [dve.do(lambda e: e.tensor_tensor(b_small[:, 0:H], b_small[:, 0:H], dt_bias[:, :], ALU.add), consts),
                act.do(lambda e: e.activation(neg_a[:, :], neg_a[:, :], ACT.Exp), consts)]
        fold.append(dve.do(lambda e: e.tensor_scalar(neg_a[:, :], neg_a[:, :], -1.0, None, ALU.mult), fold[1]))
        for f in range(NF):
            m = dve.do(lambda e, f=f: e.tensor_scalar(w_out[:, f, :], w_out[:, f, :], norm_w[:, f:f + 1], None, ALU.mult))
            fold.append(m)
        done["fold"] = fold[-1]
        setup_line = line("setup_loaded")
        zf = Z[:, :, :].rearrange("p f t -> p (f t)")
        l = sp.dma(setup_line, zf[:, 0:NQ * P], d["low_sel"])
        l = sp.dma(setup_line, zf[:, NQ * P:(NQ + NT + 1) * P], d["high_sel"])
        dve.do(lambda e: e.tensor_copy(low_sel[:, :, :].rearrange("p q s -> p (q s)"), zf[:, 0:NQ * P]), l)
        for i in range(3):
            o = (NQ + i) * P
            done["z_free"] = dve.do(lambda e, i=i, o=o: e.tensor_copy(high_sel[i][:, :], zf[:, o:o + P]))
        done["sel"] = done["z_free"]
        z0 = pool.do(lambda e: e.memset(high_buf[:, :, :], 0.0))
        done["high0"] = pool.do(lambda e: e.tensor_copy(high_buf[0:3 * H, :, :], bc(head_ind[0:3 * H, :], 1, P)), z0, consts)
        for lb in low_bufs:
            z0 = pool.do(lambda e, lb=lb: e.memset(lb[:, :, :], 0.0), done["high0"])
            for q in range(NQ):
                done["low0"] = pool.do(lambda e, lb=lb, q=q: e.tensor_copy(
                    lb[0:QT, q * QT:(q + 1) * QT, :], bc(ident[0:QT, 0:QT], 2, H)), z0)
        for pad, _ in pad_ring.free:
            done["pad0"] = dve.do(lambda e, pad=pad: e.memset(pad[:, 0:KCONV - 1], 0.0))
        for st in (q_stack, k_stack):
            z0 = pool.do(lambda e, st=st: e.memset(st[:, :, :], 0.0), done["low0"])
        done["stack0"] = pool.do(lambda e: e.memset(k_stack[64:SLOTROWS, :, :], 1.0), z0)
        z0 = pool.do(lambda e: e.memset(V9[:, :, :, :], 0.0), done["stack0"])
        done["v9"] = pool.do(lambda e: e.memset(V9[:, :, :, AD:AD + 1], 1.0), z0)

        def layer_norm_stats(x, n, st, mv, rs, *marks, by_newton=False):
            for i in range(n):
                m = dve.do(lambda e, i=i: e.bn_stats(st[:, i, :], x[:, i, :]), *marks)
            for i in range(n):
                m = dve.do(lambda e, i=i: e.bn_aggr(mv[:, i, :], st[:, i, :]), m)
            if not by_newton:
                m = act.do(lambda e: e.activation(rs[:, 0:n], mv[:, 0:n, 1], ACT.Ln, bias=eps_col[:, :]), m, done["eps"],
                           rs_free.get(id(rs)))
                return act.do(lambda e: e.activation(rs[:, 0:n], rs[:, 0:n], ACT.Exp, scale=-0.5), m)
            v, t = root_v[:, 0:n], root_t[:, 0:n]
            m = dve.do(lambda e: e.tensor_scalar(v, mv[:, 0:n, 1], EPS, None, ALU.add), m, rs_free.get("v"))
            m1 = dve.do(lambda e: e.tensor_scalar(t.bitcast(I32), v.bitcast(I32), 1, None, ALU.logical_shift_right), m)
            m1 = dve.do(lambda e: e.tensor_scalar(rs[:, 0:n].bitcast(I32), t.bitcast(I32), -1.0, float(ROOT_GUESS),
                                                  ALU.mult, ALU.add), m1)
            m = pool.do(lambda e: e.tensor_scalar(v, v, -0.5, None, ALU.mult), m1)
            for _ in range(3):
                m = pool.do(lambda e: e.tensor_tensor(t, rs[:, 0:n], rs[:, 0:n], ALU.mult), m, m1)
                m = pool.do(lambda e: e.tensor_tensor(t, t, v, ALU.mult), m)
                m = pool.do(lambda e: e.tensor_scalar(t, t, 1.5, None, ALU.add), m)
                m = pool.do(lambda e: e.tensor_tensor(rs[:, 0:n], rs[:, 0:n], t, ALU.mult), m)
            rs_free["v"] = m
            return m

        rs_free = {}

        def normalise(out_, x, n, mv, rs, m_rs, *marks):
            for i in range(n):
                m = dve.do(lambda e, i=i: e.tensor_scalar(out_[:, i, :], x[:, i, :], mv[:, i, 0:1], rs[:, i:i + 1],
                                                          ALU.subtract, ALU.mult), m_rs, *marks)
            rs_free[id(rs)] = m
            return m

        def transpose_tiles(out_, x, n, ps, m_x, *marks):
            bank, free = ps.take()
            for i in range(n):
                m = pe.do(lambda e, i=i: e.transpose(bank[:, i * P:(i + 1) * P], x[:, i, :], ident[:, :]),
                          m_x, consts, *free)
            m = act.do(lambda e: e.activation(out_[:, 0:n * P], bank[:, 0:n * P], ACT.Copy), m, *marks)
            ps.give(bank, m)
            return m

        last = {}

        def ssm_gates(x, m_x):
            L = last.get
            m_rs = layer_norm_stats(x, NT, lnst_a, lnmv_a, lnrs_a, *m_x)
            m = normalise(xn_a, x, NT, lnmv_a, lnrs_a, m_rs, L("xn_a"))
            m_xnT = transpose_tiles(xnT_a, xn_a, NT, psA, m, L("xnT_a"))
            last["xn_a"] = m_xnT
            yield
            for i in range(NT):
                bank, free = psA.take()
                m = pe.do(lambda e, i=i, bank=bank: e.matmul(bank[:, 0:NSML], xnT_a[:, i * P:(i + 1) * P], w_small[:, :],
                                                             start=True, stop=True), m_xnT, *free)
                m = dve.do(lambda e, i=i, bank=bank: e.tensor_tensor(U[:, i, :], bank[:, 0:NSML], b_small[:, :], ALU.add),
                           m, L("Z"), fold[0], done["z_free"])
                psA.give(bank, m)
            m = dve.do(lambda e: e.tensor_tensor(U[:, :, H:], U[:, :, H:], bc(lvl_scale[:, :], 1, NT), ALU.mult), m, consts)
            yield
            m = act.do(lambda e: e.activation(W1t[:, :, :], U[:, :, :], ACT.Abs), m)
            m_e = act.do(lambda e: e.activation(W1t[:, :, :], W1t[:, :, :], ACT.Exp, scale=-1.0), m)
            m_w = dve.do(lambda e: e.tensor_scalar(W2t[:, :, :], W1t[:, :, :], 1.0, None, ALU.add), m_e)
            yield
            m_ln = act.do(lambda e: e.activation(SPL[:, :, :], W2t[:, :, :], ACT.Ln), m_w, L("SPL"))
            m_d = dve.do(lambda e: e.tensor_scalar(W2t[:, :, :], W2t[:, :, :], -1.0, TINY, ALU.add, ALU.max), m_ln)
            m_d = dve.do(lambda e: e.reciprocal(W2t[:, :, :], W2t[:, :, :]), m_d)
            m = dve.do(lambda e: e.scalar_tensor_tensor(out=W1t[:, :, :], in0=SPL[:, :, :], scalar=TINY, in1=W1t[:, :, :],
                                                        op0=ALU.max, op1=ALU.mult), m_ln)
            m = dve.do(lambda e: e.tensor_tensor(W1t[:, :, :], W1t[:, :, :], W2t[:, :, :], ALU.mult), m, m_d)
            m_sp = dve.do(lambda e: e.scalar_tensor_tensor(out=SPL[:, :, :], in0=U[:, :, :], scalar=0.0, in1=W1t[:, :, :],
                                                           op0=ALU.max, op1=ALU.add), m)
            dt = SPL[:, :, 0:H]
            m_g = dve.do(lambda e: e.tensor_tensor(g_t[:, :, :], dt, bc(neg_a[:, :], 1, NT), ALU.mult), m_sp, fold[2])
            yield
            bank, free = psA.take()
            for i in range(NT):
                for j in range(i + 1):
                    m = pe.do(lambda e, i=i, j=j, bank=bank: e.matmul(
                        bank[:, i * H:(i + 1) * H], (tri if i == j else ones_f)[:, :], g_t[:, j, :],
                        start=(j == 0), stop=(j == i)), m_g, done["ones"], *free)
            m_gc = dve.do(lambda e, bank=bank: e.tensor_copy(gc[:, :, :].rearrange("p i h -> p (i h)"), bank[:, 0:NT * H]),
                          m, L("gc"))
            psA.give(bank, m_gc)
            m = dve.do(lambda e: e.tensor_scalar(CL[:, :, :, :].rearrange("p i l h -> p i (l h)"), SPL[:, :, 2 * H:],
                                                 1e-37, None, ALU.max), m_sp)
            m = act.do(lambda e: e.activation(CL[:, :, :, :], CL[:, :, :, :], ACT.Ln), m)
            m_ld = dve.do(lambda e: e.tensor_scalar(ln_dt[:, :, :], dt, 1e-37, None, ALU.max), m_sp, L("gc"))
            m_ld = act.do(lambda e: e.activation(ln_dt[:, :, :], ln_dt[:, :, :], ACT.Ln), m_ld)
            for i in range(NT):
                m_c = dve.do(lambda e, i=i: e.tensor_tensor(CL[:, i, :, :], CL[:, i, :, :], bc(gc[:, i, :], 1, NLV), ALU.add),
                             m, m_gc)
            yield
            cl = CL[:, :, :, :].rearrange("p i l h -> p i (l h)")
            cr = W2t[:, :, 0:NLV * H]
            m = dve.do(lambda e: e.tensor_copy(c_parts[:, :, 0, :], cl), m_c, *last.get("c_parts", ()))
            m2 = dve.do(lambda e: e.tensor_tensor(gc[:, :, :], ln_dt[:, :, :], gc[:, :, :], ALU.subtract), m_c, m_ld)
            m = dve.do(lambda e: e.tensor_tensor(cr, cl, c_parts[:, :, 0, :], ALU.subtract), m)
            m2 = dve.do(lambda e: e.tensor_copy(s_parts[:, :, 0, :], gc[:, :, :]), m2, L("s_parts"))
            m = dve.do(lambda e: e.tensor_copy(c_parts[:, :, 1, :], cr), m)
            m2 = dve.do(lambda e: e.tensor_tensor(gr[:, :, :], gc[:, :, :], s_parts[:, :, 0, :], ALU.subtract), m2)
            m_cp = dve.do(lambda e: e.tensor_tensor(c_parts[:, :, 2, :], cr, c_parts[:, :, 1, :], ALU.subtract), m)
            m2 = dve.do(lambda e: e.tensor_copy(s_parts[:, :, 1, :], gr[:, :, :]), m2)
            m_s = dve.do(lambda e: e.tensor_tensor(s_parts[:, :, 2, :], gr[:, :, :], s_parts[:, :, 1, :], ALU.subtract), m2)
            last["gc"], last["U"] = m_s, m_s
            stored = [sp.dma(lvl_out[i], dram(lvl_scr[i], 0, [[H, P], [P * H, 3 * NLV], [1, H]]),
                             c_parts[:, i, :, :].rearrange("p a (l h) -> p (a l) h", h=H), m_cp, last.get(f"scr{i}"))
                      for i in range(NT)]
            last["c_parts"] = tuple(stored)
            bank, free = psA.take()
            bview = bank[:, :].bitcast(BF16)
            for i in range(NT):
                m = pe.do(lambda e, i=i, bview=bview: e.transpose(
                    bview[0:3 * H, i * P:(i + 1) * P], s_parts[:, i, :, :].rearrange("p a h -> p (a h)"), ident_bf[:, :]),
                    m_s, done["identb"], *free)
            last["s_parts"] = m
            for i, src in enumerate((0, 1, 0)):
                m_hs = dve.do(lambda e, i=i, src=src, bview=bview: e.tensor_copy(
                    high_sel[i][0:3 * H, :], bview[0:3 * H, src * P:(src + 1) * P]), m, L("high_sel"), done["sel"])
            psA.give(bank, m_hs)
            plane = NLV * P * H
            m_ld = []
            for t in range(NT):
                w = (stored[t], L(f"low{t}"), L("high"), done["low0"], done["high0"])
                for k in range(LOW):
                    for j in range(QT >> (k + 1)):
                        r, t0, n_t = OFF_NODE + node_row(k, j), (j << (k + 1)) + (1 << k), 1 << k
                        sp.dma(lvl_in[t], low_bufs[t][r:r + 2 * NODES + 1:NODES, :, :].rearrange(
                            "a (q i) h -> a q (i h)", q=NQ)[:, :, t0 * H:(t0 + n_t) * H],
                            dram(lvl_scr[t], (k * P + t0) * H, [[plane, 3], [QT * H, NQ], [1, n_t * H]]), *w)
                for node, (k, t0, n_t) in enumerate(((LOW, QT, QT), (LOW, 3 * QT, QT), (LOW + 1, 2 * QT, 2 * QT))):
                    r = high_row(t, node)
                    m = sp.dma(lvl_in[t], high_buf[r:r + 3, t0:t0 + n_t, :].rearrange("a t h -> a (t h)"),
                               dram(lvl_scr[t], (k * P + t0) * H, [[plane, 3], [1, n_t * H]]), *w)
                if t:
                    m = sp.dma(lvl_in[t], high_buf[OFF_TOP:OFF_TOP + 3, :, :].rearrange("a t h -> a (t h)"),
                               dram(lvl_scr[t], (NLV - 1) * P * H, [[plane, 3], [1, P * H]]), *w)
                last[f"scr{t}"] = m
                m_ld.append(m)
                yield
            return m_xnT, m_sp, m_hs, m_ld

        def ssm_project(gates):
            m_xnT, m_sp, m_hs, m_ld = gates
            L = last.get

            def conv_front(c):
                bank, free = psA.take()
                m = pe.do(lambda e: e.matmul(bank[:, 0:T], w_in[:, DIM + c * P:DIM + (c + 1) * P], xnT_a[:, :],
                                             start=True, stop=True), m_xnT, consts, *free)
                pad, pfree = pad_ring.take()
                m = act.do(lambda e: e.activation(pad[:, KCONV - 1:], bank[:, 0:T], ACT.Identity,
                                                  bias=b_in[:, NF + c:NF + c + 1]), m, done["pad0"], *pfree)
                psA.give(bank, m)
                cv, cfree = conv_ring.take()
                m = dve.do(lambda e: e.tensor_scalar(cv[:, :], pad[:, 0:T], conv_w[:, c, 0:1], None, ALU.mult), m, *cfree)
                for k in range(1, KCONV):
                    m = dve.do(lambda e, k=k: e.scalar_tensor_tensor(out=cv[:, :], in0=pad[:, k:k + T],
                                                                     scalar=conv_w[:, c, k:k + 1], in1=cv[:, :],
                                                                     op0=ALU.mult, op1=ALU.add), m)
                pad_ring.give(pad, m)
                return cv, m

            def conv_silu(front_, out_, *marks):
                cv, m = front_
                m = act.do(lambda e: e.activation(out_, cv[:, :], ACT.Silu), m, *marks)
                conv_ring.give(cv, m)
                return m

            fb, fc = conv_front(NF), conv_front(NF + 1)
            marks = {}
            fronts, shown = {}, {}
            n2 = NF // 2
            for step in range(n2 + 2):
                if step < n2:
                    fronts[step] = [conv_front(2 * step), conv_front(2 * step + 1)]
                if step == 0:
                    m_b = conv_silu(fb, bmT[:, :], L("bmT"))
                    m_cc = conv_silu(fc, cmT[:, :], L("bmT"))
                if 1 <= step <= n2:
                    f2 = step - 1
                    xb, xfree = xs_ring.take()
                    for k in range(2):
                        m = conv_silu(fronts[f2][k], xb[:, k, :], *xfree)
                    shown[f2] = (xb, m)
                if step < n2:
                    for f in (2 * step, 2 * step + 1):
                        bank, free = psA.take()
                        m = pe.do(lambda e, f=f, bank=bank: e.matmul(bank[:, 0:T], w_in[:, f * P:(f + 1) * P], xnT_a[:, :],
                                                                     start=True, stop=True), *free)
                        last["xnT_a"] = m
                        m_z = act.do(lambda e, f=f, bank=bank: e.activation(Z[:, f, :], bank[:, 0:T], ACT.Silu,
                                                                            bias=b_in[:, f:f + 1]), m, L("U"), *last["c_parts"])
                        psA.give(bank, m_z)
                if step == 1:
                    bank, free = psA.take()
                    for k, (s_, t_) in enumerate(((0, 0), (1, 1), (0, 1))):
                        m = pe.do(lambda e, k=k, s_=s_, t_=t_, bank=bank: e.matmul(
                            bank[:, k * P:(k + 1) * P], bmT[:, s_ * P:(s_ + 1) * P], cmT[:, t_ * P:(t_ + 1) * P],
                            start=True, stop=True), m_b, m_cc, *free)
                    last["bmT"] = m
                    m_qk = dve.do(lambda e, bank=bank: e.tensor_copy(QK[:, :, :].rearrange("p k t -> p (k t)"),
                                                                     bank[:, 0:3 * P]), m, L("QK"))
                    psA.give(bank, m_qk)
                    m = m_qk
                    for i in range(NT):
                        m = dve.do(lambda e, i=i: e.tensor_tensor(qk_scr, QK[:, i, :], ident[:, :], ALU.mult), m, last["xn_a"])
                        m = dve.do(lambda e, i=i: e.tensor_reduce(qk_diag[:, i:i + 1], qk_scr, AX.X, ALU.add), m)
                    for i in range(NT):
                        m1 = dve.do(lambda e, i=i: e.scalar_tensor_tensor(
                            out=ccoef[:, i, :], in0=SPL[:, i, H:2 * H], scalar=qk_diag[:, i:i + 1], in1=SPL[:, i, 0:H],
                            op0=ALU.mult, op1=ALU.mult), m, L("ccoef"))
                    last["xn_a"] = m
                    m_cf = dve.do(lambda e: e.tensor_tensor(ccoef[:, :, :], ccoef[:, :, :], bc(d_skip[:, :], 1, NT), ALU.add), m1)
                if step >= 2:
                    f2 = step - 2
                    xb, m_s2 = shown.pop(f2)
                    bank, free = psA.take()
                    for i in range(NT):
                        for k in range(2):
                            m = pe.do(lambda e, i=i, k=k, bank=bank, xb=xb: e.transpose(
                                bank[:, i * 2 * P + k * P:i * 2 * P + (k + 1) * P], xb[:, k, i * P:(i + 1) * P],
                                ident[:, :]), m_s2, *free)
                    xs_ring.give(xb, m)
                    m_x = act.do(lambda e, bank=bank, f2=f2: e.activation(
                        X[:, :, f2 * 2 * P:(f2 + 1) * 2 * P], bank[:, :].rearrange("p (i c) -> p i c", i=NT), ACT.Copy),
                        m, L("X"))
                    psA.give(bank, m_x)
                yield
            last["SPL"] = m_cf
            return m_z, m_x, m_qk, m_cf

        def ssm_attend(x, m_xin, gates, proj):
            m_xnT, m_sp, m_hs, m_ld = gates
            m_z, m_x_all, m_qk, m_cf = proj
            L = last.get
            ready = {}

            def weights(t, hg):
                h0, tiles = hg * HG, []
                for s_ in ([t] if t == 0 else [0, t]):
                    diag = s_ == t
                    att, afree = att_ring.take()
                    sel = high_sel[t if diag else 2]
                    for half in range(2):
                        bank, free = psA.take()
                        bv = bank[:, :].rearrange("p (t h) -> p t h", h=HG)
                        c = half * 64
                        m = pe.do(lambda e, bv=bv, c=c, sel=sel, diag=diag, h0=h0: e.matmul(
                            bv, sel[0:R_HIGH, :], high_buf[0:R_HIGH, c:c + 64, h0:h0 + HG],
                            start=True, stop=not diag, skip_group_check=True), *m_ld, m_hs, *free)
                        if diag:
                            for q in (2 * half, 2 * half + 1):
                                m = pe.do(lambda e, bv=bv, c=c, q=q, h0=h0, t=t: e.matmul(
                                    bv[:, q * QT - c:(q + 1) * QT - c, :], low_sel[0:R_LOW, q, :],
                                    low_bufs[t][0:R_LOW, q * QT:(q + 1) * QT, h0:h0 + HG],
                                    start=False, stop=(q % 2 == 1), skip_group_check=True))
                            last[f"low{t}"] = m
                        m_e = act.do(lambda e, bv=bv, c=c, att=att: e.activation(
                            att[:, :, c:c + 64].rearrange("p h t -> p t h"), bv, ACT.Exp), m, *afree)
                        psA.give(bank, m_e)
                    last["high"] = last["high_sel"] = m
                    kq = t if diag else 2
                    m_a = dve.do(lambda e, att=att, kq=kq: e.tensor_tensor(
                        att[:, :, :], att[:, :, :], bc(QK[:, kq, :], 1, HG), ALU.mult), m_e, m_qk)
                    tiles.append((att, s_))
                last["QK"] = m_a
                own, ofree = own_ring.take()
                m_own = pool.do(lambda e, own=own, t=t, h0=h0: e.tensor_tensor(
                    own[:, :].rearrange("p (h c) -> p h c", c=HD),
                    X[:, t, h0 * HD:(h0 + HG) * HD].rearrange("p (h c) -> p h c", c=HD),
                    bc(ccoef[:, t, h0:h0 + HG], 2, HD), ALU.mult), m_x_all, m_cf, *ofree)
                last["ccoef"] = m_own
                ready[t, hg] = (tiles, own, m_a, m_own)

            def sums(t, hg):
                tiles, own, m_a, m_own = ready.pop((t, hg))
                bank, free = psA.take()
                for f in range(HG // 2):
                    fc = (hg * HG // 2 + f) * P
                    pe.run(lambda e, bank=bank, f=f, own=own: e.matmul(
                        bank[:, f * P:(f + 1) * P], own[:, f * P:(f + 1) * P], ident[:, :], start=True, stop=False,
                        skip_group_check=True), m_own, *free)
                    for att, s_ in tiles:
                        for k in range(2):
                            mm = (lambda e, f=f, k=k, att=att, s_=s_, bank=bank, fc=fc: e.matmul(
                                bank[k * HD:(k + 1) * HD, f * P:(f + 1) * P], X[:, s_, fc + k * HD:fc + (k + 1) * HD],
                                att[:, 2 * f + k, :], start=False, stop=(s_ == t), skip_group_check=True))
                            m = pe.do(mm, m_a, m_x_all)
                for att, _ in tiles:
                    att_ring.give(att, m)
                own_ring.give(own, m)
                last["X"] = m
                f0 = hg * HG // 2
                m = dve.do(lambda e, bank=bank, f0=f0: e.tensor_tensor(
                    Z[:, f0:f0 + HG // 2, t * P:(t + 1) * P], bank[:, :].rearrange("p (f t) -> p f t", t=P),
                    Z[:, f0:f0 + HG // 2, t * P:(t + 1) * P], ALU.mult), m, m_z)
                psA.give(bank, m)
                return m

            units = [(t, hg) for t in range(NT) for hg in range(H // HG)]
            for k, unit in enumerate(units + [None]):
                if unit:
                    weights(*unit)
                if k:
                    m_yz = sums(*units[k - 1])
                yield

            bank, free = psA.take()
            for g4 in range(NF // 4):
                sqa, sfree = att_ring.take()
                sq = sqa[:, :, :].rearrange("p (a b) t -> p a (b t)", b=NT)
                m = act.do(lambda e, g4=g4, sq=sq: e.activation(sq, Z[:, 4 * g4:4 * g4 + 4, :], ACT.Square), m_yz, *sfree)
                for j in range(4):
                    m = pe.do(lambda e, j=j, sq=sq, g4=g4, bank=bank: e.matmul(
                        bank[32 * j:32 * j + 32, 0:T], ones_f[:, 0:32], sq[:, j, :], start=(g4 == 0),
                        stop=(g4 == NF // 4 - 1), skip_group_check=True), m, *free)
                att_ring.give(sqa, m)
            ssq, qfree = conv_ring.take()
            m = act.do(lambda e, bank=bank: e.activation(ssq[:, :], bank[:, 0:T], ACT.Copy), m, *qfree)
            yield
            obank, ofree = psA.take()
            for i in range(NT):
                for f in range(NF):
                    m_op = pe.do(lambda e, i=i, f=f: e.matmul(
                        obank[:, i * P:(i + 1) * P], Z[:, f, i * P:(i + 1) * P], w_out[:, f, :],
                        start=(f == 0), stop=(f == NF - 1)), m_yz, done["fold"], *ofree)
            last["Z"] = m_op
            for i in range(NT):
                m_ss = pe.do(lambda e, i=i: e.matmul(bank[:, T + i:T + i + 1], ssq[:, i * P:(i + 1) * P],
                                                     share[:, :], start=True, stop=True, skip_group_check=True),
                             m, done["share"])
            conv_ring.give(ssq, m_ss)
            m = act.do(lambda e: e.activation(rms[:, :], bank[:, T:T + NT], ACT.Ln, scale=1.0 / DIM, bias=eps_col[:, :]),
                       m_ss, L("rms"), done["eps"])
            psA.give(bank, m)
            m_rms = act.do(lambda e: e.activation(rms[:, :], rms[:, :], ACT.Exp, scale=-0.5), m)
            yield
            for i in range(NT):
                m2 = dve.do(lambda e, i=i: e.scalar_tensor_tensor(
                    out=osb[:, i, :], in0=obank[:, i * P:(i + 1) * P], scalar=rms[:, i:i + 1], in1=b_out[:, :],
                    op0=ALU.mult, op1=ALU.add), m_op, m_rms, L("xn_a"))
            psA.give(obank, m2)
            last["rms"] = m2
            m2 = dve.do(lambda e: e.tensor_tensor(x[:, :, :], x[:, :, :], osb[:, :, :], ALU.add), m2, *m_xin)
            last["xn_a"] = m2
            yield
            return m2

        late = {}

        def affine(y, g, b, m):
            m = dve.do(lambda e: e.tensor_tensor(y[:, :, :], y[:, :, :], bc(g[:, :], 1, GT), ALU.mult), m)
            return dve.do(lambda e: e.tensor_tensor(y[:, :, :], y[:, :, :], bc(b[:, :], 1, GT), ALU.add), m)

        def ffn_attend(x, m_x, lay):
            L = late.get
            x1, x1T, w_e = x1_b[lay], x1T_b[lay], w_e_b[lay]
            m_rs = layer_norm_stats(x, GT, lnst, lnmv, lnrs, *m_x)
            m_src = normalise(src_t, x, GT, lnmv, lnrs, m_rs, L("src_t"))
            m_sT = transpose_tiles(srcT, src_t, GT, psB, m_src, L("srcT"))
            yield
            m_max_ready = None
            for side, (w, b, st) in enumerate(((w_q, b_q, q_stack), (w_k, b_k, k_stack))):
                bank, free = psB.take()
                m = pe.do(lambda e, w=w, bank=bank: e.matmul(bank[:, 0:GW], w[:, :], srcT[:, :], start=True, stop=True),
                          m_sT, *free)
                m = act.do(lambda e, b=b, bank=bank: e.activation(qf[:, :], bank[:, 0:GW], ACT.Identity, bias=b[:, 0:1]),
                           m, L("qf"))
                psB.give(bank, m)
                m = dve.do(lambda e: e.tensor_copy(qparts[:, 0, :], qf[:, :]), m, L("qparts"))
                m = dve.do(lambda e: e.tensor_tensor(qr[:, :], qf[:, :], qparts[:, 0, :], ALU.subtract), m, L("w_eT"))
                m = dve.do(lambda e: e.tensor_copy(qparts[:, 1, :], qr[:, :]), m)
                m = dve.do(lambda e: e.tensor_tensor(qparts[:, 2, :], qr[:, :], qparts[:, 1, :], ALU.subtract), m)
                late["qf"] = m
                scr = qk_scrd[side]
                m = sp.dma(qk_out[side], scr.rearrange("a p t -> p a t"), qparts[:, :, :], m, L("stacked"))
                late["qparts"] = m
                for i in range(3):
                    for j in range(3):
                        r = (3 * i + j) * AD
                        part = i if side == 0 else j
                        m_st = sp.dma(qk_in[side], st[r:r + AD, :, :],
                                      dram(scr, part * P * GW, [[GW, AD], [AD * GW, NH], [1, GW]]),
                                      m, L("stack_free"), done["stack0"])
                if side == 0:
                    m_qst = m_st
                yield
            late["stacked"] = m_st
            bank, free = psB.take()
            for i in range(GT):
                m = pe.do(lambda e, i=i, bank=bank: e.matmul(bank[:, i * P:(i + 1) * P], srcT[:, i * P:(i + 1) * P], w_v[:, :],
                                                             start=True, stop=True), *free)
            late["srcT"] = m
            for i in range(GT):
                m_v = dve.do(lambda e, i=i, bank=bank: e.tensor_tensor(
                    V9[:, i, :, 0:AD], bank[:, i * P:(i + 1) * P].rearrange("p (h c) -> p h c", c=AD),
                    b_v[:, :].rearrange("p (h c) -> p h c", c=AD), ALU.add), m, L("V9"), done["v9"])
            psB.give(bank, m_v)
            yield
            for i in range(GT):
                s0 = (i // NT) * T
                for h2 in range(NH // 2):
                    bank, free = psB.take()
                    for k in range(2):
                        h = 2 * h2 + k
                        m = pe.do(lambda e, h=h, k=k, i=i, s0=s0, bank=bank: e.matmul(
                            bank[:, k * T:(k + 1) * T], q_stack[0:ROW_MAX, h, i * P:(i + 1) * P],
                            k_stack[0:ROW_MAX, h, s0:s0 + T], start=True, stop=True), m_qst, m_st, *free)
                    m = dve.do(lambda e, i=i, h2=h2, bank=bank: e.tensor_reduce(
                        nmax[:, i, 2 * h2:2 * h2 + 2], bank[:, :].rearrange("p (h k) -> p h k", k=T), AX.X, ALU.max),
                        m, L("nmax"))
                    psB.give(bank, m)
                    if h2 % 4 == 3:
                        yield
            m = dve.do(lambda e: e.tensor_scalar(nmax_bf[:, :, :], nmax[:, :, :], -1.0, None, ALU.mult), m, L("nmax"))
            bank, free = psB.take()
            bview = bank[:, :].bitcast(BF16)
            for i in range(GT):
                m2 = pe.do(lambda e, i=i, bview=bview: e.transpose(bview[0:NH, i * P:(i + 1) * P], nmax_bf[:, i, :],
                                                                   ident_bf[:, :]), m, *free)
            late["nmax"] = m2
            m = act.do(lambda e, bview=bview: e.activation(maxT[:, :], bview[0:NH, 0:GW], ACT.Copy), m2, L("maxT"))
            psB.give(bank, m)
            for h in range(NH):
                m_mx = sp.dma(max_in, q_stack[ROW_MAX:ROW_MAX + 1, h, :], maxT[h:h + 1, :], m)
            late["maxT"] = m_mx
            yield
            for s in range(GS):
                for g in range(NH // 4):
                    pts = []
                    for kt in range(NT):
                        for h2 in range(2):
                            bank, free = psB.take()
                            for k in range(2):
                                h = 4 * g + 2 * h2 + k
                                m = pe.do(lambda e, h=h, k=k, kt=kt, s=s, bank=bank: e.matmul(
                                    bank[:, k * T:(k + 1) * T], k_stack[:, h, s * T + kt * P:s * T + (kt + 1) * P],
                                    q_stack[:, h, s * T:(s + 1) * T], start=True, stop=True), m_mx, *free)
                            late["stack_free"] = m
                            pt, pfree = pt_ring.take()
                            m_p = act.do(lambda e, pt=pt, bank=bank: e.activation(
                                pt[:, :, :].rearrange("p h q -> p (h q)"), bank[:, :], ACT.Exp, scale=float(AD) ** -0.5),
                                m, *pfree)
                            psB.give(bank, m_p)
                            pts.append((pt, kt, h2))
                    if g % 2 == 0:
                        obank, ofree = psB.take()
                    c0 = (g % 2) * T
                    for kt in range(NT):
                        for j in range(4):
                            pt = [p_ for p_, kt_, h2_ in pts if kt_ == kt and h2_ == j // 2][0]
                            m = pe.do(lambda e, j=j, kt=kt, pt=pt, s=s, g=g, obank=obank, c0=c0: e.matmul(
                                obank[32 * j:32 * j + 32, c0:c0 + T], V9[:, s * NT + kt, 4 * g + j, :], pt[:, j % 2, :],
                                start=(kt == 0), stop=(kt == NT - 1), skip_group_check=True), m_p, m_v, *ofree)
                    for pt, _, _ in pts:
                        pt_ring.give(pt, m)
                    if g % 2:
                        m_o = dve.do(lambda e, g=g, obank=obank: e.tensor_copy(
                            O_sb[:, g - 1:g + 1, :].rearrange("p g t -> p (g t)"), obank[:, :]), m, L("O_sb"))
                        psB.give(obank, m_o)
                    yield
                late["V9"] = m
                for qt in range(NT):
                    bank, free = psB.take()
                    for g in range(4):
                        m = pe.do(lambda e, g=g, qt=qt, bank=bank: e.transpose(
                            bank[:, g * P:(g + 1) * P], O_sb[:, g, qt * P:(qt + 1) * P], ident[:, :]), m_o, *free)
                    bh = bank[:, :].rearrange("p (h c) -> p h c", c=32)
                    m = dve.do(lambda e, bh=bh: e.reciprocal(rden[:, :], bh[:, :, AD]), m, L("rden"))
                    m = dve.do(lambda e, bh=bh, i=s * NT + qt: e.tensor_tensor(
                        o_tok[:, i, :].rearrange("p (h c) -> p h c", c=AD), bh[:, :, 0:AD], bc(rden[:, :], 2, AD), ALU.mult),
                        m, L("ff"))
                    psB.give(bank, m)
                    late["rden"] = m
                late["O_sb"] = m
            m_oT = transpose_tiles(qf, o_tok, GT, psB, m, late["qf"])
            late["ff"] = m_oT
            bank, free = psB.take()
            for i in range(GT):
                m = pe.do(lambda e, i=i, bank=bank: e.matmul(bank[:, i * P:(i + 1) * P], qf[:, i * P:(i + 1) * P], w_o[:, :],
                                                             start=True, stop=True), m_oT, *free)
            late["qf"] = m
            m = dve.do(lambda e, bank=bank: e.tensor_tensor(x1[:, :, :], bank[:, 0:GW].rearrange("p (i c) -> p i c", c=HID),
                                                            src_t[:, :, :], ALU.add), m, L(("x1", lay)))
            late["src_t"] = m
            psB.give(bank, m)
            m = dve.do(lambda e: e.tensor_tensor(x1[:, :, :], x1[:, :, :], bc(b_o[:, :], 1, GT), ALU.add), m)
            m_rs = layer_norm_stats(x1, GT, lnst, lnmv, lnrs, m)
            m = normalise(x1, x1, GT, lnmv, lnrs, m_rs)
            m_x1 = affine(x1, ln1_g, ln1_b, m)
            m_x1T = transpose_tiles(x1T, x1, GT, psB, m_x1, L(("x1T", lay)))
            yield
            bank, free = psB.take()
            for i in range(GT):
                m = pe.do(lambda e, i=i, bank=bank: e.matmul(bank[:, i * NE:(i + 1) * NE], x1T[:, i * P:(i + 1) * P],
                                                             w_gate[:, :], start=True, stop=True), m_x1T, *free)
            m = dve.do(lambda e, bank=bank: e.tensor_tensor(gate_l[:, :, :], bank[:, 0:GT * NE].rearrange("p (i n) -> p i n", n=NE),
                                                            bc(b_gate[:, :], 1, GT), ALU.add), m)
            psB.give(bank, m)
            m = dve.do(lambda e: e.tensor_reduce(gate_s[:, :], gate_l[:, :, :], AX.X, ALU.max), m)
            m = dve.do(lambda e: e.tensor_tensor(gate_l[:, :, :], gate_l[:, :, :], bc(gate_s[:, :], 2, NE), ALU.subtract), m)
            m = act.do(lambda e: e.activation(gate_l[:, :, :], gate_l[:, :, :], ACT.Exp), m)
            m = dve.do(lambda e: e.tensor_reduce(gate_s[:, :], gate_l[:, :, :], AX.X, ALU.add), m)
            m = dve.do(lambda e: e.reciprocal(gate_s[:, :], gate_s[:, :]), m)
            m = dve.do(lambda e: e.tensor_tensor(gate_l[:, :, :], gate_l[:, :, :], bc(gate_s[:, :], 2, NE), ALU.mult), m)
            mine, other = bc(gate_l[:, :, :], 3, NE), bc(gate_l[:, :, :], 2, NE)
            m1 = dve.do(lambda e: e.tensor_tensor(gate_g[:, :, :, :], other, mine, ALU.is_gt), m, L("ff"))
            m = dve.do(lambda e: e.tensor_tensor(gate_q[:, :, :, :], other, mine, ALU.is_equal), m)
            bf = bc(before[:, :].rearrange("p (a b) -> p a b", b=NE), 1, GT)
            m = dve.do(lambda e: e.tensor_tensor(gate_q[:, :, :, :], gate_q[:, :, :, :], bf, ALU.mult), m)
            m = dve.do(lambda e: e.tensor_tensor(gate_g[:, :, :, :], gate_g[:, :, :, :], gate_q[:, :, :, :], ALU.add), m, m1)
            m = dve.do(lambda e: e.tensor_reduce(w_e[:, :, :], gate_g[:, :, :, :], AX.X, ALU.add), m, L(("w_e", lay)))
            m_w = dve.do(lambda e: e.scalar_tensor_tensor(out=w_e[:, :, :], in0=w_e[:, :, :], scalar=1.5, in1=gate_l[:, :, :],
                                                          op0=ALU.is_lt, op1=ALU.mult), m)
            yield
            return m_x1, m_x1T, m_w

        def ffn_experts(x, m_x, att_marks, lay):
            L = late.get
            x1, x1T, w_e = x1_b[lay], x1T_b[lay], w_e_b[lay]
            m_x1, m_x1T, m_w = att_marks
            bank, free = psB.take()
            for i in range(GT):
                m = pe.do(lambda e, i=i, bank=bank: e.transpose(bank[0:NE, i * P:(i + 1) * P], w_e[:, i, :], ident[:, :]),
                          m_w, *free)
            m = act.do(lambda e, bank=bank: e.activation(w_eT[:, :], bank[0:NE, 0:GW], ACT.Copy), m, L("w_eT"))
            psB.give(bank, m)
            bank, free = psB.take()
            for i in range(GT):
                m2 = pe.do(lambda e, i=i, bank=bank: e.matmul(bank[:, i * P:(i + 1) * P], w_eT[:, i * P:(i + 1) * P], b_2[:, :],
                                                              start=True, stop=True), m, *free)
            late["w_eT"] = m2
            m_ff = dve.do(lambda e, bank=bank: e.tensor_tensor(ff[:, :, :], bank[:, 0:GW].rearrange("p (i c) -> p i c", c=HID),
                                                               x1[:, :, :], ALU.add), m2, m_x1, L("ff"))
            late["x1", lay] = m_ff
            psB.give(bank, m_ff)
            yield
            hidden = {}
            for step in range(NE + 1):
                if step < NE:
                    hb, hfree = h_ring.take()
                    for k in range(2):
                        bank, free = psB.take()
                        m = pe.do(lambda e, ex=step, k=k, bank=bank: e.matmul(
                            bank[:, 0:GW], w_1[:, ex, k * P:(k + 1) * P], x1T[:, :], start=True, stop=True), m_x1T, *free)
                        late["x1T", lay] = m
                        m_h = act.do(lambda e, ex=step, k=k, bank=bank, hb=hb: e.activation(
                            hb[:, k, :], bank[:, 0:GW], ACT.Relu, bias=b_1[:, 2 * ex + k:2 * ex + k + 1]), m, *hfree)
                        psB.give(bank, m_h)
                    hidden[step] = (hb, m_h)
                if step:
                    ex = step - 1
                    hb, m_h = hidden.pop(ex)
                    bank, free = psB.take()
                    for i in range(GT):
                        for k in range(2):
                            m = pe.do(lambda e, ex=ex, i=i, k=k, bank=bank, hb=hb: e.matmul(
                                bank[:, i * P:(i + 1) * P], hb[:, k, i * P:(i + 1) * P], w_2[:, 2 * ex + k, :],
                                start=(k == 0), stop=(k == 1)), m_h, *free)
                    h_ring.give(hb, m)
                    for i in range(GT):
                        m_ff2 = dve.do(lambda e, ex=ex, i=i, bank=bank: e.scalar_tensor_tensor(
                            out=ff[:, i, :], in0=bank[:, i * P:(i + 1) * P], scalar=w_e[:, i, ex:ex + 1], in1=ff[:, i, :],
                            op0=ALU.mult, op1=ALU.add), m, m_ff)
                    psB.give(bank, m_ff2)
                    m_ff = m_ff2
                yield
            late["w_e", lay] = m_ff
            m_rs = layer_norm_stats(ff, GT, lnst, lnmv, lnrs, m_ff, by_newton=True)
            m = normalise(ff, ff, GT, lnmv, lnrs, m_rs)
            m = affine(ff, ln2_g, ln2_b, m)
            m = dve.do(lambda e: e.tensor_tensor(x[:, :, :], x[:, :, :], ff[:, :, :], ALU.add), m, *m_x)
            late["ff"] = m
            yield
            return m

        def mix_layer(x, m_x):
            L = late.get
            m_rs = layer_norm_stats(x, GT, lnst, lnmv, lnrs, *m_x, by_newton=True)
            m = normalise(src_t, x, GT, lnmv, lnrs, m_rs, L("src_t"))
            m_sT = transpose_tiles(srcT, src_t, GT, psB, m, L("srcT"))
            late["src_t"] = m_sT
            bank, free = psB.take()
            m = pe.do(lambda e, bank=bank: e.matmul(bank[:, 0:GW], w_val[:, :], srcT[:, :], start=True, stop=True), m_sT, *free)
            bv = bank[:, 0:GW].rearrange("p (s t) -> p s t", t=T)
            act.do(lambda e, bv=bv: e.activation(v_ext[:, :, MAXSH:MAXSH + T], bv, ACT.Copy, scale=0.5), m, L("O_sb"))
            act.do(lambda e, bv=bv: e.activation(v_ext[:, :, 0:MAXSH], bv[:, :, T - MAXSH:], ACT.Copy, scale=0.5))
            m_v = act.do(lambda e, bv=bv: e.activation(v_ext[:, :, MAXSH + T:], bv[:, :, 0:MAXSH], ACT.Copy, scale=0.5))
            psB.give(bank, m_v)
            m_acc = None
            for k, shift in enumerate((0,) + SHIFTS):
                bank, free = psB.take()
                m = pe.do(lambda e, k=k, bank=bank: e.matmul(bank[:, 0:GW], w_mix[:, k * P:(k + 1) * P], srcT[:, :],
                                                             start=True, stop=True), *free)
                buf, bfree = pt_ring.take()
                sg = buf[:, 0, :] if GS == 1 else None
                m_s = act.do(lambda e, sg=sg, bank=bank: e.activation(sg, bank[:, 0:GW], ACT.Tanh, scale=0.5), m, *bfree)
                psB.give(bank, m_s)
                vv = v_ext[:, :, MAXSH + shift:MAXSH + shift + T]
                sv = sg.rearrange("p (s t) -> p s t", t=T)
                prod = mix_acc[:, :] if k == 0 else buf[:, 1, :]
                m_acc = dve.do(lambda e, vv=vv, sv=sv, prod=prod: e.scalar_tensor_tensor(
                    out=prod.rearrange("p (s t) -> p s t", t=T), in0=sv, scalar=1.0, in1=vv, op0=ALU.add, op1=ALU.mult),
                    m_s, m_v, m_acc, L(("x1T", 0)))
                if k:
                    m_acc = dve.do(lambda e, prod=prod: e.tensor_tensor(mix_acc[:, :], mix_acc[:, :], prod, ALU.add), m_acc)
                pt_ring.give(buf, m_acc)
                yield
            late["srcT"], late["O_sb"] = m_s, m_acc
            bank, free = psB.take()
            for i in range(GT):
                m = pe.do(lambda e, i=i, bank=bank: e.transpose(bank[:, i * P:(i + 1) * P], mix_acc[:, i * P:(i + 1) * P],
                                                                ident[:, :]), m_acc, *free)
            late["x1T", 0] = m
            m = act.do(lambda e, bank=bank: e.activation(ff[:, :, :].rearrange("p i c -> p (i c)"), bank[:, 0:GW], ACT.Copy),
                       m, L("ff"))
            psB.give(bank, m)
            m_rs = layer_norm_stats(ff, GT, lnst, lnmv, lnrs, m, by_newton=True)
            m = normalise(ff, ff, GT, lnmv, lnrs, m_rs)
            m = affine(ff, mix_g, mix_b, m)
            m = dve.do(lambda e: e.tensor_tensor(x[:, :, :], x[:, :, :], ff[:, :, :], ALU.add), m, *m_x)
            late["ff"] = m
            yield
            return m

        xin = d["x"].rearrange("b (i p) c -> p b i c", p=P)
        xout = out.rearrange("b (i p) c -> p b i c", p=P)
        xs, m_xs = {}, {}
        gates, proj, attended = {}, {}, {}

        def load_x(n):
            if n < n_batch:
                xs[n], free = x_ring.take()
                m_xs[n] = (sp.dma(x_in[n % 5], xs[n][:, :, :], xin[:, n], *free),)

        def first_gates(n):
            if n < n_batch and "a" in layers:
                gates[n] = yield from ssm_gates(xs[n], m_xs[n])

        def project(n):
            if n < n_batch and "a" in layers:
                proj[n] = yield from ssm_project(gates[n])

        def attend(n):
            if n < n_batch and "a" in layers:
                m = yield from ssm_attend(xs[n], m_xs[n], gates[n], proj[n])
                m_xs[n] = (m,)
            load_x(n + 2)
            yield from first_gates(n + 1)

        def ffn_first(n, lay):
            if 0 <= n < n_batch and "f" in layers:
                attended[n, lay] = yield from ffn_attend(xs[n], m_xs[n], lay)

        def back_exp(n):
            yield from ffn_first(n - 1, 0)
            if layers.count("f") > 1:
                yield from ffn_first(n - 2, 1)

        def experts(n, lay):
            if (n, lay) in attended:
                m_xs[n] = ((yield from ffn_experts(xs[n], m_xs[n], attended.pop((n, lay)), lay)),)

        def back_silu(n):
            yield from experts(n - 2, 0)
            if 0 <= n - 2 < n_batch and "b" in layers:
                m_xs[n - 2] = ((yield from mix_layer(xs[n - 2], m_xs[n - 2])),)
            yield from experts(n - 3, 1)
            if 0 <= n - 3:
                x = xs.pop(n - 3)
                x_ring.give(x, sp.dma(x_out, xout[:, n - 3], x[:, :, :], *m_xs.pop(n - 3)))

        def emitted():
            return sum(len(q.ops) for q in (pe, act, dve))

        expect = {}

        def weave(name, a, b):
            strands = {name + "0": a, name + "1": b}
            spent = dict.fromkeys(strands, 0)
            while strands:
                k = min(strands, key=lambda k: spent[k] / expect.get(k, 1))
                before_ = emitted()
                try:
                    next(strands[k])
                except StopIteration:
                    del strands[k]
                spent[k] += emitted() - before_
            for k, v in spent.items():
                expect[k] = max(v, expect.get(k, 1))

        def table(name):
            act.run(lambda e: e.preload_act_table_set(name))

        load_x(0)
        load_x(1)
        table("natural_log_exp_and_others")
        for _ in first_gates(0):
            pass
        for n in range(n_batch + 3):
            table("silu_and_others")
            weave("silu", project(n), back_silu(n))
            table("natural_log_exp_and_others")
            weave("exp", attend(n), back_exp(n))
        sp.wait([(x_out[0], x_out[1])])

        block = ctx.enter_context(nc.Block())

        @block.sync
        def _(e):
            for op in sp.ops:
                op(e)

        @block.tensor
        def _(e):
            for op in pe.ops:
                op(e)

        @block.scalar
        def _(e):
            for op in act.ops:
                op(e)

        @block.vector
        def _(e):
            for op in dve.ops:
                op(e)

        @block.gpsimd
        def _(e):
            for op in pool.ops:
                op(e)



def lay_out(i):
    def f(a):
        return np.ascontiguousarray(a)

    a = {k: np.asarray(v) for k, v in i.items()}
    pa, pb, pf = "L0_attn_a_", "L0_attn_b_", "L0_ffn_"
    w, b = a[pa + "in_proj_w"], a[pa + "in_proj_b"]
    n_big = DIM + CONV
    lvl_w = w[n_big + H:].reshape(H, NLV_W, HID).transpose(1, 0, 2)[:NLV + 1].reshape(-1, HID)
    lvl_b = b[n_big + H:].reshape(H, NLV_W).T[:NLV + 1].reshape(-1)
    o = {
        "x": a[pa + "hidden_states"],
        "in_wT": f(w[:n_big].T), "in_b_cols": f(b[:n_big].reshape(-1, P).T),
        "small_wT": f(np.concatenate([w[n_big:n_big + H], lvl_w]).T),
        "small_b": np.concatenate([b[n_big:n_big + H], lvl_b]),
        "dt_bias": a[pa + "dt_bias"], "A_log": a[pa + "A_log"], "D": a[pa + "D"],
        "L_lvl": f(a[pa + "L"].T[:NLV + 1]).reshape(-1),
        "conv_cols": f(a[pa + "conv_w"].reshape(-1, P, KCONV).transpose(1, 0, 2)),
        "norm_cols": f(a[pa + "norm_w"].reshape(-1, P).T),
        "out_wT": f(a[pa + "out_proj_w"].T.reshape(NF, P, HID).transpose(1, 0, 2)), "out_b": a[pa + "out_proj_b"],
        "gate_WT": f(a[pb + "gate_W"].T), "value_WT": f(a[pb + "value_W"].T),
        "gamma": a[pb + "gamma"], "beta": a[pb + "beta"],
        "bq": a[pf + "bq"].reshape(P, 1), "bk": a[pf + "bk"].reshape(P, 1),
        "W1": f(a[pf + "W1"].transpose(1, 0, 2)),
        "b1_cols": f(a[pf + "b1"].reshape(-1, P).T),
        "W2": f(a[pf + "W2"].reshape(-1, P, HID).transpose(1, 0, 2)), "b2": a[pf + "b2"],
    }
    for n in ("Wq", "Wk", "Wv", "Wo", "bv", "bo", "gW", "gb", "ln1_g", "ln1_b", "ln2_g", "ln2_b"):
        o[n] = a[pf + n]
    o.update(shape_constants())
    return o


def kernel(**inputs):
    import concourse.bacc as _bacc
    from concourse.bass_utils import run_bass_kernel_spmd as _run

    nc = _bacc.Bacc("TRN2", target_bir_lowering=False, num_devices=1)
    arrays = lay_out(inputs)
    d = {n: nc.dram_tensor("in_" + n, v.shape, mybir.dt.from_np(v.dtype), kind="ExternalInput").ap()
         for n, v in arrays.items()}
    out = nc.dram_tensor("out_0", (BATCH, T, HID), F32, kind="ExternalOutput").ap()
    build(nc, d, out)
    r = _run(nc, [{"in_" + n: v for n, v in arrays.items()}], core_ids=[0])
    return r.results[0]["out_0"]
```

```python
import numpy as np
import concourse.bass as bass
from concourse import mybir
from concourse.alu_op_type import AluOpType as ALU
from contextlib import ExitStack

F32 = mybir.dt.float32
BF16 = mybir.dt.bfloat16
I32 = mybir.dt.int32
ACT = mybir.ActivationFunctionType
AX = mybir.AxisListType

P = 128
BATCH, T, HID = 16, 256, 128
NT = T // P
H, HD, NS, NLV_W, KCONV = 32, 64, 128, 15, 4
DIM = H * HD
NF = DIM // P
CONV = DIM + 2 * NS
NLV = T.bit_length() - 1
QT = 32
NQ = P // QT
NODES = QT - 1
LOW = QT.bit_length() - 1
HG = 8
NSML = H * (1 + NLV + 1)
OFF_MASK, OFF_NODE = 0, QT
NHI = 3
OFF_HIGH, OFF_TOP = 3 * H, 3 * H + 3 * NHI * NT
R_LOW, R_HIGH = QT + 3 * NODES, OFF_TOP + 3
NH, AD, FF, NE = 16, 8, 256, 8
SLOTROWS = 96
ROW_MAX = 9 * AD
GS = 1
GT = GS * NT
GW = GS * T
SHIFTS = (-32, -16, -4, -1, 1, 4, 16, 32)
NG = len(SHIFTS) + 1
MAXSH = max(SHIFTS)
SLACK = 2
EPS = 1e-5
ROOT_GUESS = 0x5F3759DF
NEG = -1e30
TINY = 1e-30


class Queue:

    expected = {}
    step_end = 0.0

    def __init__(self, sem, cost):
        self.sem, self.count, self.ops, self.seen, self.cost, self.clock = sem, 0, [], {}, cost, 0.0

    def wait(self, marks):
        for m in marks:
            if m is None:
                continue
            sem, value = m
            self.clock = max(self.clock, Queue.expected.get((id(sem), value), 0.0))
            if self.seen.get(id(sem), 0) < value:
                self.seen[id(sem)] = value
                self.ops.append(lambda e, s=sem, v=value: e.wait_ge(s, v))

    def expect(self, mark, latency):
        self.clock += self.cost
        Queue.expected[id(mark[0]), mark[1]] = self.clock + latency
        Queue.step_end = max(Queue.step_end, self.clock + latency)
        return mark

    def run(self, make, *marks):
        self.wait(marks)
        self.clock += self.cost
        self.ops.append(make)

    def do(self, make, *marks):
        self.wait(marks)
        self.count += 1
        self.ops.append(lambda e: make(e).then_inc(self.sem, 1))
        return self.expect((self.sem, self.count), 0.1)

    def dma(self, line, out, in_, *marks):
        self.wait(marks)
        line[1] += 16
        self.ops.append(lambda e, s=line[0]: e.dma_start(out, in_).then_inc(s, 16))
        return self.expect((line[0], line[1]), 2.0)


class Slots:

    def __init__(self, bufs):
        self.free = [(b, ()) for b in bufs]

    def take(self):
        return self.free.pop(0)

    def give(self, buf, *marks):
        self.free.append((buf, marks))


def bc(ap, axis, n):
    dims = [list(d) for d in ap.ap]
    dims.insert(axis, [0, n])
    return bass.AP(tensor=ap.tensor, offset=ap.offset, ap=dims)


def dram(ap, offset, dims):
    return bass.AP(tensor=ap.tensor, offset=ap.offset + offset, ap=dims)


def shape_constants():
    c = {}
    c["ident"] = np.eye(P, dtype=np.float32)
    c["tri"] = np.triu(np.ones((P, P), np.float32))
    low = np.zeros((P, NQ, P), np.float32)
    for q in range(NQ):
        for r in range(QT):
            low[OFF_MASK + r, q, q * QT + r:] = NEG
        for k in range(LOW):
            for j in range(QT >> (k + 1)):
                s0 = q * QT + (j << (k + 1))
                for part in range(3):
                    low[OFF_NODE + part * NODES + node_row(k, j), q, s0:s0 + (1 << k)] = 1.0
    c["low_sel"] = low.reshape(P, NQ * P)
    hi = np.zeros((P, NT + 1, P), np.float32)
    for t in range(NT):
        for part in range(3):
            for node, (s0, s1) in enumerate(((0, QT), (2 * QT, 3 * QT), (0, 2 * QT))):
                hi[high_row(t, node) + part, t, s0:s1] = 1.0
            hi[OFF_TOP + part, NT, :] = 1.0
    c["high_sel"] = hi.reshape(P, (NT + 1) * P)
    ind = np.zeros((P, H), np.float32)
    for r in range(3 * H):
        ind[r, r % H] = 1.0
    c["head_ind"] = ind
    before = np.zeros((P, NE, NE), np.float32)
    for e in range(NE):
        before[:, e, :e] = 1.0
    c["before"] = before.reshape(P, NE * NE)
    return c


def node_row(k, j):
    return sum(QT >> (i + 1) for i in range(k)) + j


def high_row(t, node):
    return OFF_HIGH + 3 * (NHI * t + node)


def build(nc, d, out, n_batch=BATCH, layers="afbf"):
    ctx = ExitStack()
    with ctx:
        def sb(name, shape, dt=F32):
            return ctx.enter_context(nc.sbuf_tensor(name, shape, dt))

        def ring(name, n, shape, dt=F32):
            return Slots([sb(f"{name}{i}", shape, dt) for i in range(n)])

        def line(name):
            return [ctx.enter_context(nc.semaphore(name)), 0]

        pe, act, dve, pool, sp = (Queue(ctx.enter_context(nc.semaphore(n)), cost) for n, cost in (
            ("pe_done", 0.25), ("act_done", 0.42), ("dve_done", 0.38), ("pool_done", 0.3), ("sp_done", 0.6)))

        const_line = line("const_loaded")
        loaded = {}

        def load(name, shape, src, dt=F32):
            t = sb("c_" + name, shape, dt)
            sp.dma(const_line, t[tuple(slice(None) for _ in shape)], src)
            loaded[name] = t
            return t

        def row_bc(ap, n):
            return dram(ap, 0, [[0, P], [1, n]])

        w_in = load("w_in", [P, DIM + CONV], d["in_wT"])
        w_small = load("w_small", [P, NSML], d["small_wT"])
        b_small = load("b_small", [P, NSML], row_bc(d["small_b"], NSML))
        dt_bias = load("dt_bias", [P, H], row_bc(d["dt_bias"], H))
        lvl_scale = load("lvl_scale", [P, (NLV + 1) * H], row_bc(d["L_lvl"], (NLV + 1) * H))
        neg_a = load("neg_a", [P, H], row_bc(d["A_log"], H))
        d_skip = load("d_skip", [P, H], row_bc(d["D"], H))
        b_in = load("b_in", [P, 2 * NF + 2], d["in_b_cols"])
        conv_w = load("conv_w", [P, NF + 2, KCONV], d["conv_cols"])
        w_out = load("w_out", [P, NF, HID], d["out_wT"])
        norm_w = load("norm_w", [P, NF], d["norm_cols"])
        b_out = load("b_out", [P, HID], row_bc(d["out_b"], HID))
        ident = load("ident", [P, P], d["ident"])
        tri = load("tri", [P, P], d["tri"])
        before = load("before", [P, NE * NE], d["before"])
        head_ind = load("head_ind", [P, H], d["head_ind"])
        w_q, w_k, w_v, w_o = (load(n, [P, P], d[n]) for n in ("Wq", "Wk", "Wv", "Wo"))
        b_q, b_k = (load(n, [P, 1], d[n]) for n in ("bq", "bk"))
        b_v, b_o, ln1_g, ln1_b, ln2_g, ln2_b, mix_g, mix_b = (
            load(n, [P, HID], row_bc(d[n], HID))
            for n in ("bv", "bo", "ln1_g", "ln1_b", "ln2_g", "ln2_b", "gamma", "beta"))
        w_gate = load("w_gate", [P, NE], d["gW"])
        b_gate = load("b_gate", [P, NE], row_bc(d["gb"], NE))
        w_1 = load("w_1", [P, NE, FF], d["W1"])
        b_1 = load("b_1", [P, NE * FF // P], d["b1_cols"])
        w_2 = load("w_2", [P, NE * FF // P, HID], d["W2"])
        b_2 = load("b_2", [NE, HID], d["b2"])
        w_mix = load("w_mix", [P, NG * HID], d["gate_WT"])
        w_val = load("w_val", [P, HID], d["value_WT"])
        consts = (const_line[0], const_line[1])

        x_ring = ring("x_", 4, [P, GT, HID])
        xn_a = sb("xn_a", [P, NT, HID])
        xnT_a = sb("xnT_a", [P, T])
        SPL = sb("SPL", [P, NT, NSML])
        Z = sb("Z", [P, NF, T])
        at = 3 * NT * NSML + 3 * NT * H
        work = sb("work", [P, at + NT * 3 * NLV * H // 2])
        U, W1t, W2t = (work[:, k * NT * NSML:(k + 1) * NT * NSML].rearrange("p (i c) -> p i c", i=NT) for k in range(3))
        CL = W1t[:, :, 0:NLV * H].rearrange("p i (l h) -> p i l h", h=H)
        at = 3 * NT * NSML
        g_t, gr, ln_dt = (work[:, at + k * NT * H:at + (k + 1) * NT * H].rearrange("p (i h) -> p i h", i=NT)
                          for k in range(3))
        at += 3 * NT * H
        c_parts = work[:, at:at + NT * 3 * NLV * H // 2].bitcast(BF16).rearrange("p (i a c) -> p i a c", i=NT, a=3)
        pads = [work[:, k * 3 * P:k * 3 * P + KCONV - 1 + T] for k in range(2)]
        xs_bufs = [work[:, (3 + 2 * k) * T:(5 + 2 * k) * T].rearrange("p (k t) -> p k t", k=2) for k in range(3)]
        bmT, cmT = work[:, 9 * T:10 * T], work[:, 10 * T:11 * T]
        pad_ring, xs_ring = Slots(pads), Slots(xs_bufs)
        gc = sb("gc", [P, NT, H])
        s_parts = sb("s_parts", [P, NT, 3, H], BF16)
        ccoef = sb("ccoef", [P, NT, H])
        qk_diag = sb("qk_diag", [P, NT])
        QK = sb("QK", [P, 3, P])
        X = sb("X", [P, NT, DIM])
        own_ring = ring("own", 2, [P, HG * HD])
        low_buf = sb("low", [P, T, H], BF16)
        high_buf = sb("high", [P, P, H], BF16)
        low_sel = sb("low_sel", [P, NQ, P], BF16)
        high_sel = [sb(f"high_sel{i}", [P, P], BF16) for i in range(3)]
        att_ring = ring("att", 4, [P, HG, P])
        rms = sb("rms", [P, NT])
        ident_bf = sb("ident_bf", [P, P], BF16)
        ones_f = sb("ones_f", [P, P])
        share = sb("share", [P, 1])
        eps_col = sb("eps_col", [P, 1])
        ln_a = (sb("lnst_a", [P, NT, 6]), sb("lnmv_a", [P, NT, 2]), sb("lnrs_a", [P, NT]), None, None)
        osb, qk_scr = xn_a, xn_a[:, 0, :]

        src_b = [sb(f"src{i}", [P, GT, HID]) for i in range(2)]
        srcT_b = [sb(f"srcT{i}", [P, GW]) for i in range(2)]
        qparts = sb("qparts", [P, 3, GW], BF16)
        q_stack = sb("q_stack", [SLOTROWS, NH, GW], BF16)
        k_stack = sb("k_stack", [SLOTROWS, NH, GW], BF16)
        V9 = sb("V9", [P, GT, NH, 32])
        nmax = sb("nmax", [P, GT, NH])
        nmax_bf = sb("nmax_bf", [P, GT, NH], BF16)
        maxT = sb("maxT", [NH, GW], BF16)
        pt_ring = ring("pt", 5, [P, 2, T])
        O_sb = sb("O_sb", [P, 4, T])
        rden = sb("rden", [P, NH])
        x1_b = [sb(f"x1_{i}", [P, GT, HID]) for i in range(2)]
        x1T_b = [sb(f"x1T_{i}", [P, GW]) for i in range(2)]
        gate_l = sb("gate_l", [P, GT, NE])
        gate_s = sb("gate_s", [P, GT])
        w_e_b = [sb(f"w_e{i}", [P, GT, NE]) for i in range(2)]
        h_ring = pt_ring
        ff_b = [sb(f"ff{i}", [P, GT, HID]) for i in range(2)]
        gate_gq = [[ff_[:, :, :].rearrange("p i c -> p (i c)")[:, k * GT * NE * NE:(k + 1) * GT * NE * NE].rearrange(
            "p (i a b) -> p i a b", i=GT, a=NE) for k in range(2)] for ff_ in ff_b]
        v_ext = O_sb[:, :, :].rearrange("p g t -> p (g t)")[:, 0:GS * (T + 2 * MAXSH)].rearrange("p (s t) -> p s t", s=GS)
        mix_acc = x1T_b[0]
        ln_b = [(sb(f"lnst{i}", [P, GT, 6]), sb(f"lnmv{i}", [P, GT, 2]), sb(f"lnrs{i}", [P, GT]),
                 sb(f"root_v{i}", [P, GT]), sb(f"root_t{i}", [P, GT])) for i in range(3)]

        psA = Slots([ctx.enter_context(nc.psum_tensor(f"psA{i}", [P, 512], F32)) for i in range(4)])
        psB = Slots([ctx.enter_context(nc.psum_tensor(f"psB{i}", [P, 512], F32)) for i in range(4)])

        lvl_scr = nc.dram_tensor("lvl_scr", [3, NLV, T, H], BF16)[:, :, :, :]
        qk_scrd = [nc.dram_tensor(f"qk_scr{i}", [NH, ROW_MAX, GW], BF16)[:, :, :] for i in range(2)]
        lvl_out, lvl_in = line("lvl_stored"), line("lvl_loaded")
        qk_out = [line("q_stored"), line("k_stored")]
        qk_in = [line("q_stacked"), line("k_stacked")]
        max_in = line("max_stacked")
        x_in = [line(f"x_loaded{i}") for i in range(4)]
        x_out = line("x_stored")

        done = {}
        done["ones"] = dve.do(lambda e: e.memset(ones_f[:, :], 1.0))
        done["eps"] = dve.do(lambda e: e.memset(eps_col[:, :], EPS))
        done["share"] = dve.do(lambda e: e.memset(share[:, :], 1.0 / 32))
        done["identb"] = dve.do(lambda e: e.tensor_copy(ident_bf[:, :], ident[:, :]), consts)
        fold = [dve.do(lambda e: e.tensor_tensor(b_small[:, 0:H], b_small[:, 0:H], dt_bias[:, :], ALU.add), consts),
                act.do(lambda e: e.activation(neg_a[:, :], neg_a[:, :], ACT.Exp), consts)]
        fold.append(dve.do(lambda e: e.tensor_scalar(neg_a[:, :], neg_a[:, :], -1.0, None, ALU.mult), fold[1]))
        for f in range(NF):
            m = dve.do(lambda e, f=f: e.tensor_scalar(w_out[:, f, :], w_out[:, f, :], norm_w[:, f:f + 1], None, ALU.mult))
            fold.append(m)
        done["fold"] = fold[-1]
        setup_line = line("setup_loaded")
        zf = Z[:, :, :].rearrange("p f t -> p (f t)")
        l = sp.dma(setup_line, zf[:, 0:NQ * P], d["low_sel"])
        l = sp.dma(setup_line, zf[:, NQ * P:(NQ + NT + 1) * P], d["high_sel"])
        dve.do(lambda e: e.tensor_copy(low_sel[:, :, :].rearrange("p q s -> p (q s)"), zf[:, 0:NQ * P]), l)
        for i in range(3):
            o = (NQ + i) * P
            done["z_free"] = dve.do(lambda e, i=i, o=o: e.tensor_copy(high_sel[i][:, :], zf[:, o:o + P]))
        done["sel"] = done["z_free"]
        z0 = pool.do(lambda e: e.memset(high_buf[:, :, :], 0.0))
        done["high0"] = pool.do(lambda e: e.tensor_copy(high_buf[0:3 * H, :, :], bc(head_ind[0:3 * H, :], 1, P)), z0, consts)
        z0 = dve.do(lambda e: e.memset(low_buf[:, :, :], 0.0))
        for q in range(T // QT):
            done["low0"] = pool.do(lambda e, q=q: e.tensor_copy(
                low_buf[0:QT, q * QT:(q + 1) * QT, :], bc(ident[0:QT, 0:QT], 2, H)), z0, done["high0"])
        for st in (q_stack, k_stack):
            z0 = pool.do(lambda e, st=st: e.memset(st[:, :, :], 0.0), done["low0"])
        done["stack0"] = pool.do(lambda e: e.memset(k_stack[64:SLOTROWS, :, :], 1.0), z0)
        z0 = pool.do(lambda e: e.memset(V9[:, :, :, :], 0.0), done["stack0"])
        done["v9"] = pool.do(lambda e: e.memset(V9[:, :, :, AD:AD + 1], 1.0), z0)

        def layer_norm_stats(x, n, bufs, *marks, by_newton=False):
            st, mv, rs, half, t = bufs
            for i in range(n):
                m = dve.do(lambda e, i=i: e.bn_stats(st[:, i, :], x[:, i, :]), *marks)
            for i in range(n):
                m = dve.do(lambda e, i=i: e.bn_aggr(mv[:, i, :], st[:, i, :]), m)
            if not by_newton:
                m = act.do(lambda e: e.activation(rs[:, 0:n], mv[:, 0:n, 1], ACT.Ln, bias=eps_col[:, :]), m, done["eps"],
                           rs_free.get(id(rs)))
                return act.do(lambda e: e.activation(rs[:, 0:n], rs[:, 0:n], ACT.Exp, scale=-0.5), m)
            m = dve.do(lambda e: e.tensor_scalar(half[:, :], mv[:, 0:n, 1], EPS, None, ALU.add), m, rs_free.get((id(rs), "v")))
            m1 = dve.do(lambda e: e.tensor_scalar(t[:, :].bitcast(I32), half[:, :].bitcast(I32), 1, None, ALU.logical_shift_right), m)
            m1 = dve.do(lambda e: e.tensor_scalar(rs[:, :].bitcast(I32), t[:, :].bitcast(I32), -1.0, float(ROOT_GUESS),
                                                  ALU.mult, ALU.add), m1)
            m = pool.do(lambda e: e.tensor_scalar(half[:, :], half[:, :], -0.5, None, ALU.mult), m1)
            for _ in range(3):
                m = pool.do(lambda e: e.tensor_tensor(t[:, :], rs[:, :], rs[:, :], ALU.mult), m, m1)
                m = pool.do(lambda e: e.tensor_tensor(t[:, :], t[:, :], half[:, :], ALU.mult), m)
                m = pool.do(lambda e: e.tensor_scalar(t[:, :], t[:, :], 1.5, None, ALU.add), m)
                m = pool.do(lambda e: e.tensor_tensor(rs[:, :], rs[:, :], t[:, :], ALU.mult), m)
            rs_free[id(rs), "v"] = m
            return m

        rs_free = {}

        def normalise(out_, x, n, bufs, m_rs, *marks):
            _, mv, rs, _, _ = bufs
            for i in range(n):
                m = dve.do(lambda e, i=i: e.tensor_scalar(out_[:, i, :], x[:, i, :], mv[:, i, 0:1], rs[:, i:i + 1],
                                                          ALU.subtract, ALU.mult), m_rs, *marks)
            rs_free[id(rs)] = m
            return m

        def transpose_tiles(out_, x, n, ps, m_x, *marks):
            bank, free = ps.take()
            for i in range(n):
                m = pe.do(lambda e, i=i: e.transpose(bank[:, i * P:(i + 1) * P], x[:, i, :], ident[:, :]),
                          m_x, consts, *free)
            m = act.do(lambda e: e.activation(out_[:, 0:n * P], bank[:, 0:n * P], ACT.Copy), m, *marks)
            ps.give(bank, m)
            return m

        last = {}

        def ssm_gates(x, m_x):
            L = last.get
            m_rs = layer_norm_stats(x, NT, ln_a, *m_x)
            yield
            m = normalise(xn_a, x, NT, ln_a, m_rs, L("xn_a"))
            m_xnT = transpose_tiles(xnT_a, xn_a, NT, psA, m, L("xnT_a"))
            last["xn_a"] = m_xnT
            yield
            for i in range(NT):
                bank, free = psA.take()
                m = pe.do(lambda e, i=i, bank=bank: e.matmul(bank[:, 0:NSML], xnT_a[:, i * P:(i + 1) * P], w_small[:, :],
                                                             start=True, stop=True), m_xnT, *free)
                m = dve.do(lambda e, i=i, bank=bank: e.tensor_tensor(U[:, i, :], bank[:, 0:NSML], b_small[:, :], ALU.add),
                           m, fold[0], *last.get("work", ()))
                psA.give(bank, m)
            m = dve.do(lambda e: e.tensor_tensor(U[:, :, H:], U[:, :, H:], bc(lvl_scale[:, :], 1, NT), ALU.mult), m, consts)
            yield
            m = act.do(lambda e: e.activation(W1t[:, :, :], U[:, :, :], ACT.Abs), m)
            m_e = act.do(lambda e: e.activation(W1t[:, :, :], W1t[:, :, :], ACT.Exp, scale=-1.0), m)
            m_w = dve.do(lambda e: e.tensor_scalar(W2t[:, :, :], W1t[:, :, :], 1.0, None, ALU.add), m_e)
            yield
            m_ln = act.do(lambda e: e.activation(SPL[:, :, :], W2t[:, :, :], ACT.Ln), m_w, L("SPL"))
            m_d = dve.do(lambda e: e.tensor_scalar(W2t[:, :, :], W2t[:, :, :], -1.0, TINY, ALU.add, ALU.max), m_ln)
            m_d = dve.do(lambda e: e.reciprocal(W2t[:, :, :], W2t[:, :, :]), m_d)
            m = dve.do(lambda e: e.scalar_tensor_tensor(out=W1t[:, :, :], in0=SPL[:, :, :], scalar=TINY, in1=W1t[:, :, :],
                                                        op0=ALU.max, op1=ALU.mult), m_ln)
            m = dve.do(lambda e: e.tensor_tensor(W1t[:, :, :], W1t[:, :, :], W2t[:, :, :], ALU.mult), m, m_d)
            m_sp = dve.do(lambda e: e.scalar_tensor_tensor(out=SPL[:, :, :], in0=U[:, :, :], scalar=0.0, in1=W1t[:, :, :],
                                                           op0=ALU.max, op1=ALU.add), m)
            dt = SPL[:, :, 0:H]
            m_g = dve.do(lambda e: e.tensor_tensor(g_t[:, :, :], dt, bc(neg_a[:, :], 1, NT), ALU.mult), m_sp, fold[2])
            yield
            bank, free = psA.take()
            for i in range(NT):
                for j in range(i + 1):
                    m = pe.do(lambda e, i=i, j=j, bank=bank: e.matmul(
                        bank[:, i * H:(i + 1) * H], (tri if i == j else ones_f)[:, :], g_t[:, j, :],
                        start=(j == 0), stop=(j == i)), m_g, done["ones"], *free)
            m_gc = dve.do(lambda e, bank=bank: e.tensor_copy(gc[:, :, :].rearrange("p i h -> p (i h)"), bank[:, 0:NT * H]),
                          m, L("gc"))
            psA.give(bank, m_gc)
            m = dve.do(lambda e: e.tensor_scalar(CL[:, :, :, :].rearrange("p i l h -> p i (l h)"), SPL[:, :, 2 * H:],
                                                 1e-37, None, ALU.max), m_sp)
            m = act.do(lambda e: e.activation(CL[:, :, :, :], CL[:, :, :, :], ACT.Ln), m)
            m_ld = dve.do(lambda e: e.tensor_scalar(ln_dt[:, :, :], dt, 1e-37, None, ALU.max), m_sp, L("gc"))
            m_ld = act.do(lambda e: e.activation(ln_dt[:, :, :], ln_dt[:, :, :], ACT.Ln), m_ld)
            for i in range(NT):
                m_c = dve.do(lambda e, i=i: e.tensor_tensor(CL[:, i, :, :], CL[:, i, :, :], bc(gc[:, i, :], 1, NLV), ALU.add),
                             m, m_gc)
            yield
            cl = CL[:, :, :, :].rearrange("p i l h -> p i (l h)")
            cr = W2t[:, :, 0:NLV * H]
            m = dve.do(lambda e: e.tensor_copy(c_parts[:, :, 0, :], cl), m_c)
            m2 = dve.do(lambda e: e.tensor_tensor(gc[:, :, :], ln_dt[:, :, :], gc[:, :, :], ALU.subtract), m_c, m_ld)
            m = dve.do(lambda e: e.tensor_tensor(cr, cl, c_parts[:, :, 0, :], ALU.subtract), m)
            m2 = dve.do(lambda e: e.tensor_copy(s_parts[:, :, 0, :], gc[:, :, :]), m2, L("s_parts"))
            m = dve.do(lambda e: e.tensor_copy(c_parts[:, :, 1, :], cr), m)
            m2 = dve.do(lambda e: e.tensor_tensor(gr[:, :, :], gc[:, :, :], s_parts[:, :, 0, :], ALU.subtract), m2)
            m_cp = dve.do(lambda e: e.tensor_tensor(c_parts[:, :, 2, :], cr, c_parts[:, :, 1, :], ALU.subtract), m)
            m2 = dve.do(lambda e: e.tensor_copy(s_parts[:, :, 1, :], gr[:, :, :]), m2)
            m_s = dve.do(lambda e: e.tensor_tensor(s_parts[:, :, 2, :], gr[:, :, :], s_parts[:, :, 1, :], ALU.subtract), m2)
            last["gc"] = m_s
            for i in range(NT):
                m_st = sp.dma(lvl_out, dram(lvl_scr, i * P * H, [[H, P], [T * H, 3 * NLV], [1, H]]),
                              c_parts[:, i, :, :].rearrange("p a (l h) -> p (a l) h", h=H), m_cp, L("scr"))
            last["gate_work"] = (m_s, m_st)
            yield
            return m_xnT, m_sp, m_s, m_st

        def ssm_place(gates):
            m_xnT, m_sp, m_s, m_st = gates
            L = last.get
            bank, free = psA.take()
            bview = bank[:, :].bitcast(BF16)
            for i in range(NT):
                m = pe.do(lambda e, i=i, bview=bview: e.transpose(
                    bview[0:3 * H, i * P:(i + 1) * P], s_parts[:, i, :, :].rearrange("p a h -> p (a h)"), ident_bf[:, :]),
                    m_s, done["identb"], *free)
            last["s_parts"] = m
            for i, src in enumerate((0, 1, 0)):
                m_hs = dve.do(lambda e, i=i, src=src, bview=bview: e.tensor_copy(
                    high_sel[i][0:3 * H, :], bview[0:3 * H, src * P:(src + 1) * P]), m, L("high_sel"), done["sel"])
            psA.give(bank, m_hs)
            plane = NLV * T * H
            w = (m_st, L("low"), L("high"), done["low0"], done["high0"])
            loads = []
            for k in range(LOW):
                for j in range(QT >> (k + 1)):
                    r, t0, n_t = OFF_NODE + node_row(k, j), (j << (k + 1)) + (1 << k), 1 << k
                    loads.append((low_buf[r:r + 2 * NODES + 1:NODES, :, :].rearrange(
                        "a (q i) h -> a q (i h)", q=NT * NQ)[:, :, t0 * H:(t0 + n_t) * H],
                        dram(lvl_scr, (k * T + t0) * H, [[plane, 3], [QT * H, NT * NQ], [1, n_t * H]])))
            for node, (k, t0, n_t) in enumerate(((LOW, QT, QT), (LOW, 3 * QT, QT), (LOW + 1, 2 * QT, 2 * QT))):
                for t in range(NT):
                    r = high_row(t, node)
                    loads.append((high_buf[r:r + 3, t0:t0 + n_t, :].rearrange("a t h -> a (t h)"),
                                  dram(lvl_scr, (k * T + t * P + t0) * H, [[plane, 3], [1, n_t * H]])))
            loads.append((high_buf[OFF_TOP:OFF_TOP + 3, :, :].rearrange("a t h -> a (t h)"),
                          dram(lvl_scr, ((NLV - 1) * T + P) * H, [[plane, 3], [1, P * H]])))

            def load_some(n):
                for dst, src in loads[:n]:
                    last["scr"] = sp.dma(lvl_in, dst, src, *w)
                del loads[:n]
                return last["scr"]
            return m_hs, load_some

        def ssm_project(gates):
            m_xnT, m_sp, _, _ = gates
            L = last.get
            m_hs, load_some = ssm_place(gates)
            work_free = last["gate_work"]
            for pad in pads:
                m_pad = dve.do(lambda e, pad=pad: e.memset(pad[:, 0:KCONV - 1], 0.0), *work_free)

            def conv_front(c, cv, *cfree):
                bank, free = psA.take()
                m = pe.do(lambda e: e.matmul(bank[:, 0:T], w_in[:, DIM + c * P:DIM + (c + 1) * P], xnT_a[:, :],
                                             start=True, stop=True), m_xnT, consts, *free)
                pad, pfree = pad_ring.take()
                m = act.do(lambda e: e.activation(pad[:, KCONV - 1:], bank[:, 0:T], ACT.Identity,
                                                  bias=b_in[:, NF + c:NF + c + 1]), m, m_pad, *work_free, *pfree)
                psA.give(bank, m)
                m = dve.do(lambda e: e.tensor_scalar(cv, pad[:, 0:T], conv_w[:, c, 0:1], None, ALU.mult), m, *cfree, *work_free)
                for k in range(1, KCONV):
                    m = dve.do(lambda e, k=k: e.scalar_tensor_tensor(out=cv, in0=pad[:, k:k + T],
                                                                     scalar=conv_w[:, c, k:k + 1], in1=cv,
                                                                     op0=ALU.mult, op1=ALU.add), m)
                pad_ring.give(pad, m)
                return m

            def conv_silu(cv, m):
                return act.do(lambda e: e.activation(cv, cv, ACT.Silu), m)

            fb, fc = conv_front(NF, bmT, L("bmT")), conv_front(NF + 1, cmT, L("bmT"))
            fronts, shown = {}, {}
            n2 = NF // 2
            for step in range(n2 + 2):
                if step < n2:
                    xb, xfree = xs_ring.take()
                    for k in range(2):
                        m_fr = conv_front(2 * step + k, xb[:, k, :], *xfree)
                    fronts[step] = (xb, m_fr)
                if step == 0:
                    m_b = conv_silu(bmT, fb)
                    m_cc = conv_silu(cmT, fc)
                if 1 <= step <= n2:
                    f2 = step - 1
                    xb, m_f = fronts.pop(f2)
                    for k in range(2):
                        m = conv_silu(xb[:, k, :], m_f)
                    shown[f2] = (xb, m)
                if step < n2:
                    for f in (2 * step, 2 * step + 1):
                        bank, free = psA.take()
                        m = pe.do(lambda e, f=f, bank=bank: e.matmul(bank[:, 0:T], w_in[:, f * P:(f + 1) * P], xnT_a[:, :],
                                                                     start=True, stop=True), *free)
                        last["xnT_a"] = m
                        m_z = act.do(lambda e, f=f, bank=bank: e.activation(Z[:, f, :], bank[:, 0:T], ACT.Silu,
                                                                            bias=b_in[:, f:f + 1]), m, L("Z"), done["z_free"])
                        psA.give(bank, m_z)
                load_some(5)
                if step == 1:
                    bank, free = psA.take()
                    for k, (s_, t_) in enumerate(((0, 0), (1, 1), (0, 1))):
                        m = pe.do(lambda e, k=k, s_=s_, t_=t_, bank=bank: e.matmul(
                            bank[:, k * P:(k + 1) * P], bmT[:, s_ * P:(s_ + 1) * P], cmT[:, t_ * P:(t_ + 1) * P],
                            start=True, stop=True), m_b, m_cc, *free)
                    last["bmT"] = m
                    m_qk = dve.do(lambda e, bank=bank: e.tensor_copy(QK[:, :, :].rearrange("p k t -> p (k t)"),
                                                                     bank[:, 0:3 * P]), m, L("QK"))
                    psA.give(bank, m_qk)
                    m = m_qk
                    for i in range(NT):
                        m = dve.do(lambda e, i=i: e.tensor_tensor(qk_scr, QK[:, i, :], ident[:, :], ALU.mult), m, last["xn_a"])
                        m = dve.do(lambda e, i=i: e.tensor_reduce(qk_diag[:, i:i + 1], qk_scr, AX.X, ALU.add), m)
                    for i in range(NT):
                        m1 = dve.do(lambda e, i=i: e.scalar_tensor_tensor(
                            out=ccoef[:, i, :], in0=SPL[:, i, H:2 * H], scalar=qk_diag[:, i:i + 1], in1=SPL[:, i, 0:H],
                            op0=ALU.mult, op1=ALU.mult), m, L("ccoef"))
                    last["xn_a"] = m
                    m_cf = dve.do(lambda e: e.tensor_tensor(ccoef[:, :, :], ccoef[:, :, :], bc(d_skip[:, :], 1, NT), ALU.add), m1)
                if step >= 2:
                    f2 = step - 2
                    xb, m_s2 = shown.pop(f2)
                    bank, free = psA.take()
                    for i in range(NT):
                        for k in range(2):
                            m = pe.do(lambda e, i=i, k=k, bank=bank, xb=xb: e.transpose(
                                bank[:, i * 2 * P + k * P:i * 2 * P + (k + 1) * P], xb[:, k, i * P:(i + 1) * P],
                                ident[:, :]), m_s2, *free)
                    xs_ring.give(xb, m)
                    m_tr = m
                    m_x = act.do(lambda e, bank=bank, f2=f2: e.activation(
                        X[:, :, f2 * 2 * P:(f2 + 1) * 2 * P], bank[:, :].rearrange("p (i c) -> p i c", i=NT), ACT.Copy),
                        m, L("X"))
                    psA.give(bank, m_x)
                yield
            last["SPL"] = m_cf
            last["work"] = (m_fr, m_tr, m_x)
            return m_z, m_x, m_qk, m_cf, m_hs, load_some(NSML)

        def ssm_attend(x, m_xin, proj):
            m_z, m_x_all, m_qk, m_cf, m_hs, m_ld = proj
            L = last.get
            ready = {}

            def weights(t, hg):
                h0, tiles = hg * HG, []
                for s_ in ([t] if t == 0 else [0, t]):
                    diag = s_ == t
                    att, afree = att_ring.take()
                    sel = high_sel[t if diag else 2]
                    for half in range(2):
                        bank, free = psA.take()
                        bv = bank[:, :].rearrange("p (t h) -> p t h", h=HG)
                        c = half * 64
                        m = pe.do(lambda e, bv=bv, c=c, sel=sel, diag=diag, h0=h0: e.matmul(
                            bv, sel[0:R_HIGH, :], high_buf[0:R_HIGH, c:c + 64, h0:h0 + HG],
                            start=True, stop=not diag, skip_group_check=True), m_ld, m_hs, *free)
                        if diag:
                            for q in (2 * half, 2 * half + 1):
                                m = pe.do(lambda e, bv=bv, c=c, q=q, h0=h0, t=t: e.matmul(
                                    bv[:, q * QT - c:(q + 1) * QT - c, :], low_sel[0:R_LOW, q, :],
                                    low_buf[0:R_LOW, t * P + q * QT:t * P + (q + 1) * QT, h0:h0 + HG],
                                    start=False, stop=(q % 2 == 1), skip_group_check=True))
                            last["low"] = m
                        m_e = act.do(lambda e, bv=bv, c=c, att=att: e.activation(
                            att[:, :, c:c + 64].rearrange("p h t -> p t h"), bv, ACT.Exp), m, *afree)
                        psA.give(bank, m_e)
                    last["high"] = last["high_sel"] = m
                    kq = t if diag else 2
                    m_a = dve.do(lambda e, att=att, kq=kq: e.tensor_tensor(
                        att[:, :, :], att[:, :, :], bc(QK[:, kq, :], 1, HG), ALU.mult), m_e, m_qk)
                    tiles.append((att, s_))
                last["QK"] = m_a
                own, ofree = own_ring.take()
                m_own = pool.do(lambda e, own=own, t=t, h0=h0: e.tensor_tensor(
                    own[:, :].rearrange("p (h c) -> p h c", c=HD),
                    X[:, t, h0 * HD:(h0 + HG) * HD].rearrange("p (h c) -> p h c", c=HD),
                    bc(ccoef[:, t, h0:h0 + HG], 2, HD), ALU.mult), m_x_all, m_cf, *ofree)
                last["ccoef"] = m_own
                ready[t, hg] = (tiles, own, m_a, m_own)

            def sums(t, hg):
                tiles, own, m_a, m_own = ready.pop((t, hg))
                bank, free = psA.take()
                for f in range(HG // 2):
                    fc = (hg * HG // 2 + f) * P
                    pe.run(lambda e, bank=bank, f=f, own=own: e.matmul(
                        bank[:, f * P:(f + 1) * P], own[:, f * P:(f + 1) * P], ident[:, :], start=True, stop=False,
                        skip_group_check=True), m_own, *free)
                    for att, s_ in tiles:
                        for k in range(2):
                            mm = (lambda e, f=f, k=k, att=att, s_=s_, bank=bank, fc=fc: e.matmul(
                                bank[k * HD:(k + 1) * HD, f * P:(f + 1) * P], X[:, s_, fc + k * HD:fc + (k + 1) * HD],
                                att[:, 2 * f + k, :], start=False, stop=(s_ == t), skip_group_check=True))
                            m = pe.do(mm, m_a, m_x_all)
                for att, _ in tiles:
                    att_ring.give(att, m)
                own_ring.give(own, m)
                last["X"] = m
                f0 = hg * HG // 2
                m = dve.do(lambda e, bank=bank, f0=f0: e.tensor_tensor(
                    Z[:, f0:f0 + HG // 2, t * P:(t + 1) * P], bank[:, :].rearrange("p (f t) -> p f t", t=P),
                    Z[:, f0:f0 + HG // 2, t * P:(t + 1) * P], ALU.mult), m, m_z)
                psA.give(bank, m)
                return m

            units = [(t, hg) for t in range(NT) for hg in range(H // HG)]
            for k, unit in enumerate(units + [None]):
                if unit:
                    weights(*unit)
                if k:
                    m_yz = sums(*units[k - 1])
                yield

            bank, free = psA.take()
            for g4 in range(NF // 4):
                sqa, sfree = att_ring.take()
                sq = sqa[:, :, :].rearrange("p (a b) t -> p a (b t)", b=NT)
                m = act.do(lambda e, g4=g4, sq=sq: e.activation(sq, Z[:, 4 * g4:4 * g4 + 4, :], ACT.Square), m_yz, *sfree)
                for j in range(4):
                    m = pe.do(lambda e, j=j, sq=sq, g4=g4, bank=bank: e.matmul(
                        bank[32 * j:32 * j + 32, 0:T], ones_f[:, 0:32], sq[:, j, :], start=(g4 == 0),
                        stop=(g4 == NF // 4 - 1), skip_group_check=True), m, *free)
                att_ring.give(sqa, m)
            sbuf, sfree = att_ring.take()
            ssq = sbuf[:, 0:2, :].rearrange("p a t -> p (a t)")
            m = act.do(lambda e, bank=bank: e.activation(ssq, bank[:, 0:T], ACT.Copy), m, *sfree)
            yield
            obank, ofree = psA.take()
            for i in range(NT):
                for f in range(NF):
                    m_op = pe.do(lambda e, i=i, f=f: e.matmul(
                        obank[:, i * P:(i + 1) * P], Z[:, f, i * P:(i + 1) * P], w_out[:, f, :],
                        start=(f == 0), stop=(f == NF - 1)), m_yz, done["fold"], *ofree)
            last["Z"] = m_op
            for i in range(NT):
                m_ss = pe.do(lambda e, i=i: e.matmul(bank[:, T + i:T + i + 1], ssq[:, i * P:(i + 1) * P],
                                                     share[:, :], start=True, stop=True, skip_group_check=True),
                             m, done["share"])
            att_ring.give(sbuf, m_ss)
            m = act.do(lambda e: e.activation(rms[:, :], bank[:, T:T + NT], ACT.Ln, scale=1.0 / DIM, bias=eps_col[:, :]),
                       m_ss, L("rms"), done["eps"])
            psA.give(bank, m)
            m_rms = act.do(lambda e: e.activation(rms[:, :], rms[:, :], ACT.Exp, scale=-0.5), m)
            yield
            for i in range(NT):
                m2 = dve.do(lambda e, i=i: e.scalar_tensor_tensor(
                    out=osb[:, i, :], in0=obank[:, i * P:(i + 1) * P], scalar=rms[:, i:i + 1], in1=b_out[:, :],
                    op0=ALU.mult, op1=ALU.add), m_op, m_rms, L("xn_a"))
            psA.give(obank, m2)
            last["rms"] = m2
            m2 = dve.do(lambda e: e.tensor_tensor(x[:, :, :], x[:, :, :], osb[:, :, :], ALU.add), m2, *m_xin)
            last["xn_a"] = m2
            yield
            return m2

        late = {}

        def affine(y, g, b, m):
            m = dve.do(lambda e: e.tensor_tensor(y[:, :, :], y[:, :, :], bc(g[:, :], 1, GT), ALU.mult), m)
            return dve.do(lambda e: e.tensor_tensor(y[:, :, :], y[:, :, :], bc(b[:, :], 1, GT), ALU.add), m)

        def ffn_front(x, m_x, lay, by_newton):
            L = late.get
            src_t, srcT = src_b[lay], srcT_b[lay]
            m_rs = layer_norm_stats(x, GT, ln_b[lay], *m_x, by_newton=by_newton)
            yield
            m_src = normalise(src_t, x, GT, ln_b[lay], m_rs, L(("src_t", lay)))
            m_sT = transpose_tiles(srcT, src_t, GT, psB, m_src, L(("srcT", lay)))
            yield
            m_st = []
            for side, (w, b, st) in enumerate(((w_q, b_q, q_stack), (w_k, b_k, k_stack))):
                bank, free = psB.take()
                m = pe.do(lambda e, w=w, bank=bank: e.matmul(bank[:, 0:GW], w[:, :], srcT[:, :], start=True, stop=True),
                          m_sT, *free)
                buf, bfree = pt_ring.take()
                qf, qr = buf[:, 0, :], buf[:, 1, :]
                m = act.do(lambda e, b=b, bank=bank, qf=qf: e.activation(qf, bank[:, 0:GW], ACT.Identity, bias=b[:, 0:1]),
                           m, *bfree)
                psB.give(bank, m)
                m = dve.do(lambda e, qf=qf: e.tensor_copy(qparts[:, 0, :], qf), m, L("qparts"))
                m = dve.do(lambda e, qf=qf, qr=qr: e.tensor_tensor(qr, qf, qparts[:, 0, :], ALU.subtract), m)
                m = dve.do(lambda e, qr=qr: e.tensor_copy(qparts[:, 1, :], qr), m)
                m = dve.do(lambda e, qr=qr: e.tensor_tensor(qparts[:, 2, :], qr, qparts[:, 1, :], ALU.subtract), m)
                pt_ring.give(buf, m)
                for rep_ in range(3):
                    first, step = (rep_, 3) if side == 0 else (3 * rep_, 1)
                    m = sp.dma(qk_out[side], dram(qk_scrd[side], first * GW, [[9 * GW, P], [step * GW, 3], [1, GW]]),
                               qparts[:, :, :], m, L(("scr", side)))
                late["qparts"] = m
                m = sp.dma(qk_in[side], st[0:ROW_MAX, :, :],
                           dram(qk_scrd[side], 0, [[GW, ROW_MAX], [ROW_MAX * GW, NH], [1, GW]]),
                           m, L("stack_free"), done["stack0"])
                late["scr", side] = m
                m_st.append(m)
                yield
            bank, free = psB.take()
            for i in range(GT):
                m = pe.do(lambda e, i=i, bank=bank: e.matmul(bank[:, i * P:(i + 1) * P], srcT[:, i * P:(i + 1) * P], w_v[:, :],
                                                             start=True, stop=True), *free)
            late["srcT", lay] = m
            for i in range(GT):
                m_v = dve.do(lambda e, i=i, bank=bank: e.tensor_tensor(
                    V9[:, i, :, 0:AD], bank[:, i * P:(i + 1) * P].rearrange("p (h c) -> p h c", c=AD),
                    b_v[:, :].rearrange("p (h c) -> p h c", c=AD), ALU.add), m, L("V9"), done["v9"])
            psB.give(bank, m_v)
            yield
            return m_st, m_v

        def ffn_attend(front, lay):
            L = late.get
            m_st, m_v = front
            for i in range(GT):
                s0 = (i // NT) * T
                for h2 in range(NH // 2):
                    bank, free = psB.take()
                    for k in range(2):
                        h = 2 * h2 + k
                        m = pe.do(lambda e, h=h, k=k, i=i, s0=s0, bank=bank: e.matmul(
                            bank[:, k * T:(k + 1) * T], q_stack[0:ROW_MAX, h, i * P:(i + 1) * P],
                            k_stack[0:ROW_MAX, h, s0:s0 + T], start=True, stop=True), *m_st, *free)
                    m = dve.do(lambda e, i=i, h2=h2, bank=bank: e.tensor_reduce(
                        nmax[:, i, 2 * h2:2 * h2 + 2], bank[:, :].rearrange("p (h k) -> p h k", k=T), AX.X, ALU.max),
                        m, L("nmax"))
                    psB.give(bank, m)
                    if h2 % 4 == 3:
                        yield
            m = dve.do(lambda e: e.tensor_scalar(nmax_bf[:, :, :], nmax[:, :, :], -1.0, None, ALU.mult), m, L("nmax"))
            bank, free = psB.take()
            bview = bank[:, :].bitcast(BF16)
            for i in range(GT):
                m2 = pe.do(lambda e, i=i, bview=bview: e.transpose(bview[0:NH, i * P:(i + 1) * P], nmax_bf[:, i, :],
                                                                   ident_bf[:, :]), m, *free)
            late["nmax"] = m2
            m = act.do(lambda e, bview=bview: e.activation(maxT[:, :], bview[0:NH, 0:GW], ACT.Copy), m2, L("maxT"))
            psB.give(bank, m)
            m_mx = sp.dma(max_in, q_stack[ROW_MAX:ROW_MAX + 1, :, :], maxT[:, :], m)
            late["maxT"] = m_mx
            yield
            for s in range(GS):
                for g in range(NH // 4):
                    pts = []
                    for kt in range(NT):
                        for h2 in range(2):
                            bank, free = psB.take()
                            for k in range(2):
                                h = 4 * g + 2 * h2 + k
                                m = pe.do(lambda e, h=h, k=k, kt=kt, s=s, bank=bank: e.matmul(
                                    bank[:, k * T:(k + 1) * T], k_stack[:, h, s * T + kt * P:s * T + (kt + 1) * P],
                                    q_stack[:, h, s * T:(s + 1) * T], start=True, stop=True), m_mx, *free)
                            late["stack_free"] = m
                            pt, pfree = pt_ring.take()
                            m_p = act.do(lambda e, pt=pt, bank=bank: e.activation(
                                pt[:, :, :].rearrange("p h q -> p (h q)"), bank[:, :], ACT.Exp, scale=float(AD) ** -0.5),
                                m, *pfree)
                            psB.give(bank, m_p)
                            pts.append((pt, kt, h2))
                    if g % 2 == 0:
                        obank, ofree = psB.take()
                    c0 = (g % 2) * T
                    for kt in range(NT):
                        for j in range(4):
                            pt = [p_ for p_, kt_, h2_ in pts if kt_ == kt and h2_ == j // 2][0]
                            m = pe.do(lambda e, j=j, kt=kt, pt=pt, s=s, g=g, obank=obank, c0=c0: e.matmul(
                                obank[32 * j:32 * j + 32, c0:c0 + T], V9[:, s * NT + kt, 4 * g + j, :], pt[:, j % 2, :],
                                start=(kt == 0), stop=(kt == NT - 1), skip_group_check=True), m_p, m_v, *ofree)
                    for pt, _, _ in pts:
                        pt_ring.give(pt, m)
                    if g % 2:
                        m_o = dve.do(lambda e, g=g, obank=obank: e.tensor_copy(
                            O_sb[:, g - 1:g + 1, :].rearrange("p g t -> p (g t)"), obank[:, :]), m, L("O_sb"))
                        psB.give(obank, m_o)
                    yield
                late["V9"] = m
            return m_o

        def ffn_tail(m_o, lay):
            L = late.get
            x1, x1T, w_e, src_t, o_tok = x1_b[lay], x1T_b[lay], w_e_b[lay], src_b[lay], ff_b[lay]
            gate_g, gate_q = gate_gq[lay]
            for s in range(GS):
                for qt in range(NT):
                    bank, free = psB.take()
                    for g in range(4):
                        m = pe.do(lambda e, g=g, qt=qt, bank=bank: e.transpose(
                            bank[:, g * P:(g + 1) * P], O_sb[:, g, qt * P:(qt + 1) * P], ident[:, :]), m_o, *free)
                    bh = bank[:, :].rearrange("p (h c) -> p h c", c=32)
                    m = dve.do(lambda e, bh=bh: e.reciprocal(rden[:, :], bh[:, :, AD]), m, L("rden"))
                    m = dve.do(lambda e, bh=bh, i=s * NT + qt: e.tensor_tensor(
                        o_tok[:, i, :].rearrange("p (h c) -> p h c", c=AD), bh[:, :, 0:AD], bc(rden[:, :], 2, AD), ALU.mult),
                        m, L(("ff", lay)))
                    psB.give(bank, m)
                    late["rden"] = m
                late["O_sb"] = m
            yield
            abuf, afree = pt_ring.take()
            attnT = abuf[:, 0, :]
            m_oT = transpose_tiles(attnT, o_tok, GT, psB, m, *afree)
            late["ff", lay] = m_oT
            bank, free = psB.take()
            for i in range(GT):
                m = pe.do(lambda e, i=i, bank=bank: e.matmul(bank[:, i * P:(i + 1) * P], attnT[:, i * P:(i + 1) * P], w_o[:, :],
                                                             start=True, stop=True), m_oT, *free)
            pt_ring.give(abuf, m)
            m = dve.do(lambda e, bank=bank: e.tensor_tensor(x1[:, :, :], bank[:, 0:GW].rearrange("p (i c) -> p i c", c=HID),
                                                            src_t[:, :, :], ALU.add), m, L(("x1", lay)))
            late["src_t", lay] = m
            psB.give(bank, m)
            yield
            m = dve.do(lambda e: e.tensor_tensor(x1[:, :, :], x1[:, :, :], bc(b_o[:, :], 1, GT), ALU.add), m)
            m_rs = layer_norm_stats(x1, GT, ln_b[lay], m)
            yield
            m = normalise(x1, x1, GT, ln_b[lay], m_rs)
            m_x1 = affine(x1, ln1_g, ln1_b, m)
            m_x1T = transpose_tiles(x1T, x1, GT, psB, m_x1, L(("x1T", lay)))
            yield
            bank, free = psB.take()
            for i in range(GT):
                m = pe.do(lambda e, i=i, bank=bank: e.matmul(bank[:, i * NE:(i + 1) * NE], x1T[:, i * P:(i + 1) * P],
                                                             w_gate[:, :], start=True, stop=True), m_x1T, *free)
            m = dve.do(lambda e, bank=bank: e.tensor_tensor(gate_l[:, :, :], bank[:, 0:GT * NE].rearrange("p (i n) -> p i n", n=NE),
                                                            bc(b_gate[:, :], 1, GT), ALU.add), m)
            psB.give(bank, m)
            m = dve.do(lambda e: e.tensor_reduce(gate_s[:, :], gate_l[:, :, :], AX.X, ALU.max), m)
            m = dve.do(lambda e: e.tensor_tensor(gate_l[:, :, :], gate_l[:, :, :], bc(gate_s[:, :], 2, NE), ALU.subtract), m)
            m = act.do(lambda e: e.activation(gate_l[:, :, :], gate_l[:, :, :], ACT.Exp), m)
            m = dve.do(lambda e: e.tensor_reduce(gate_s[:, :], gate_l[:, :, :], AX.X, ALU.add), m)
            m = dve.do(lambda e: e.reciprocal(gate_s[:, :], gate_s[:, :]), m)
            m = dve.do(lambda e: e.tensor_tensor(gate_l[:, :, :], gate_l[:, :, :], bc(gate_s[:, :], 2, NE), ALU.mult), m)
            mine, other = bc(gate_l[:, :, :], 3, NE), bc(gate_l[:, :, :], 2, NE)
            m1 = dve.do(lambda e: e.tensor_tensor(gate_g[:, :, :, :], other, mine, ALU.is_gt), m, L(("ff", lay)))
            m = dve.do(lambda e: e.tensor_tensor(gate_q[:, :, :, :], other, mine, ALU.is_equal), m)
            bf = bc(before[:, :].rearrange("p (a b) -> p a b", b=NE), 1, GT)
            m = dve.do(lambda e: e.tensor_tensor(gate_q[:, :, :, :], gate_q[:, :, :, :], bf, ALU.mult), m)
            m = dve.do(lambda e: e.tensor_tensor(gate_g[:, :, :, :], gate_g[:, :, :, :], gate_q[:, :, :, :], ALU.add), m, m1)
            m = dve.do(lambda e: e.tensor_reduce(w_e[:, :, :], gate_g[:, :, :, :], AX.X, ALU.add), m, L(("w_e", lay)))
            m_w = dve.do(lambda e: e.scalar_tensor_tensor(out=w_e[:, :, :], in0=w_e[:, :, :], scalar=1.5, in1=gate_l[:, :, :],
                                                          op0=ALU.is_lt, op1=ALU.mult), m)
            late["ff", lay] = m_w
            yield
            return m_x1, m_x1T, m_w

        def ffn_experts(x, m_x, att_marks, lay):
            L = late.get
            x1, x1T, w_e, ff = x1_b[lay], x1T_b[lay], w_e_b[lay], ff_b[lay]
            m_x1, m_x1T, m_w = att_marks
            ln_bufs = ln_b[1 if lay else 2]
            tb, tfree = h_ring.take()
            w_eT = tb[0:NE, 0, :]
            bank, free = psB.take()
            for i in range(GT):
                m = pe.do(lambda e, i=i, bank=bank: e.transpose(bank[0:NE, i * P:(i + 1) * P], w_e[:, i, :], ident[:, :]),
                          m_w, *free)
            m = act.do(lambda e, bank=bank: e.activation(w_eT[:, :], bank[0:NE, 0:GW], ACT.Copy), m, *tfree)
            psB.give(bank, m)
            bank, free = psB.take()
            for i in range(GT):
                m2 = pe.do(lambda e, i=i, bank=bank: e.matmul(bank[:, i * P:(i + 1) * P], w_eT[:, i * P:(i + 1) * P], b_2[:, :],
                                                              start=True, stop=True), m, *free)
            h_ring.give(tb, m2)
            m_ff = dve.do(lambda e, bank=bank: e.tensor_tensor(ff[:, :, :], bank[:, 0:GW].rearrange("p (i c) -> p i c", c=HID),
                                                               x1[:, :, :], ALU.add), m2, m_x1, L(("ff", lay)))
            late["x1", lay] = m_ff
            psB.give(bank, m_ff)
            yield
            hidden = {}
            for step in range(NE + 1):
                if step < NE:
                    hb, hfree = h_ring.take()
                    for k in range(2):
                        bank, free = psB.take()
                        m = pe.do(lambda e, ex=step, k=k, bank=bank: e.matmul(
                            bank[:, 0:GW], w_1[:, ex, k * P:(k + 1) * P], x1T[:, :], start=True, stop=True), m_x1T, *free)
                        late["x1T", lay] = m
                        m_h = act.do(lambda e, ex=step, k=k, bank=bank, hb=hb: e.activation(
                            hb[:, k, :], bank[:, 0:GW], ACT.Relu, bias=b_1[:, 2 * ex + k:2 * ex + k + 1]), m, *hfree)
                        psB.give(bank, m_h)
                    hidden[step] = (hb, m_h)
                if step:
                    ex = step - 1
                    hb, m_h = hidden.pop(ex)
                    bank, free = psB.take()
                    for i in range(GT):
                        for k in range(2):
                            m = pe.do(lambda e, ex=ex, i=i, k=k, bank=bank, hb=hb: e.matmul(
                                bank[:, i * P:(i + 1) * P], hb[:, k, i * P:(i + 1) * P], w_2[:, 2 * ex + k, :],
                                start=(k == 0), stop=(k == 1)), m_h, *free)
                    h_ring.give(hb, m)
                    for i in range(GT):
                        m_ff2 = dve.do(lambda e, ex=ex, i=i, bank=bank: e.scalar_tensor_tensor(
                            out=ff[:, i, :], in0=bank[:, i * P:(i + 1) * P], scalar=w_e[:, i, ex:ex + 1], in1=ff[:, i, :],
                            op0=ALU.mult, op1=ALU.add), m, m_ff)
                    psB.give(bank, m_ff2)
                    m_ff = m_ff2
                yield
            late["w_e", lay] = m_ff
            m_rs = layer_norm_stats(ff, GT, ln_bufs, m_ff, by_newton=True)
            yield
            m = normalise(ff, ff, GT, ln_bufs, m_rs)
            m = affine(ff, ln2_g, ln2_b, m)
            m = dve.do(lambda e: e.tensor_tensor(x[:, :, :], x[:, :, :], ff[:, :, :], ALU.add), m, *m_x)
            late["ff", lay] = m
            yield
            return m

        def mix_layer(x, m_x):
            L = late.get
            lay = 1
            src_t, srcT, ff = src_b[lay], srcT_b[lay], ff_b[0]
            m_rs = layer_norm_stats(x, GT, ln_b[2], *m_x, by_newton=True)
            yield
            m = normalise(src_t, x, GT, ln_b[2], m_rs, L(("src_t", lay)))
            m_sT = transpose_tiles(srcT, src_t, GT, psB, m, L(("srcT", lay)))
            late["src_t", lay] = m_sT
            bank, free = psB.take()
            m = pe.do(lambda e, bank=bank: e.matmul(bank[:, 0:GW], w_val[:, :], srcT[:, :], start=True, stop=True), m_sT, *free)
            bv = bank[:, 0:GW].rearrange("p (s t) -> p s t", t=T)
            act.do(lambda e, bv=bv: e.activation(v_ext[:, :, MAXSH:MAXSH + T], bv, ACT.Copy, scale=0.5), m, L("O_sb"))
            act.do(lambda e, bv=bv: e.activation(v_ext[:, :, 0:MAXSH], bv[:, :, T - MAXSH:], ACT.Copy, scale=0.5))
            m_v = act.do(lambda e, bv=bv: e.activation(v_ext[:, :, MAXSH + T:], bv[:, :, 0:MAXSH], ACT.Copy, scale=0.5))
            psB.give(bank, m_v)
            m_acc = None
            for k, shift in enumerate((0,) + SHIFTS):
                bank, free = psB.take()
                m = pe.do(lambda e, k=k, bank=bank: e.matmul(bank[:, 0:GW], w_mix[:, k * P:(k + 1) * P], srcT[:, :],
                                                             start=True, stop=True), *free)
                buf, bfree = pt_ring.take()
                sg = buf[:, 0, :] if GS == 1 else None
                m_s = act.do(lambda e, sg=sg, bank=bank: e.activation(sg, bank[:, 0:GW], ACT.Tanh, scale=0.5), m, *bfree)
                psB.give(bank, m_s)
                vv = v_ext[:, :, MAXSH + shift:MAXSH + shift + T]
                sv = sg.rearrange("p (s t) -> p s t", t=T)
                prod = mix_acc[:, :] if k == 0 else buf[:, 1, :]
                m_acc = dve.do(lambda e, vv=vv, sv=sv, prod=prod: e.scalar_tensor_tensor(
                    out=prod.rearrange("p (s t) -> p s t", t=T), in0=sv, scalar=1.0, in1=vv, op0=ALU.add, op1=ALU.mult),
                    m_s, m_v, m_acc, L(("x1T", 0)))
                if k:
                    m_acc = dve.do(lambda e, prod=prod: e.tensor_tensor(mix_acc[:, :], mix_acc[:, :], prod, ALU.add), m_acc)
                pt_ring.give(buf, m_acc)
                yield
            late["srcT", lay], late["O_sb"] = m_s, m_acc
            bank, free = psB.take()
            for i in range(GT):
                m = pe.do(lambda e, i=i, bank=bank: e.transpose(bank[:, i * P:(i + 1) * P], mix_acc[:, i * P:(i + 1) * P],
                                                                ident[:, :]), m_acc, *free)
            late["x1T", 0] = m
            m = act.do(lambda e, bank=bank: e.activation(ff[:, :, :].rearrange("p i c -> p (i c)"), bank[:, 0:GW], ACT.Copy),
                       m, L(("ff", 0)))
            psB.give(bank, m)
            m_rs = layer_norm_stats(ff, GT, ln_b[2], m, by_newton=True)
            yield
            m = normalise(ff, ff, GT, ln_b[2], m_rs)
            m = affine(ff, mix_g, mix_b, m)
            m = dve.do(lambda e: e.tensor_tensor(x[:, :, :], x[:, :, :], ff[:, :, :], ALU.add), m, *m_x)
            late["ff", 0] = m
            yield
            return m

        xin = d["x"].rearrange("b (i p) c -> p b i c", p=P)
        xout = out.rearrange("b (i p) c -> p b i c", p=P)
        xs, m_xs = {}, {}
        gates, proj, attended = {}, {}, {}

        def load_x(n):
            if n < n_batch:
                xs[n], free = x_ring.take()
                m_xs[n] = (sp.dma(x_in[n % 4], xs[n][:, :, :], xin[:, n], *free),)

        def first_gates(n):
            if n < n_batch and "a" in layers:
                gates[n] = yield from ssm_gates(xs[n], m_xs[n])

        def project(n):
            if n < n_batch and "a" in layers:
                proj[n] = yield from ssm_project(gates[n])

        def attend(n):
            if n < n_batch and "a" in layers:
                m = yield from ssm_attend(xs[n], m_xs[n], proj[n])
                m_xs[n] = (m,)

        last_f = layers.count("f") - 1
        fronts, sums_done = {}, {}
        strands = {}

        def front(n, lay, by_newton):
            if 0 <= n < n_batch and lay <= last_f:
                fronts[n, lay] = yield from ffn_front(xs[n], m_xs[n], lay, by_newton)

        def softmaxes(n):
            if (n - 1, 0) in fronts:
                sums_done[n - 1, 0] = yield from ffn_attend(fronts.pop((n - 1, 0)), 0)
                tail = first_tail(n)
                next(tail)
                strands["first_tail"] = tail
            yield from front(n - 2, 1, False)
            if (n - 2, 1) in fronts:
                sums_done[n - 2, 1] = yield from ffn_attend(fronts.pop((n - 2, 1)), 1)
                attended[n - 2, 1] = yield from ffn_tail(sums_done.pop((n - 2, 1)), 1)

        def first_tail(n):
            attended[n - 1, 0] = yield from ffn_tail(sums_done.pop((n - 1, 0)), 0)

        def experts(n, lay):
            if (n, lay) in attended:
                m_xs[n] = ((yield from ffn_experts(xs[n], m_xs[n], attended.pop((n, lay)), lay)),)

        def middle(n):
            yield from experts(n - 2, 0)
            if 0 <= n - 2 < n_batch and "b" in layers:
                m_xs[n - 2] = ((yield from mix_layer(xs[n - 2], m_xs[n - 2])),)

        def ends(n):
            yield from front(n - 1, 0, True)
            yield from experts(n - 3, 1)
            if 0 <= n - 3:
                x = xs.pop(n - 3)
                x_ring.give(x, sp.dma(x_out, xout[:, n - 3], x[:, :, :], *m_xs.pop(n - 3)))

        def emitted():
            return sum(len(q.ops) for q in (pe, act, dve))

        expect = {}

        def weave(**named):
            strands.update(named)
            spent, back = {}, {}
            while strands:
                now, count = pe.clock, emitted()
                k = min(strands, key=lambda k: (max(back.get(k, 0) - now, 0), spent.get(k, 0) / expect.get(k, 1)))
                Queue.step_end = 0.0
                try:
                    next(strands[k])
                except StopIteration:
                    del strands[k]
                spent[k] = spent.get(k, 0) + emitted() - count
                back[k] = Queue.step_end + SLACK
            for k, v in spent.items():
                expect[k] = max(v, expect.get(k, 1))

        def table(name):
            act.run(lambda e: e.preload_act_table_set(name))

        load_x(0)
        table("natural_log_exp_and_others")
        for _ in first_gates(0):
            pass
        for n in range(n_batch + 3):
            table("silu_and_others")
            weave(project=project(n), middle=middle(n), ends=ends(n))
            table("natural_log_exp_and_others")
            load_x(n + 1)
            weave(attend=attend(n), gates=first_gates(n + 1), softmaxes=softmaxes(n))
        sp.wait([(x_out[0], x_out[1])])

        block = ctx.enter_context(nc.Block())

        @block.sync
        def _(e):
            for op in sp.ops:
                op(e)

        @block.tensor
        def _(e):
            for op in pe.ops:
                op(e)

        @block.scalar
        def _(e):
            for op in act.ops:
                op(e)

        @block.vector
        def _(e):
            for op in dve.ops:
                op(e)

        @block.gpsimd
        def _(e):
            for op in pool.ops:
                op(e)



def lay_out(i):
    def f(a):
        return np.ascontiguousarray(a)

    a = {k: np.asarray(v) for k, v in i.items()}
    pa, pb, pf = "L0_attn_a_", "L0_attn_b_", "L0_ffn_"
    w, b = a[pa + "in_proj_w"], a[pa + "in_proj_b"]
    n_big = DIM + CONV
    lvl_w = w[n_big + H:].reshape(H, NLV_W, HID).transpose(1, 0, 2)[:NLV + 1].reshape(-1, HID)
    lvl_b = b[n_big + H:].reshape(H, NLV_W).T[:NLV + 1].reshape(-1)
    o = {
        "x": a[pa + "hidden_states"],
        "in_wT": f(w[:n_big].T), "in_b_cols": f(b[:n_big].reshape(-1, P).T),
        "small_wT": f(np.concatenate([w[n_big:n_big + H], lvl_w]).T),
        "small_b": np.concatenate([b[n_big:n_big + H], lvl_b]),
        "dt_bias": a[pa + "dt_bias"], "A_log": a[pa + "A_log"], "D": a[pa + "D"],
        "L_lvl": f(a[pa + "L"].T[:NLV + 1]).reshape(-1),
        "conv_cols": f(a[pa + "conv_w"].reshape(-1, P, KCONV).transpose(1, 0, 2)),
        "norm_cols": f(a[pa + "norm_w"].reshape(-1, P).T),
        "out_wT": f(a[pa + "out_proj_w"].T.reshape(NF, P, HID).transpose(1, 0, 2)), "out_b": a[pa + "out_proj_b"],
        "gate_WT": f(a[pb + "gate_W"].T), "value_WT": f(a[pb + "value_W"].T),
        "gamma": a[pb + "gamma"], "beta": a[pb + "beta"],
        "bq": a[pf + "bq"].reshape(P, 1), "bk": a[pf + "bk"].reshape(P, 1),
        "W1": f(a[pf + "W1"].transpose(1, 0, 2)),
        "b1_cols": f(a[pf + "b1"].reshape(-1, P).T),
        "W2": f(a[pf + "W2"].reshape(-1, P, HID).transpose(1, 0, 2)), "b2": a[pf + "b2"],
    }
    for n in ("Wq", "Wk", "Wv", "Wo", "bv", "bo", "gW", "gb", "ln1_g", "ln1_b", "ln2_g", "ln2_b"):
        o[n] = a[pf + n]
    o.update(shape_constants())
    return o


def kernel(**inputs):
    import concourse.bacc as _bacc
    from concourse.bass_utils import run_bass_kernel_spmd as _run

    nc = _bacc.Bacc("TRN2", target_bir_lowering=False, num_devices=1)
    arrays = lay_out(inputs)
    d = {n: nc.dram_tensor("in_" + n, v.shape, mybir.dt.from_np(v.dtype), kind="ExternalInput").ap()
         for n, v in arrays.items()}
    out = nc.dram_tensor("out_0", (BATCH, T, HID), F32, kind="ExternalOutput").ap()
    build(nc, d, out)
    r = _run(nc, [{"in_" + n: v for n, v in arrays.items()}], core_ids=[0])
    return r.results[0]["out_0"]
```
